# Optimizing a Trainium2 kernel written in Bass

```python
import numpy as np
import jax
import jax.numpy as jnp

def _softmax(x, axis=-1):
    return jax.nn.softmax(x, axis=axis)

def _gelu(x):
    return jax.nn.gelu(x, approximate=True)

def _silu(x):
    return jax.nn.silu(x)

def _sigmoid(x):
    return jax.nn.sigmoid(x)

def _layernorm(x, axis=-1, eps=1e-05):
    m = jnp.mean(x, axis=axis, keepdims=True)
    v = jnp.var(x, axis=axis, keepdims=True)
    return (x - m) / jnp.sqrt(v + eps)

def _scatter_add(tgt, idx, src, axis=0):
    return tgt.at[idx].add(src)

def _segment_sum(src, seg, n):
    return jax.ops.segment_sum(src, seg, n)
kernel_name = 'mk_macaron_d1_jaxref_r8_ef9ecc'

def setup_inputs(seed: int=0):
    np.random.seed(seed)
    _w = jnp.asarray

    def _L0_attn_setup():
        import jax, jax.numpy as jnp
        import numpy as np
        HIDDEN = 512
        N_HEADS = 32
        N_KV_HEADS = 8
        HEAD_DIM = HIDDEN // N_HEADS
        N_REP = N_HEADS // N_KV_HEADS
        KV_DIM = N_KV_HEADS * HEAD_DIM

        def _kaiming_uniform(key, out_f, in_f):
            bound = 1.0 / np.sqrt(in_f)
            return jax.random.uniform(key, (out_f, in_f), jnp.float32, -bound, bound)

        def bitnet_linear(x, weight, scale_param):
            s = jnp.maximum(jnp.mean(jnp.abs(weight), axis=1), 1e-08)
            binary_w = jnp.sign(weight / s[:, None])
            y = jnp.einsum('bsi,oi->bso', x, binary_w)
            y = y * (s * scale_param)[None, None, :]
            return jnp.nan_to_num(y, nan=0.0, posinf=1000000.0, neginf=-1000000.0)
        key = jax.random.key(seed)
        ks = jax.random.split(key, 5)
        return {'hidden_states': jax.random.normal(ks[0], (1, 256, HIDDEN), jnp.float32), 'q_weight': _kaiming_uniform(ks[1], HIDDEN, HIDDEN), 'q_scale': jnp.ones((HIDDEN,), jnp.float32), 'k_weight': _kaiming_uniform(ks[2], KV_DIM, HIDDEN), 'k_scale': jnp.ones((KV_DIM,), jnp.float32), 'v_weight': _kaiming_uniform(ks[3], KV_DIM, HIDDEN), 'v_scale': jnp.ones((KV_DIM,), jnp.float32), 'o_weight': _kaiming_uniform(ks[4], HIDDEN, HIDDEN), 'o_scale': jnp.ones((HIDDEN,), jnp.float32)}
    _L0_attn_in = _L0_attn_setup()

    def _L0_ffn_setup():
        import jax, jax.numpy as jnp
        import numpy as np
        GROUP = 64

        def dequant_q40(w, s, out_features, in_features):
            msb = w >> 4
            lsb = (w & 15 ^ 8) - 8
            g = jnp.concatenate([msb, lsb], axis=1).reshape(-1, GROUP)
            deq = g.astype(s.dtype) * s[:, None]
            return deq.reshape(out_features, in_features)
        key = jax.random.key(seed)
        ks = jax.random.split(key, 7)
        dim, hidden = (512, 1376)
        B, S = (2, 256)

        def packed(k, din, dout):
            return jax.random.randint(k, (din * dout // GROUP // 2, GROUP), -128, 128, dtype=jnp.int32)

        def scales(k, din, dout):
            return (jax.random.uniform(k, (din * dout // GROUP,), dtype=jnp.float32) + 0.5) * 0.01
        x = jax.random.normal(ks[0], (B, S, dim), dtype=jnp.float32)
        w1 = packed(ks[1], dim, hidden)
        s1 = scales(ks[2], dim, hidden)
        w2 = packed(ks[3], hidden, dim)
        s2 = scales(ks[4], hidden, dim)
        w3 = packed(ks[5], dim, hidden)
        s3 = scales(ks[6], dim, hidden)
        return {'x': x, 'w1': w1, 's1': s1, 'w2': w2, 's2': s2, 'w3': w3, 's3': s3}
    _L0_ffn_in = _L0_ffn_setup()
    _d = {'L0_attn_hidden_states': _L0_attn_in['hidden_states'], 'L0_attn_q_weight': _L0_attn_in['q_weight'], 'L0_attn_q_scale': _L0_attn_in['q_scale'], 'L0_attn_k_weight': _L0_attn_in['k_weight'], 'L0_attn_k_scale': _L0_attn_in['k_scale'], 'L0_attn_v_weight': _L0_attn_in['v_weight'], 'L0_attn_v_scale': _L0_attn_in['v_scale'], 'L0_attn_o_weight': _L0_attn_in['o_weight'], 'L0_attn_o_scale': _L0_attn_in['o_scale'], 'L0_ffn_w1': _L0_ffn_in['w1'], 'L0_ffn_s1': _L0_ffn_in['s1'], 'L0_ffn_w2': _L0_ffn_in['w2'], 'L0_ffn_s2': _L0_ffn_in['s2'], 'L0_ffn_w3': _L0_ffn_in['w3'], 'L0_ffn_s3': _L0_ffn_in['s3']}
    _x0 = _d['L0_attn_hidden_states']
    _d['L0_attn_hidden_states'] = jax.random.normal(jax.random.fold_in(jax.random.key(seed), 1), (2, 1024, 512), dtype=_x0.dtype)
    del _x0
    return _d

def reference(L0_attn_hidden_states, L0_attn_q_weight, L0_attn_q_scale, L0_attn_k_weight, L0_attn_k_scale, L0_attn_v_weight, L0_attn_v_scale, L0_attn_o_weight, L0_attn_o_scale, L0_ffn_w1, L0_ffn_s1, L0_ffn_w2, L0_ffn_s2, L0_ffn_w3, L0_ffn_s3):

    def _L0_attn_ref(hidden_states, q_weight, q_scale, k_weight, k_scale, v_weight, v_scale, o_weight, o_scale):
        import jax, jax.numpy as jnp
        import numpy as np
        HIDDEN = 512
        N_HEADS = 32
        N_KV_HEADS = 8
        HEAD_DIM = HIDDEN // N_HEADS
        N_REP = N_HEADS // N_KV_HEADS
        KV_DIM = N_KV_HEADS * HEAD_DIM

        def _kaiming_uniform(key, out_f, in_f):
            bound = 1.0 / np.sqrt(in_f)
            return jax.random.uniform(key, (out_f, in_f), jnp.float32, -bound, bound)

        def bitnet_linear(x, weight, scale_param):
            s = jnp.maximum(jnp.mean(jnp.abs(weight), axis=1), 1e-08)
            binary_w = jnp.sign(weight / s[:, None])
            y = jnp.einsum('bsi,oi->bso', x, binary_w)
            y = y * (s * scale_param)[None, None, :]
            return jnp.nan_to_num(y, nan=0.0, posinf=1000000.0, neginf=-1000000.0)
        b, s, _ = hidden_states.shape
        q = bitnet_linear(hidden_states, q_weight, q_scale)
        k = bitnet_linear(hidden_states, k_weight, k_scale)
        v = bitnet_linear(hidden_states, v_weight, v_scale)
        q = q.reshape(b, s, N_HEADS, HEAD_DIM).transpose(0, 2, 1, 3)
        k = k.reshape(b, s, N_KV_HEADS, HEAD_DIM).transpose(0, 2, 1, 3)
        v = v.reshape(b, s, N_KV_HEADS, HEAD_DIM).transpose(0, 2, 1, 3)
        k = jnp.repeat(k, N_REP, axis=1)
        v = jnp.repeat(v, N_REP, axis=1)
        scores = jnp.einsum('bhqd,bhkd->bhqk', q, k) / np.sqrt(HEAD_DIM)
        attn = jax.nn.softmax(scores, axis=-1)
        out = jnp.einsum('bhqk,bhkd->bhqd', attn, v)
        out = out.transpose(0, 2, 1, 3).reshape(b, s, HIDDEN)
        return bitnet_linear(out, o_weight, o_scale)

    def _L0_ffn_ref(x, w1, s1, w2, s2, w3, s3):
        import jax, jax.numpy as jnp
        import numpy as np
        GROUP = 64

        def dequant_q40(w, s, out_features, in_features):
            msb = w >> 4
            lsb = (w & 15 ^ 8) - 8
            g = jnp.concatenate([msb, lsb], axis=1).reshape(-1, GROUP)
            deq = g.astype(s.dtype) * s[:, None]
            return deq.reshape(out_features, in_features)
        dim = x.shape[-1]
        hidden = w1.shape[0] * w1.shape[1] * 2 // dim
        W1 = dequant_q40(w1, s1, hidden, dim)
        W3 = dequant_q40(w3, s3, hidden, dim)
        W2 = dequant_q40(w2, s2, dim, hidden)
        a = jnp.einsum('bsd,hd->bsh', x, W1)
        b = jnp.einsum('bsd,hd->bsh', x, W3)
        h = jax.nn.silu(a) * b
        return jnp.einsum('bsh,dh->bsd', h, W2)
    x = L0_attn_hidden_states
    x = x + 0.5 * _L0_ffn_ref(_layernorm(x, axis=-1), L0_ffn_w1, L0_ffn_s1, L0_ffn_w2, L0_ffn_s2, L0_ffn_w3, L0_ffn_s3)
    x = x + _L0_attn_ref(_layernorm(x, axis=-1), L0_attn_q_weight, L0_attn_q_scale, L0_attn_k_weight, L0_attn_k_scale, L0_attn_v_weight, L0_attn_v_scale, L0_attn_o_weight, L0_attn_o_scale)
    x = x + 0.5 * _L0_ffn_ref(_layernorm(x, axis=-1), L0_ffn_w1, L0_ffn_s1, L0_ffn_w2, L0_ffn_s2, L0_ffn_w3, L0_ffn_s3)
    return x

_drawn_inputs = setup_inputs


def setup_inputs(seed=0):
    import zlib

    import numpy as np

    out = dict(_drawn_inputs(seed))
    spreads = {'L0_attn_q_scale': (1.0, 0.6),
     'L0_attn_k_scale': (1.0, 0.6),
     'L0_attn_v_scale': (1.0, 0.6),
     'L0_attn_o_scale': (1.0, 0.6)}
    factors = {'L0_attn_q_weight': 8.0,
     'L0_attn_k_weight': 8.0,
     'L0_attn_v_weight': 5.876,
     'L0_attn_o_weight': 6.054}
    for name, (base, spread) in spreads.items():
        noise = np.random.default_rng([zlib.crc32(name.encode()), seed]).standard_normal(out[name].shape)
        drawn = base * np.exp(spread * noise) if base else spread * noise
        out[name] = jnp.asarray(drawn.astype(out[name].dtype))
    for name, factor in factors.items():
        out[name] = (out[name] * factor).astype(out[name].dtype)
    return out
```

```python
import concourse.bass as bass
from concourse import mybir
from contextlib import ExitStack

F32 = mybir.dt.float32
F32R = mybir.dt.float32r
BF16 = mybir.dt.bfloat16
F16 = mybir.dt.float16
I32 = mybir.dt.int32
ACT = mybir.ActivationFunctionType
ALU = mybir.AluOpType
AX = mybir.AxisListType

P = 128
BATCH, SEQ, D = 2, 1024, 512
TOK = BATCH * SEQ
HID = 1376
GROUP = 64
NH, NKV, HD = 32, 8, 16
REP = NH // NKV
KVD = NKV * HD
DC = D // P
HC = -(-HID // P)
HTAIL = HID - (HC - 1) * P
TT = 512
NT = TOK // TT
SUB = TT // P
LN_EPS = 1e-5
FIN_LIMIT = 1e6
FREE = 16


class Chain:

    def __init__(self, eng, sem, apart=None):
        self.eng, self.sem, self.apart, self.n, self.at = eng, sem, apart, 0, 0

    def enter(self, base):
        self.at, self.n = base, 0

    def add(self, ins):
        self.n += 1
        ins.then_inc(self.sem, 1)

    def wait(self):
        self.eng.wait_ge(self.sem, self.at + self.n)

    def wait_apart(self):
        self.wait()
        self.eng.sem_inc(self.apart, 1)

    def link(self, ins):
        self.add(ins)
        self.wait()


def layernorm_stats(nc, dve, chain, xin, stats, mv, stats_ready):
    for s in range(SUB):
        chain.add(nc.vector.bn_stats(stats[:, s, :], xin[:, s, :]))
    chain.wait_apart()
    for s in range(SUB):
        last = nc.vector.bn_aggr(mv[:, s, :], stats[:, s, :])
    last.then_inc(stats_ready, 1)


def rstd_on_pool(nc, chain, mv, ve, rstd, tmp, neg_half, rstd_ready):
    g = nc.gpsimd
    chain.link(g.tensor_scalar(ve[:, :], mv[:, :, 1], LN_EPS, None, ALU.add))
    chain.link(g.tensor_tensor(rstd[:, :], ve[:, :], neg_half[:, :], ALU.pow))
    chain.link(g.tensor_tensor(tmp[:, :], rstd[:, :], rstd[:, :], ALU.mult))
    chain.add(g.tensor_tensor(tmp[:, :], tmp[:, :], ve[:, :], ALU.mult))
    chain.wait_apart()
    chain.link(g.tensor_scalar(tmp[:, :], tmp[:, :], -0.5, 1.5, ALU.mult, ALU.add))
    g.tensor_tensor(rstd[:, :], rstd[:, :], tmp[:, :], ALU.mult).then_inc(rstd_ready, 1)


RSTD_LINKS = 5


def weight_prep(nc, ctx, sem, io, W):
    with ExitStack() as c:
        sb = lambda n, s, d: c.enter_context(nc.sbuf_tensor(n, s, d))
        bank = [c.enter_context(nc.psum_tensor(f"prep_bank{i}", [P, DC, P], F32)) for i in range(4)]
        ident = W["ident"]
        packed = [sb(f"packed{i}", [P, DC, GROUP], I32) for i in range(2)]
        nib = sb("nib", [P, DC, 2, GROUP], I32)
        gscale = [sb(f"gscale{i}", [P, DC, 2], F32) for i in range(2)]
        deq = [sb(f"deq{i}", [P, DC, 2, GROUP], F32) for i in range(2)]
        PR = HID * 4 // (2 * GROUP)
        packed2 = sb("packed2", [P, PR, GROUP], I32)
        gscale2 = sb("gscale2", [P, PR, 2], F32)
        deq2 = sb("deq2", [P, PR, 2, GROUP], F32)
        wrow = [sb(f"wrow{i}", [P, D], F32) for i in range(2)]
        wsign = [sb(f"wsign{i}", [P, D], F32) for i in range(2)]
        NS = DC + 1 + 1 + DC
        wmean = sb("wmean", [P, NS], F32)
        wrecip = sb("wrecip", [P, NS], F32)
        par_scale = sb("par_scale", [P, NS], F32)
        row_scale = sb("row_scale", [P, NS], F32)

        w_view = [io[n].rearrange("(o k) c -> o (k c)", k=DC) for n in ("w1", "w3")]
        s_view = [io[n].rearrange("(o g) -> o g", g=2 * DC) for n in ("s1", "s3")]
        FULL = HC - 1
        rows = lambda ch: P if not isinstance(ch, int) or ch < FULL else HTAIL

        packed_ready = [sem(f"packed_ready{i}") for i in range(2)]
        packed_used, deq_ready, deq_used = sem("packed_used"), sem("deq_ready"), sem("deq_used")
        hi_done, lo_done = sem("prep_hi_done"), sem("prep_lo_done")
        packed2_ready, deq2_ready, tr2_ready = sem("packed2_ready"), sem("deq2_ready"), sem("tr2_ready")
        hi2_done, lo2_done = sem("hi2_done"), sem("lo2_done")
        wrow_ready = [sem(f"wrow_ready{i}") for i in range(2)]
        wrow_used, wrecip_ready, wsign_ready = sem("wrow_used"), sem("wrecip_ready"), sem("wsign_ready")
        sign_tr, sign_out = sem("sign_tr"), sem("sign_out")
        par_ready, row_ready, row_stored, row_back = (sem(n) for n in ("par_ready", "row_ready", "row_stored", "row_back"))
        ident_zero, ident_ready, prep_dve = sem("ident_zero"), sem("ident_ready"), sem("prep_dve")

        SIGN = [("wq", j) for j in range(DC)] + [("wk", 0), ("wv", 0)] + [("wo", j) for j in range(DC)]

        block = c.enter_context(nc.Block())

        @block.sync
        def _(sp):
            def load(ch, w):
                n = rows(ch)
                src = bass.ds(ch * P, n) if not isinstance(ch, int) else slice(ch * P, ch * P + n)
                if not isinstance(ch, int) or ch > 0:
                    sp.wait_ge(deq_ready, 2 * ch + w - 1)
                sp.dma_start(packed[w][0:n].rearrange("p k c -> p (k c)"), w_view[w][src, :]).then_inc(packed_ready[w], 16)
                sp.dma_start(gscale[w][0:n].rearrange("p k h -> p (k h)"), s_view[w][src, :]).then_inc(packed_ready[w], 16)

            for w in range(2):
                load(0, w)
            with nc.allow_non_contiguous_dma("one scale per row"):
                for name, at, n in (("qs", 0, DC), ("ks", DC, 1), ("vs", DC + 1, 1), ("os", DC + 2, DC)):
                    sp.dma_start(par_scale[:, at:at + n], io[name].rearrange("(c p) -> p c", p=P)).then_inc(par_ready, 16)
            sp.dma_start(packed2.rearrange("p r c -> p (r c)"), io["w2"].rearrange("(p r) c -> p (r c)", p=P)).then_inc(packed2_ready, 16)
            sp.dma_start(gscale2.rearrange("p r h -> p (r h)"), io["s2"].rearrange("(p g) -> p g", p=P)).then_inc(packed2_ready, 16)
            for u in range(2):
                name, j = SIGN[u]
                sp.dma_start(wrow[u][:, :], io[name][j * P:(j + 1) * P, :]).then_inc(wrow_ready[u], 16)
            with sp.Fori(1, FULL) as ch:
                for w in range(2):
                    load(ch, w)
            for w in range(2):
                load(FULL, w)
            for u in range(2, NS):
                name, j = SIGN[u]
                sp.wait_ge(wrow_used, u - 1)
                sp.dma_start(wrow[u % 2][:, :], io[name][j * P:(j + 1) * P, :]).then_inc(wrow_ready[u % 2], 16)
            sp.wait_ge(row_ready, 1)
            with nc.allow_non_contiguous_dma("one scale per row"):
                sp.dma_start(io["row_scratch"].rearrange("(c p) -> p c", p=P), row_scale[:, DC + 1:NS]).then_inc(row_stored, 16)
            sp.wait_ge(row_stored, 16)
            sp.dma_start(W["vo_scale"][:, :], io["row_scratch"][None, :].to_broadcast([P, KVD + D])).then_inc(row_back, 16)
            sp.wait_ge(row_back, 16)

        @block.gpsimd
        def _(pool):
            nc.gpsimd.memset(ident[:, :], 0.0).then_inc(ident_zero, 1)
            pool.wait_ge(ident_zero, 1)
            nc.gpsimd.affine_select(out=ident[:, :], in_=ident[:, :], compare_op=ALU.not_equal, fill=1.0, base=0,
                                    pattern=[[-1, P]], channel_multiplier=1).then_inc(ident_ready, 1)
            nc.gpsimd.memset(W["neg_half"][:, :], -0.5)

        @block.vector
        def _(dve):
            chain = Chain(dve, prep_dve)
            dve.sem_inc(lo_done, FREE)

            def dequant(ch, w):
                n = rows(ch)
                dve.wait_ge(packed_ready[w], ch * 32 + 32)
                dve.wait_ge(deq_ready, 2 * ch + w)
                chain.add(nc.vector.tensor_scalar(nib[0:n, :, 0, :], packed[w][0:n], 4, None, ALU.arith_shift_right))
                nc.vector.tensor_scalar(nib[0:n, :, 1, :], packed[w][0:n], 28, 28, ALU.arith_shift_left,
                                        ALU.arith_shift_right).then_inc(packed_used, 1)
                dve.wait_ge(packed_used, 2 * ch + w + 1)
                chain.wait()
                dve.wait_ge(deq_used, 2 * ch + FREE)
                nc.vector.tensor_tensor(deq[w][0:n], nib[0:n], gscale[w][0:n].unsqueeze(3).to_broadcast([n, DC, 2, GROUP]),
                                        ALU.mult).then_inc(deq_ready, 1)

            def low_part(ch, w):
                n = rows(ch)
                cols = bass.ds(ch * P, n) if not isinstance(ch, int) else slice(ch * P, ch * P + n)
                dve.wait_ge(hi_done, 2 * ch + w + 1)
                nc.vector.tensor_tensor(W["up_lo"][w][:, :, cols], bank[w][:, :, 0:n],
                                        W["up_hi"][w][:, :, cols].bitcast(F32), ALU.subtract).then_inc(lo_done, 1)

            dequant(0, 0)
            with dve.Fori(0, FULL - 1) as ch:
                chain.enter(ch * 2 + 1)
                dequant(ch, 1)
                low_part(ch, 0)
                dequant(ch + 1, 0)
                low_part(ch, 1)
            chain.enter((FULL - 1) * 2 + 1)
            dequant(FULL - 1, 1)
            low_part(FULL - 1, 0)
            dequant(FULL, 0)
            low_part(FULL - 1, 1)
            dequant(FULL, 1)
            low_part(FULL, 0)
            low_part(FULL, 1)

            dve.wait_ge(packed2_ready, 32)
            deq2_int = deq2.bitcast(I32)
            chain.add(nc.vector.tensor_scalar(deq2_int[:, :, 0, :], packed2[:, :, :], 4, None, ALU.arith_shift_right))
            chain.link(nc.vector.tensor_scalar(deq2_int[:, :, 1, :], packed2[:, :, :], 28, 28, ALU.arith_shift_left,
                                               ALU.arith_shift_right))
            nc.vector.tensor_tensor(deq2[:, :, :, :], deq2_int[:, :, :, :],
                                    gscale2[:, :, :].unsqueeze(3).to_broadcast([P, PR, 2, GROUP]),
                                    ALU.mult).then_inc(deq2_ready, 1)
            for u in range(NS):
                dve.wait_ge(wrow_ready[u % 2], (u // 2 + 1) * 16)
                chain.link(nc.vector.tensor_reduce(wmean[:, u:u + 1], wrow[u % 2][:, :], AX.X, ALU.add,
                                                   apply_absolute_value=True))
                chain.link(nc.vector.tensor_scalar(wmean[:, u:u + 1], wmean[:, u:u + 1], 1.0 / D, 1e-8, ALU.mult, ALU.max))
                nc.vector.reciprocal(wrecip[:, u:u + 1], wmean[:, u:u + 1]).then_inc(wrecip_ready, 1)
                if u < HC:
                    n = P if u < FULL else HTAIL
                    dve.wait_ge(hi2_done, u + 1)
                    nc.vector.tensor_tensor(W["down_lo"][0:n, u, :].rearrange("h (p j) -> h j p", j=4), bank[2 + u % 2][0:n],
                                            W["down_hi"][0:n, u, :].bitcast(F32).rearrange("h (p j) -> h j p", j=4),
                                            ALU.subtract).then_inc(lo2_done, 1)
            u = HC - 1
            dve.wait_ge(hi2_done, u + 1)
            nc.vector.tensor_tensor(W["down_lo"][0:HTAIL, u, :].rearrange("h (p j) -> h j p", j=4), bank[2 + u % 2][0:HTAIL],
                                    W["down_hi"][0:HTAIL, u, :].bitcast(F32).rearrange("h (p j) -> h j p", j=4),
                                    ALU.subtract).then_inc(lo2_done, 1)
            dve.wait_ge(par_ready, 64)
            chain.link(nc.vector.tensor_tensor(row_scale[:, :], wmean[:, :], par_scale[:, :], ALU.mult))
            nc.vector.tensor_copy(W["qk_scale"][:, :], row_scale[:, 0:DC + 1]).then_inc(row_ready, 1)

        @block.scalar
        def _(act):
            def high_part(ch, w):
                n = rows(ch)
                cols = bass.ds(ch * P, n) if not isinstance(ch, int) else slice(ch * P, ch * P + n)
                act.wait_ge(deq_used, 2 * ch + w + 1 + FREE)
                nc.scalar.copy(W["up_hi"][w][:, :, cols], bank[w][:, :, 0:n]).then_inc(hi_done, 1)

            with act.Fori(0, FULL) as ch:
                for w in range(2):
                    high_part(ch, w)
            for w in range(2):
                high_part(FULL, w)
            for u in range(HC):
                n = P if u < FULL else HTAIL
                act.wait_ge(tr2_ready, u + 1)
                nc.scalar.copy(W["down_hi"][0:n, u, :].rearrange("h (p j) -> h j p", j=4), bank[2 + u % 2][0:n]).then_inc(hi2_done, 1)
                if u < NS:
                    act.wait_ge(wrecip_ready, u + 1)
                    if u >= 2:
                        act.wait_ge(sign_tr, u - 1)
                    nc.scalar.activation(wsign[u % 2][:, :], wrow[u % 2][:, :], ACT.Sign,
                                         scale=wrecip[:, u:u + 1]).then_inc(wrow_used, 1)
                    act.wait_ge(sign_tr, u + 1)
                    name, j = SIGN[u]
                    if name == "wo":
                        out = W["o_sign"][:, :, j * P:(j + 1) * P]
                    else:
                        at = {"wq": 0, "wk": D, "wv": D + KVD}[name] + j * P
                        out = W["qkv_sign"][:, :, at:at + P]
                    nc.scalar.copy(out, bank[u % 2][:, :, :]).then_inc(sign_out, 1)

        @block.tensor
        def _(pe):
            pe.sem_inc(deq_used, FREE)
            pe.wait_ge(ident_ready, 1)

            def turn(ch, w):
                n = rows(ch)
                pe.wait_ge(deq_ready, 2 * ch + w + 1)
                pe.wait_ge(lo_done, 2 * ch + FREE)
                for k in range(DC):
                    last = nc.tensor.transpose(bank[w][:, k, 0:n], deq[w][0:n, k].rearrange("p h c -> p (h c)"), ident[0:n, 0:n])
                last.then_inc(deq_used, 1)

            turn_all(pe, turn, FULL)
            pe.wait_ge(deq2_ready, 1)
            d2 = deq2.rearrange("p r h c -> p (r h c)").rearrange("p (j n) -> p j n", j=4)
            for u in range(HC):
                n = P if u < FULL else HTAIL
                if u >= 2:
                    pe.wait_ge(lo2_done, u - 1)
                for j in range(4):
                    last = nc.tensor.transpose(bank[2 + u % 2][0:n, j, :], d2[:, j, u * P:u * P + n], ident[:, :])
                last.then_inc(tr2_ready, 1)
                if u < NS:
                    if u < 2:
                        pe.wait_ge(lo_done, 2 * HC + FREE)
                    else:
                        pe.wait_ge(sign_out, u - 1)
                    pe.wait_ge(wrow_used, u + 1)
                    for k in range(DC):
                        last = nc.tensor.transpose(bank[u % 2][:, k, :], wsign[u % 2][:, k * P:(k + 1) * P], ident[:, :])
                    last.then_inc(sign_tr, 1)


def turn_all(pe, turn, full):
    with pe.Fori(0, full) as ch:
        turn(ch, 0)
        turn(ch, 1)
    turn(full, 0)
    turn(full, 1)


def ffn(nc, sem, tag, W, src, dst):
    with ExitStack() as c:
        sb = lambda n, s, d: c.enter_context(nc.sbuf_tensor(f"{tag}_{n}", s, d))
        S = lambda n: sem(f"{tag}_{n}")
        up_bank = [[c.enter_context(nc.psum_tensor(f"{tag}_up{i}{w}", [P, TT], F32)) for w in range(2)] for i in range(2)]
        y_bank = [c.enter_context(nc.psum_tensor(f"{tag}_y{s}", [P, D], F32)) for s in range(SUB)]
        turn_bank = [up_bank[1][0], up_bank[1][1], up_bank[0][0], up_bank[1][0]]
        xin = sb("xin", [P, SUB, D], F32)
        xres = sb("xres", [P, SUB, D], F32)
        xT_hi, xT_lo = sb("xT_hi", [P, DC, TT], F32R), sb("xT_lo", [P, DC, TT], F32R)
        sil, h = sb("sil", [P, TT], F32), sb("h", [P, TT], F32)
        h_hi = [sb(f"h_hi{i}", [P, TT], F32R) for i in range(2)]
        h_lo = [sb(f"h_lo{i}", [P, TT], F32R) for i in range(2)]
        stats, mv = sb("stats", [P, SUB, 6], F32), sb("mv", [P, SUB, 2], F32)
        ve, rstd, tmp = sb("ve", [P, SUB], F32), sb("rstd", [P, SUB], F32), sb("tmp", [P, SUB], F32)

        xin_ready, xres_ready, out_stored = S("xin_ready"), S("xres_ready"), S("out_stored")
        stats_ready, rstd_ready, xn_ready = S("stats_ready"), S("rstd_ready"), S("xn_ready")
        turned, xT_hi_done, xT_lo_done = S("turned"), S("xT_hi_done"), S("xT_lo_done")
        up_ready, a_read, b_read, hi_done, lo_done = (S(n) for n in ("up_ready", "a_read", "b_read", "h_hi_done", "h_lo_done"))
        down_done, y_done = S("down_done"), S("y_done")
        dve_chain, pool_chain = S("dve_chain"), S("pool_chain")
        rows = lambda m: P if m < HC - 1 else HTAIL
        tile = lambda ap, t: (ap[bass.ds(t * TT, TT), :] if not isinstance(t, int) else ap[t * TT:(t + 1) * TT, :]
                              ).rearrange("(s p) d -> p s d", p=P)

        block = c.enter_context(nc.Block())

        @block.sync
        def _(sp):
            def load_in(t):
                sp.wait_ge(turned, SUB * t)
                sp.dma_start(xin[:, :, :], tile(src, t)).then_inc(xin_ready, 16)

            def residual(t):
                sp.wait_ge(out_stored, 16 * t + FREE)
                sp.dma_start(xres[:, :, :], tile(src, t)).then_inc(xres_ready, 16)

            def store(t):
                sp.wait_ge(y_done, SUB * (t + 1) + FREE)
                sp.dma_start(tile(dst, t), xres[:, :, :]).then_inc(out_stored, 16)

            sp.sem_inc(out_stored, FREE)
            load_in(0)
            with sp.Fori(0, NT - 1) as t:
                residual(t)
                load_in(t + 1)
                store(t)
            residual(NT - 1)
            store(NT - 1)
            sp.wait_ge(out_stored, 16 * NT + FREE)

        @block.gpsimd
        def _(pool):
            chain = Chain(pool, pool_chain, S("pool_apart"))
            with pool.Fori(0, NT) as t:
                chain.enter(t * RSTD_LINKS)
                pool.wait_ge(stats_ready, t + 1)
                pool.wait_ge(xn_ready, t + FREE)
                pool.sem_inc(chain.apart, 1)
                rstd_on_pool(nc, chain, mv, ve, rstd, tmp, W["neg_half"], rstd_ready)

        @block.vector
        def _(dve):
            chain = Chain(dve, dve_chain, S("dve_apart"))
            PER_TILE = SUB

            def stats_of(t):
                dve.wait_ge(xin_ready, 16 * (t + 1))
                dve.wait_ge(rstd_ready, t)
                chain.enter(t * PER_TILE)
                layernorm_stats(nc, dve, chain, xin, stats, mv, stats_ready)

            def normalise(t):
                dve.wait_ge(rstd_ready, t + 1)
                for s in range(SUB):
                    last = nc.vector.tensor_scalar(xin[:, s, :], xin[:, s, :], mv[:, s, 0:1], rstd[:, s:s + 1],
                                                   ALU.subtract, ALU.mult)
                last.then_inc(xn_ready, 1)

            def xT_low(t):
                for s in range(SUB):
                    dve.wait_ge(xT_hi_done, SUB * t + s + 1)
                    nc.vector.tensor_tensor(xT_lo[:, :, s * P:(s + 1) * P],
                                            turn_bank[s][:, :].rearrange("p (k n) -> p k n", k=DC),
                                            xT_hi[:, :, s * P:(s + 1) * P].bitcast(F32), ALU.subtract).then_inc(xT_lo_done, 1)

            def main(t, has_next):
                for m in range(HC):
                    n, c0 = rows(m), t * HC + m
                    dve.wait_ge(a_read, c0 + 1)
                    dve.wait_ge(hi_done, c0 + FREE)
                    dve.wait_ge(lo_done, c0 + FREE)
                    nc.vector.tensor_tensor(h[0:n], sil[0:n], up_bank[m % 2][1][0:n, :], ALU.mult).then_inc(b_read, 1)
                    dve.wait_ge(hi_done, c0 + 1 + FREE)
                    nc.vector.tensor_tensor(h_lo[m % 2][0:n], h[0:n], h_hi[m % 2][0:n].bitcast(F32),
                                            ALU.subtract).then_inc(lo_done, 1)
                    if m == 2 and has_next:
                        stats_of(t + 1)
                    if m == 4 and has_next:
                        normalise(t + 1)
                if has_next:
                    xT_low(t + 1)
                dve.wait_ge(xres_ready, 16 * (t + 1))
                dve.wait_ge(down_done, HC * (t + 1) + FREE)
                for s in range(SUB):
                    nc.vector.scalar_tensor_tensor(xres[:, s, :], y_bank[s][:, :], 0.5, xres[:, s, :],
                                                   ALU.mult, ALU.add).then_inc(y_done, 1)

            for signal in (b_read, lo_done, y_done, xn_ready):
                dve.sem_inc(signal, FREE)
            stats_of(0)
            normalise(0)
            xT_low(0)
            with dve.Fori(0, NT - 1) as t:
                main(t, True)
            main(NT - 1, False)

        @block.scalar
        def _(act):
            def xT_high(t):
                for s in range(SUB):
                    act.wait_ge(turned, SUB * t + s + 1)
                    nc.scalar.copy(xT_hi[:, :, s * P:(s + 1) * P],
                                   turn_bank[s][:, :].rearrange("p (k n) -> p k n", k=DC)).then_inc(xT_hi_done, 1)

            def main(t, has_next):
                for m in range(HC):
                    n, c0 = rows(m), t * HC + m
                    act.wait_ge(up_ready, c0 + 1)
                    act.wait_ge(b_read, c0 + FREE)
                    nc.scalar.activation(sil[0:n], up_bank[m % 2][0][0:n, :], ACT.Silu).then_inc(a_read, 1)
                    act.wait_ge(b_read, c0 + 1 + FREE)
                    act.wait_ge(down_done, t * HC + max(m - 1, 0) + FREE)
                    nc.scalar.copy(h_hi[m % 2][0:n], h[0:n]).then_inc(hi_done, 1)
                if has_next:
                    xT_high(t + 1)

            act.sem_inc(hi_done, FREE)
            xT_high(0)
            with act.Fori(0, NT - 1) as t:
                main(t, True)
            main(NT - 1, False)

        @block.tensor
        def _(pe):
            def turn(t, s):
                for k in range(DC):
                    last = nc.tensor.transpose(turn_bank[s][:, k * P:(k + 1) * P], xin[:, s, k * P:(k + 1) * P], W["ident"][:, :])
                last.then_inc(turned, 1)

            def up(t, m):
                n, c0 = rows(m), t * HC + m
                if m >= 2:
                    pe.wait_ge(a_read, c0 - 1)
                    pe.wait_ge(b_read, c0 - 1 + FREE)
                cols = slice(m * P, m * P + n)
                for w in range(2):
                    for k in range(DC):
                        parts = ((W["up_hi"], xT_hi), (W["up_hi"], xT_lo), (W["up_lo"], xT_hi))
                        for i, (wt, xt) in enumerate(parts):
                            last = nc.tensor.matmul(up_bank[m % 2][w][0:n, :], wt[w][:, k, cols], xt[:, k, :],
                                                    start=(k == 0 and i == 0), stop=(k == DC - 1 and i == 2))
                last.then_inc(up_ready, 1)

            def down(t, m):
                n, c0 = rows(m), t * HC + m
                if m == 0:
                    pe.wait_ge(y_done, SUB * t + FREE)
                pe.wait_ge(lo_done, c0 + 1 + FREE)
                for s in range(SUB):
                    cols = slice(s * P, (s + 1) * P)
                    parts = ((h_hi, W["down_hi"]), (h_lo, W["down_hi"]), (h_hi, W["down_lo"]))
                    for i, (ht, wt) in enumerate(parts):
                        last = nc.tensor.matmul(y_bank[s][:, :], ht[m % 2][0:n, cols], wt[0:n, m, :],
                                                start=(m == 0 and i == 0), stop=(m == HC - 1 and i == 2))
                last.then_inc(down_done, 1)

            def main(t, has_next):
                pe.wait_ge(xT_lo_done, SUB * (t + 1))
                up(t, 0)
                for m in range(1, HC):
                    up(t, m)
                    if m < HC - 1:
                        down(t, m - 1)
                if has_next:
                    pe.wait_ge(xn_ready, t + 2 + FREE)
                    pe.wait_ge(a_read, t * HC + HC - 1)
                    pe.wait_ge(b_read, t * HC + HC - 1 + FREE)
                    turn(t + 1, 0)
                    turn(t + 1, 1)
                down(t, HC - 2)
                if has_next:
                    pe.wait_ge(a_read, t * HC + HC)
                    pe.wait_ge(b_read, t * HC + HC + FREE)
                    turn(t + 1, 2)
                    pe.wait_ge(xT_lo_done, SUB * (t + 1) + 1)
                    turn(t + 1, 3)
                down(t, HC - 1)

            pe.sem_inc(down_done, FREE)
            pe.wait_ge(xn_ready, 1 + FREE)
            for s in range(SUB):
                if s == 3:
                    pe.wait_ge(xT_lo_done, 1)
                turn(0, s)
            with pe.Fori(0, NT - 1) as t:
                main(t, True)
            main(NT - 1, False)


def clean_on_pool(nc, chain, t, f, neg):
    g = nc.gpsimd
    chain.add(g.tensor_scalar(f, t, 0.0, FIN_LIMIT, ALU.max, ALU.min))
    chain.link(g.tensor_scalar(neg, t, 0.0, -FIN_LIMIT, ALU.min, ALU.max))
    return g.tensor_tensor(f, f, neg, ALU.add)


def projections(nc, sem, W, src, qparts, kparts, vaug):
    with ExitStack() as c:
        sb = lambda n, s, d: c.enter_context(nc.sbuf_tensor(f"qkv_{n}", s, d))
        S = lambda n: sem(f"qkv_{n}")
        turn_bank = [c.enter_context(nc.psum_tensor(f"qkv_turn{s}", [P, DC, P], F32)) for s in range(SUB)]
        mm_bank = [c.enter_context(nc.psum_tensor(f"qkv_mm{i}", [P, TT], F32)) for i in range(2)]
        xin = sb("xin", [P, SUB, D], F32)
        xT_hi, xT_lo = sb("xT_hi", [P, DC, TT], F16), sb("xT_lo", [P, DC, TT], F16)
        raw = [sb(f"raw{i}", [P, TT], F32) for i in range(2)]
        fin = [sb(f"fin{i}", [P, TT], F32) for i in range(2)]
        neg, rest = sb("neg", [P, TT], F32), sb("rest", [P, TT], F32)
        mask = sb("mask", [P, TT], I32)
        parts = [sb(f"parts{i}", [P, 3, TT], BF16) for i in range(2)]
        vt = sb("vt", [P, NKV, SUB, 2 * HD], F32)
        stats, mv = sb("stats", [P, SUB, 6], F32), sb("mv", [P, SUB, 2], F32)
        ve, rstd, tmp = sb("ve", [P, SUB], F32), sb("rstd", [P, SUB], F32), sb("tmp", [P, SUB], F32)

        xin_ready, stats_ready, rstd_ready, xn_ready = (S(n) for n in ("xin_ready", "stats_ready", "rstd_ready", "xn_ready"))
        turned, xT_hi_done, xT_lo_done = S("turned"), S("xT_hi_done"), S("xT_lo_done")
        mm_ready, scaled, v_scaled = S("mm_ready"), S("scaled"), S("v_scaled")
        pool_cleaned, cleaned = S("pool_cleaned"), S("cleaned")
        part1_done, rest_done, part2_done, part3_done = (S(n) for n in ("part1_done", "rest_done", "part2_done", "part3_done"))
        v_placed, v_stored, ones_set = S("v_placed"), S("v_stored"), S("ones_set")
        parts_stored = [S(f"parts_stored{i}") for i in range(2)]
        dve_chain, pool_chain = S("dve_chain"), S("pool_chain")
        NQK = DC + 1
        V = NQK
        UNITS = NQK + 1
        stores_before = lambda t, u: ((NQK + 1) // 2 if u % 2 == 0 else NQK // 2) * t + u // 2
        rowsof = lambda t: bass.ds(t * TT, TT) if not isinstance(t, int) else slice(t * TT, (t + 1) * TT)

        block = c.enter_context(nc.Block())

        @block.sync
        def _(sp):
            for signal in (parts_stored[0], parts_stored[1], v_stored):
                sp.sem_inc(signal, FREE)
            sp.dma_start(xin[:, :, :], src[0:TT, :].rearrange("(s p) d -> p s d", p=P)).then_inc(xin_ready, 16)

            def main(t, has_next):
                if has_next:
                    sp.wait_ge(turned, SUB * (t + 1))
                    sp.dma_start(xin[:, :, :], src[rowsof(t + 1), :].rearrange("(s p) d -> p s d", p=P)).then_inc(xin_ready, 16)
                b, half = t // 2, t % 2
                cols = bass.ds(half * TT, TT)
                for u in range(NQK):
                    sp.wait_ge(part3_done, NQK * t + u + 1 + FREE)
                    dst, row = (qparts, b * D + u * P) if u < DC else (kparts, b * KVD)
                    sp.dma_start(dst[:, bass.ds(row, P), cols].rearrange("a r t -> r a t"),
                                 parts[u % 2][:, :, :]).then_inc(parts_stored[u % 2], 16)
                sp.wait_ge(v_placed, t + 1 + FREE)
                dst = vaug.rearrange("(b k) h p s c -> b h p k (s c)", b=BATCH)
                sp.dma_start(dst[bass.ds(b, 1), bass.ds(half, 1)].rearrange("a o p k n -> (a o p) k n"),
                             vt.rearrange("p k s c -> p k (s c)")).then_inc(v_stored, 16)

            with sp.Fori(0, NT - 1) as t:
                main(t, True)
            main(NT - 1, False)
            sp.wait_ge(parts_stored[0], 16 * stores_before(NT, 0) + FREE)
            sp.wait_ge(parts_stored[1], 16 * stores_before(NT, 1) + FREE)
            sp.wait_ge(v_stored, 16 * NT + FREE)

        def wait_scaled(eng, t, u):
            if u < V:
                eng.wait_ge(scaled, NQK * t + u + 1 + FREE)
            else:
                eng.wait_ge(v_scaled, t + 1 + FREE)

        @block.gpsimd
        def _(pool):
            chain = Chain(pool, pool_chain, S("pool_apart"))
            nc.gpsimd.memset(vt[:, :, :, :], 1.0).then_inc(ones_set, 1)
            PER_TILE = RSTD_LINKS + 2 * UNITS

            def rstd_of(t):
                pool.wait_ge(stats_ready, t + 1)
                pool.wait_ge(xn_ready, t + FREE)
                pool.sem_inc(chain.apart, 1)
                rstd_on_pool(nc, chain, mv, ve, rstd, tmp, W["neg_half"], rstd_ready)

            def main(t, has_next):
                chain.enter(RSTD_LINKS + t * PER_TILE)
                for u in range(UNITS):
                    wait_scaled(pool, t, u)
                    if u == 1:
                        pool.wait_ge(v_placed, t + FREE)
                    else:
                        pool.wait_ge(rest_done, NQK * t + max(u - 1, 0) + FREE)
                    pool.wait_ge(pool_cleaned, UNITS * t + u + FREE)
                    pool.sem_inc(chain.apart, 1)
                    clean_on_pool(nc, chain, raw[u % 2][:, :], fin[u % 2][:, :], neg[:, :]).then_inc(pool_cleaned, 1)
                    if u == 2 and has_next:
                        rstd_of(t + 1)

            for signal in (pool_cleaned, rstd_ready):
                pool.sem_inc(signal, FREE)
            rstd_of(0)
            with pool.Fori(0, NT - 1) as t:
                main(t, True)
            main(NT - 1, False)

        @block.vector
        def _(dve):
            chain = Chain(dve, dve_chain, S("dve_apart"))
            PER_TILE = SUB + UNITS

            def stats_of(t):
                dve.wait_ge(xin_ready, 16 * (t + 1))
                dve.wait_ge(rstd_ready, t + FREE)
                layernorm_stats(nc, dve, chain, xin, stats, mv, stats_ready)

            def normalise(t):
                dve.wait_ge(rstd_ready, t + 1 + FREE)
                for s in range(SUB):
                    last = nc.vector.tensor_scalar(xin[:, s, :], xin[:, s, :], mv[:, s, 0:1], rstd[:, s:s + 1],
                                                   ALU.subtract, ALU.mult)
                last.then_inc(xn_ready, 1)

            def xT_low(t):
                for s in range(SUB):
                    dve.wait_ge(xT_hi_done, SUB * t + s + 1)
                    nc.vector.tensor_tensor(xT_lo[:, :, s * P:(s + 1) * P], turn_bank[s][:, :, :],
                                            xT_hi[:, :, s * P:(s + 1) * P], ALU.subtract).then_inc(xT_lo_done, 1)

            def main(t, has_next):
                chain.enter(SUB + t * PER_TILE)
                for u in range(UNITS):
                    i = u % 2
                    if u == V:
                        dve.wait_ge(mm_ready, UNITS * t + u + 1)
                        dve.wait_ge(pool_cleaned, UNITS * t + u - 1 + FREE)
                        dve.wait_ge(cleaned, UNITS * t + u - 1 + FREE)
                        nc.vector.tensor_tensor(raw[i][:, :].rearrange("p (s c) -> p s c", s=SUB),
                                                mm_bank[i][:, :].rearrange("p (s c) -> p s c", s=SUB),
                                                W["vo_scale"][:, 0:KVD].unsqueeze(1).to_broadcast([P, SUB, KVD]),
                                                ALU.mult).then_inc(v_scaled, 1)
                    wait_scaled(dve, t, u)
                    dve.wait_ge(cleaned, UNITS * t + u + FREE)
                    chain.add(nc.vector.tensor_scalar(mask[:, :], raw[i][:, :], 0.0, 0.0, ALU.mult, ALU.is_equal))
                    chain.wait()
                    dve.wait_ge(pool_cleaned, UNITS * t + u + 1 + FREE)
                    dve.sem_inc(chain.apart, 1)
                    nc.vector.copy_predicated(fin[i][:, :], mask[:, :], raw[i][:, :]).then_inc(cleaned, 1)
                    if u < NQK:
                        dve.wait_ge(part1_done, NQK * t + u + 1)
                        dve.wait_ge(part3_done, NQK * t + u + FREE)
                        dve.wait_ge(rest_done, NQK * t + u + FREE)
                        nc.vector.scalar_tensor_tensor(rest[:, :], fin[i][:, :], HD ** -0.5 if u < DC else 1.0,
                                                       parts[i][:, 0, :], ALU.mult, ALU.subtract).then_inc(rest_done, 1)
                        dve.wait_ge(part2_done, NQK * t + u + 1)
                        dve.wait_ge(rest_done, NQK * t + u + 1 + FREE)
                        nc.vector.tensor_tensor(parts[i][:, 2, :], rest[:, :], parts[i][:, 1, :],
                                                ALU.subtract).then_inc(part3_done, 1)
                    if u == 1 and has_next:
                        stats_of(t + 1)
                    if u == 3 and has_next:
                        normalise(t + 1)
                if has_next:
                    xT_low(t + 1)

            for signal in (v_scaled, cleaned, rest_done, part3_done, xn_ready):
                dve.sem_inc(signal, FREE)
            stats_of(0)
            normalise(0)
            xT_low(0)
            with dve.Fori(0, NT - 1) as t:
                main(t, True)
            main(NT - 1, False)

        @block.scalar
        def _(act):
            def xT_high(t):
                for s in range(SUB):
                    act.wait_ge(turned, SUB * t + s + 1)
                    nc.scalar.copy(xT_hi[:, :, s * P:(s + 1) * P], turn_bank[s][:, :, :]).then_inc(xT_hi_done, 1)

            def scale(t, u):
                act.wait_ge(mm_ready, UNITS * t + u + 1)
                act.wait_ge(cleaned, UNITS * t + u - 1 + FREE)
                nc.scalar.activation(raw[u % 2][:, :], mm_bank[u % 2][:, :], ACT.Copy,
                                     scale=W["qk_scale"][:, u:u + 1]).then_inc(scaled, 1)

            def main(t, has_next):
                scale(t, 0)
                for u in range(NQK):
                    if u + 1 < NQK:
                        scale(t, u + 1)
                    i = u % 2
                    act.wait_ge(cleaned, UNITS * t + u + 1 + FREE)
                    act.wait_ge(parts_stored[i], 16 * stores_before(t, u) + FREE)
                    nc.scalar.mul(parts[i][:, 0, :], fin[i][:, :], HD ** -0.5 if u < DC else 1.0).then_inc(part1_done, 1)
                    act.wait_ge(rest_done, NQK * t + u + 1 + FREE)
                    nc.scalar.copy(parts[i][:, 1, :], rest[:, :]).then_inc(part2_done, 1)
                act.wait_ge(cleaned, UNITS * (t + 1) + FREE)
                act.wait_ge(v_stored, 16 * t + FREE)
                nc.scalar.copy(vt[:, :, :, 0:HD], fin[V % 2][:, :].rearrange("p (s k c) -> p k s c", s=SUB, k=NKV)
                               ).then_inc(v_placed, 1)
                if has_next:
                    xT_high(t + 1)

            for signal in (scaled, v_placed):
                act.sem_inc(signal, FREE)
            act.wait_ge(ones_set, 1)
            xT_high(0)
            with act.Fori(0, NT - 1) as t:
                main(t, True)
            main(NT - 1, False)

        @block.tensor
        def _(pe):
            def turn(t, s):
                for k in range(DC):
                    last = nc.tensor.transpose(turn_bank[s][:, k, :], xin[:, s, k * P:(k + 1) * P], W["ident"][:, :])
                last.then_inc(turned, 1)

            def main(t, has_next):
                pe.wait_ge(xT_lo_done, SUB * (t + 1))
                for u in range(UNITS):
                    if u == 1:
                        pe.wait_ge(v_scaled, t + FREE)
                    else:
                        pe.wait_ge(scaled, NQK * t + max(u - 1, 0) + FREE)
                    if u < V:
                        for k in range(DC):
                            for i, xt in enumerate((xT_hi, xT_lo)):
                                last = nc.tensor.matmul(mm_bank[u % 2][:, :], W["qkv_sign"][:, k, u * P:(u + 1) * P], xt[:, k, :],
                                                        start=(k == 0 and i == 0), stop=(k == DC - 1 and i == 1))
                    else:
                        for s in range(SUB):
                            cols = slice(s * P, (s + 1) * P)
                            for k in range(DC):
                                for i, xt in enumerate((xT_hi, xT_lo)):
                                    last = nc.tensor.matmul(mm_bank[u % 2][:, cols], xt[:, k, cols], W["qkv_sign"][:, k, D + KVD:],
                                                            start=(k == 0 and i == 0), stop=(k == DC - 1 and i == 1))
                    last.then_inc(mm_ready, 1)
                if has_next:
                    pe.wait_ge(xn_ready, t + 2 + FREE)
                    for s in range(SUB):
                        turn(t + 1, s)

            pe.wait_ge(xn_ready, 1 + FREE)
            for s in range(SUB):
                turn(0, s)
            with pe.Fori(0, NT - 1) as t:
                main(t, True)
            main(NT - 1, False)


PARTS_OF_BLOCK = ((0, 0), (0, 1), (1, 0), (1, 1), (0, 2), (2, 0))
NBLK = len(PARTS_OF_BLOCK)
SROWS = NBLK * HD
MAXROW = SROWS
QT = SEQ // P
NG = BATCH * NKV


def attention(nc, sem, W, qparts, kparts, vaug, attn_out):
    with ExitStack() as c:
        sb = lambda n, s, d: c.enter_context(nc.sbuf_tensor(f"at_{n}", s, d))
        pb = lambda n, s: c.enter_context(nc.psum_tensor(f"at_{n}", s, F32))
        S = lambda n: sem(f"at_{n}")
        max_bank = [pb(f"max{i}", [P, SEQ]) for i in range(2)]
        s_bank = [pb(f"s{i}", [P, TT]) for i in range(2)]
        o_bank, turn_bank = pb("o", [P, TT]), pb("turn", [P, SUB, P])
        qst = [sb(f"qst{i}", [P, REP, SEQ], BF16) for i in range(2)]
        kst = [sb(f"kst{i}", [P, SEQ], BF16) for i in range(2)]
        vst = [sb(f"vst{i}", [P, QT, 2 * HD], F32) for i in range(2)]
        prob = [sb(f"prob{i}", [P, REP, TT], F32) for i in range(2)]
        negmax = sb("negmax", [P, REP * QT], F32)
        mrest = sb("mrest", [REP * QT, P], F32)
        mparts = sb("mparts", [REP * QT, 3, P], BF16)
        osb = sb("osb", [P, TT], F32)
        recip = sb("recip", [P, SUB, REP], F32)
        out = sb("out", [P, QT, REP, HD], F32)

        q_ready = [[S(f"q_ready{i}{h}") for h in range(2)] for i in range(2)]
        k_ready, v_ready = [S(f"k_ready{i}") for i in range(2)], [S(f"v_ready{i}") for i in range(2)]
        rows_set = S("rows_set")
        max_ready, max_read, max_turned, mparts_done, maxrow_ready = (S(n) for n in (
            "max_ready", "max_read", "max_turned", "mparts_done", "maxrow_ready"))
        s_ready, exp_done, pv_done = S("s_ready"), S("exp_done"), S("pv_done")
        o_copied, o_turned, o_normed, out_stored = (S(n) for n in ("o_copied", "o_turned", "o_normed", "out_stored"))
        dve_chain = S("dve_chain")
        NQ = 2 * QT
        NS = NQ * REP
        NM = REP * QT
        QM0, QM1 = 1, 14
        units_by = [0] * QM0 + [-(-(n - QM0 + 1) * NM // (QM1 - QM0)) for n in range(QM0, QM1)] + [NM] * (NQ - QM1)
        units_of = lambda n: range(units_by[n - 1] if n else 0, units_by[n])
        TURN0 = QT + 1
        HALVES = SEQ // TT
        LINKS = 2 * HALVES

        block = c.enter_context(nc.Block())

        @block.sync
        def _(sp):
            def load_q(g, i, half):
                rows = bass.ds(g * (REP * HD), REP * HD) if not isinstance(g, int) else slice(g * REP * HD, (g + 1) * REP * HD)
                for b, (part, _) in enumerate(PARTS_OF_BLOCK):
                    sp.dma_start(qst[i][b * HD:(b + 1) * HD, :, half * TT:(half + 1) * TT],
                                 qparts[part, rows, half * TT:(half + 1) * TT].rearrange("(h d) t -> d h t", h=REP)
                                 ).then_inc(q_ready[i][half], 16)

            def load_k(g, i):
                rows = bass.ds(g * HD, HD) if not isinstance(g, int) else slice(g * HD, (g + 1) * HD)
                for b, (_, part) in enumerate(PARTS_OF_BLOCK):
                    sp.dma_start(kst[i][b * HD:(b + 1) * HD, :], kparts[part, rows, :]).then_inc(k_ready[i], 16)

            def load_v(g, i):
                src = vaug[bass.ds(g, 1)] if not isinstance(g, int) else vaug[g:g + 1]
                sp.dma_start(vst[i][:, :, :].rearrange("p (h s) c -> p h (s c)", h=HALVES),
                             src.rearrange("o h p s c -> p (o h) (s c)")).then_inc(v_ready[i], 16)

            def max_rows(g, i):
                sp.wait_ge(mparts_done, g + 1 + FREE)
                for part in range(3):
                    sp.dma_start(qst[i][MAXROW + part:MAXROW + part + 1, :, :].rearrange("o h (t p) -> o (h t) p", p=P),
                                 mparts[:, part, :]).then_inc(maxrow_ready, 16)

            def group(g, i, has_next, has_load):
                if has_load:
                    sp.wait_ge(s_ready, NS * g + NS // 2)
                    load_q(g + 2, i, 0)
                if has_next:
                    max_rows(g + 1, 1 - i)
                if has_load:
                    sp.wait_ge(s_ready, NS * (g + 1))
                    load_k(g + 2, i)
                    load_q(g + 2, i, 1)
                    sp.wait_ge(pv_done, NQ * (g + 1) + FREE)
                    load_v(g + 2, i)
                sp.wait_ge(o_normed, HALVES * (g + 1) + FREE)
                dst = attn_out[bass.ds(g, 1)] if not isinstance(g, int) else attn_out[g:g + 1]
                sp.dma_start(dst.rearrange("o (t p) c -> (o p) t c", p=P),
                             out.rearrange("p t h d -> p t (h d)")).then_inc(out_stored, 16)

            for signal in (maxrow_ready, out_stored):
                sp.sem_inc(signal, FREE)
            for i in range(2):
                load_k(i, i)
                load_q(i, i, 0)
                load_q(i, i, 1)
                load_v(i, i)
            sp.wait_ge(rows_set, 4)
            max_rows(0, 0)
            with sp.Fori(0, NG // 2 - 1) as pair:
                for i in range(2):
                    group(pair * 2 + i, i, True, True)
            group(NG - 2, 0, True, False)
            group(NG - 1, 1, False, False)
            sp.wait_ge(out_stored, 16 * NG + FREE)

        @block.gpsimd
        def _(pool):
            for i in range(2):
                nc.gpsimd.memset(qst[i][MAXROW:P, :, :], 0.0).then_inc(rows_set, 1)
                nc.gpsimd.memset(kst[i][MAXROW:P, :], 1.0).then_inc(rows_set, 1)

        @block.vector
        def _(dve):
            chain = Chain(dve, dve_chain)

            def max_unit(g, j):
                col = (j % REP) * QT + j // REP
                if j == 0:
                    dve.wait_ge(max_turned, g + FREE)
                dve.wait_ge(max_ready, NM * g + j + 1)
                nc.vector.tensor_reduce(negmax[:, col:col + 1], max_bank[j % 2][:, :], AX.X, ALU.max,
                                        negate=True).then_inc(max_read, 1)

            def split_max(g):
                dve.wait_ge(max_turned, g + 1 + FREE)
                dve.wait_ge(maxrow_ready, 48 * g + FREE)
                m = turn_bank[0:REP * QT, 0, :]
                chain.link(nc.vector.tensor_copy(mparts[:, 0, :], m))
                chain.link(nc.vector.tensor_tensor(mrest[:, :], m, mparts[:, 0, :], ALU.subtract))
                chain.link(nc.vector.tensor_copy(mparts[:, 1, :], mrest[:, :]))
                nc.vector.tensor_tensor(mparts[:, 2, :], mrest[:, :], mparts[:, 1, :], ALU.subtract).then_inc(mparts_done, 1)

            def normalise(g, half):
                dve.wait_ge(o_turned, HALVES * g + half + 1 + FREE)
                if half == 0:
                    dve.wait_ge(out_stored, 16 * g + FREE)
                t = turn_bank[:, :, :].rearrange("p s (h e) -> p s h e", h=REP)
                chain.link(nc.vector.reciprocal(recip[:, :, :], t[:, :, :, HD]))
                nc.vector.tensor_tensor(out[:, half * SUB:(half + 1) * SUB, :, :], t[:, :, :, 0:HD],
                                        recip[:, :, :].unsqueeze(3).to_broadcast([P, SUB, REP, HD]),
                                        ALU.mult).then_inc(o_normed, 1)
                dve.wait_ge(o_normed, HALVES * g + half + 1 + FREE)

            def group(g, has_next):
                for n in range(NQ):
                    if has_next:
                        for j in units_of(n):
                            max_unit(g + 1, j)
                    if n == TURN0:
                        normalise(g, 0)
                    if n == QM1 and has_next:
                        split_max(g + 1)
                normalise(g, 1)

            for signal in (max_read, mparts_done, o_normed):
                dve.sem_inc(signal, FREE)
            for j in range(NM):
                max_unit(0, j)
            split_max(0)
            per_group = 3 + HALVES
            with dve.Fori(0, NG // 2 - 1) as pair:
                chain.enter(pair * (2 * per_group) + 3)
                for i in range(2):
                    group(pair * 2 + i, True)
            chain.enter((NG - 2) * per_group + 3)
            group(NG - 2, True)
            group(NG - 1, False)

        @block.scalar
        def _(act):
            def group(g):
                for n in range(NQ):
                    act.wait_ge(pv_done, NQ * g + max(n - 1, 0) + FREE)
                    for h in range(REP):
                        s = n * REP + h
                        act.wait_ge(s_ready, NS * g + s + 1)
                        nc.scalar.activation(prob[n % 2][:, h, :], s_bank[s % 2][:, :], ACT.Exp).then_inc(exp_done, 1)
                    if n == QT:
                        copy_out(g, 0)
                copy_out(g, 1)

            def copy_out(g, half):
                act.wait_ge(pv_done, NQ * g + (half + 1) * QT + FREE)
                act.wait_ge(o_turned, HALVES * g + half + FREE)
                nc.scalar.copy(osb[:, :], o_bank[:, :]).then_inc(o_copied, 1)

            act.sem_inc(o_copied, FREE)
            with act.Fori(0, NG) as g:
                group(g)

        @block.tensor
        def _(pe):
            def max_unit(g, i, k, j):
                t, h = j // REP, j % REP
                if j == 0:
                    pe.wait_ge(k_ready[i], 16 * NBLK * (k + 1))
                    pe.wait_ge(q_ready[i][0], 16 * NBLK * (k + 1))
                if j == NM // 2:
                    pe.wait_ge(q_ready[i][1], 16 * NBLK * (k + 1))
                pe.wait_ge(max_read, NM * g + j - 1 + FREE)
                for half in range(HALVES):
                    last = nc.tensor.matmul(max_bank[j % 2][:, half * TT:(half + 1) * TT], qst[i][0:SROWS, h, t * P:(t + 1) * P],
                                            kst[i][0:SROWS, half * TT:(half + 1) * TT], start=True, stop=True)
                last.then_inc(max_ready, 1)

            def turn_max(g):
                pe.wait_ge(max_read, NM * (g + 1) + FREE)
                pe.wait_ge(mparts_done, g + FREE)
                pe.wait_ge(o_normed, max(HALVES * g - 1, 0) + FREE if isinstance(g, int) else HALVES * g - 1 + FREE)
                nc.tensor.transpose(turn_bank[0:REP * QT, 0, :], negmax[:, :], W["ident"][:, :]).then_inc(max_turned, 1)

            def scores(g, i, n, h):
                s, half, kt = n * REP + h, n // QT, n % QT
                pe.wait_ge(exp_done, NS * g + s - 1 + FREE)
                nc.tensor.matmul(s_bank[s % 2][:, :], kst[i][:, kt * P:(kt + 1) * P], qst[i][:, h, half * TT:(half + 1) * TT],
                                 start=True, stop=True).then_inc(s_ready, 1)

            def values(g, i, n):
                half, kt = n // QT, n % QT
                pe.wait_ge(exp_done, NS * g + (n + 1) * REP + FREE)
                if kt == 0:
                    pe.wait_ge(o_copied, HALVES * g + half + FREE)
                for h in range(REP):
                    last = nc.tensor.matmul(o_bank[32 * h:32 * h + 32, :], vst[i][:, kt, :], prob[n % 2][:, h, :],
                                            start=(kt == 0), stop=(kt == QT - 1), tile_position=(0, 32 * h))
                last.then_inc(pv_done, 1)

            def turn_out(g, half, has_next):
                pe.wait_ge(o_copied, HALVES * g + half + 1 + FREE)
                pe.wait_ge(o_normed, HALVES * g + half + FREE)
                pe.wait_ge(mparts_done, g + (2 if half and has_next else 1) + FREE)
                for s in range(SUB):
                    last = nc.tensor.transpose(turn_bank[:, s, :], osb[:, s * P:(s + 1) * P], W["ident"][:, :])
                last.then_inc(o_turned, 1)

            def group(g, i, k, has_next):
                pe.wait_ge(maxrow_ready, 48 * (g + 1) + FREE)
                for n in range(NQ):
                    units = list(units_of(n)) if has_next else []
                    scores(g, i, n, 0)
                    scores(g, i, n, 1)
                    for j in units[0:1]:
                        max_unit(g + 1, 1 - i, k + i, j)
                    scores(g, i, n, 2)
                    scores(g, i, n, 3)
                    for j in units[1:]:
                        max_unit(g + 1, 1 - i, k + i, j)
                    if n == 1:
                        pe.wait_ge(v_ready[i], 16 * (k + 1))
                    if n >= 1:
                        values(g, i, n - 1)
                    if n == TURN0:
                        turn_out(g, 0, has_next)
                    if n == QM1 and has_next:
                        turn_max(g + 1)
                values(g, i, NQ - 1)
                turn_out(g, 1, has_next)

            for signal in (exp_done, pv_done, max_turned, o_turned):
                pe.sem_inc(signal, FREE)
            for j in range(NM):
                max_unit(0, 0, 0, j)
            turn_max(0)
            pe.wait_ge(rows_set, 4)
            with pe.Fori(0, NG // 2 - 1) as pair:
                for i in range(2):
                    group(pair * 2 + i, i, pair, True)
            group(NG - 2, 0, NG // 2 - 1, True)
            group(NG - 1, 1, NG // 2 - 1, False)


def output_projection(nc, sem, W, attn_out, src, dst):
    with ExitStack() as c:
        sb = lambda n, s, d: c.enter_context(nc.sbuf_tensor(f"op_{n}", s, d))
        S = lambda n: sem(f"op_{n}")
        turn_bank = [c.enter_context(nc.psum_tensor(f"op_turn{s}", [P, DC, P], F32)) for s in range(SUB)]
        mm_bank = [c.enter_context(nc.psum_tensor(f"op_mm{i}", [P, D], F32)) for i in range(2)]
        ain = sb("ain", [P, SUB, D], F32)
        res = sb("res", [P, SUB, D], F32)
        aT_hi, aT_lo = sb("aT_hi", [P, DC, TT], F32R), sb("aT_lo", [P, DC, TT], F32R)
        raw = [sb(f"raw{i}", [P, TT], F32) for i in range(2)]
        fin = [sb(f"fin{i}", [P, TT], F32) for i in range(2)]
        neg, mask = sb("neg", [P, TT], F32), sb("mask", [P, TT], I32)
        ain_ready, res_ready, stored, turned, hi_done, lo_done = (S(n) for n in (
            "ain_ready", "res_ready", "stored", "turned", "hi_done", "lo_done"))
        mm_ready, scaled, pool_cleaned, cleaned, added = (S(n) for n in ("mm_ready", "scaled", "pool_cleaned", "cleaned", "added"))
        rowsof = lambda t: bass.ds(t * TT, TT) if not isinstance(t, int) else slice(t * TT, (t + 1) * TT)
        attn_v = attn_out.rearrange("(b k) (h s p) c -> b h s p k c", b=BATCH, h=SEQ // TT, p=P)

        block = c.enter_context(nc.Block())

        @block.sync
        def _(sp):
            sp.sem_inc(stored, FREE)

            def load_in(t):
                sp.wait_ge(turned, SUB * t + FREE)
                for s in range(SUB):
                    view = attn_v[bass.ds(t // 2, 1), bass.ds(t % 2, 1), s]
                    sp.dma_start(ain[:, s, :].rearrange("p (k c) -> p k c", k=NKV),
                                 view.rearrange("b h p k c -> (b h p) k c")).then_inc(ain_ready, 16)

            def main(t, has_next):
                sp.wait_ge(stored, 16 * t + FREE)
                sp.dma_start(res[:, :, :], src[rowsof(t), :].rearrange("(s p) d -> p s d", p=P)).then_inc(res_ready, 16)
                if has_next:
                    load_in(t + 1)
                sp.wait_ge(added, SUB * (t + 1) + FREE)
                sp.dma_start(dst[rowsof(t), :].rearrange("(s p) d -> p s d", p=P), res[:, :, :]).then_inc(stored, 16)

            load_in(0)
            with sp.Fori(0, NT - 1) as t:
                main(t, True)
            main(NT - 1, False)
            sp.wait_ge(stored, 16 * NT + FREE)

        @block.gpsimd
        def _(pool):
            chain = Chain(pool, S("pool_chain"), S("pool_apart"))
            pool.sem_inc(pool_cleaned, FREE)
            with pool.Fori(0, NT) as t:
                chain.enter(t * (2 * SUB))
                for s in range(SUB):
                    pool.wait_ge(scaled, SUB * t + s + 1 + FREE)
                    pool.wait_ge(added, SUB * t + s - 1 + FREE)
                    pool.wait_ge(pool_cleaned, SUB * t + s + FREE)
                    pool.sem_inc(chain.apart, 1)
                    clean_on_pool(nc, chain, raw[s % 2][:, :], fin[s % 2][:, :], neg[:, :]).then_inc(pool_cleaned, 1)

        @block.vector
        def _(dve):
            chain = Chain(dve, S("dve_chain"), S("dve_apart"))
            for signal in (cleaned, added, scaled):
                dve.sem_inc(signal, FREE)
            with dve.Fori(0, NT) as t:
                chain.enter(t * SUB)
                for s in range(SUB):
                    dve.wait_ge(hi_done, SUB * t + s + 1)
                    nc.vector.tensor_tensor(aT_lo[:, :, s * P:(s + 1) * P], turn_bank[s][:, :, :],
                                            aT_hi[:, :, s * P:(s + 1) * P].bitcast(F32), ALU.subtract).then_inc(lo_done, 1)
                dve.wait_ge(res_ready, 16 * (t + 1))
                for s in range(SUB):
                    i = s % 2
                    dve.wait_ge(mm_ready, SUB * t + s + 1)
                    dve.wait_ge(cleaned, SUB * t + s - 1 + FREE)
                    nc.vector.tensor_tensor(raw[i][:, :], mm_bank[i][:, :], W["vo_scale"][:, KVD:], ALU.mult).then_inc(scaled, 1)
                    dve.wait_ge(scaled, SUB * t + s + 1 + FREE)
                    dve.wait_ge(cleaned, SUB * t + s + FREE)
                    chain.add(nc.vector.tensor_scalar(mask[:, :], raw[i][:, :], 0.0, 0.0, ALU.mult, ALU.is_equal))
                    chain.wait()
                    dve.wait_ge(pool_cleaned, SUB * t + s + 1 + FREE)
                    dve.sem_inc(chain.apart, 1)
                    nc.vector.copy_predicated(fin[i][:, :], mask[:, :], raw[i][:, :]).then_inc(cleaned, 1)
                    dve.wait_ge(cleaned, SUB * t + s + 1 + FREE)
                    nc.vector.tensor_tensor(res[:, s, :], fin[i][:, :], res[:, s, :], ALU.add).then_inc(added, 1)

        @block.scalar
        def _(act):
            with act.Fori(0, NT) as t:
                for s in range(SUB):
                    act.wait_ge(turned, SUB * t + s + 1 + FREE)
                    nc.scalar.copy(aT_hi[:, :, s * P:(s + 1) * P], turn_bank[s][:, :, :]).then_inc(hi_done, 1)

        @block.tensor
        def _(pe):
            pe.sem_inc(turned, FREE)
            with pe.Fori(0, NT) as t:
                pe.wait_ge(ain_ready, 16 * SUB * (t + 1))
                for s in range(SUB):
                    for k in range(DC):
                        last = nc.tensor.transpose(turn_bank[s][:, k, :], ain[:, s, k * P:(k + 1) * P], W["ident"][:, :])
                    last.then_inc(turned, 1)
                for s in range(SUB):
                    pe.wait_ge(lo_done, SUB * t + s + 1)
                    pe.wait_ge(scaled, SUB * t + s - 1 + FREE)
                    cols = slice(s * P, (s + 1) * P)
                    for k in range(DC):
                        for i, at in enumerate((aT_hi, aT_lo)):
                            last = nc.tensor.matmul(mm_bank[s % 2][:, :], at[:, k, cols], W["o_sign"][:, k, :],
                                                    start=(k == 0 and i == 0), stop=(k == DC - 1 and i == 1))
                    last.then_inc(mm_ready, 1)


def build(nc, io):
    ctx = ExitStack()
    with ctx:
        sb = lambda n, s, d: ctx.enter_context(nc.sbuf_tensor(n, s, d))
        sem = lambda n: ctx.enter_context(nc.semaphore(n))
        W = {
            "ident": sb("ident", [P, P], F32),
            "neg_half": sb("neg_half", [P, SUB], F32),
            "up_hi": [sb(f"up_hi{w}", [P, DC, HID], F32R) for w in range(2)],
            "up_lo": [sb(f"up_lo{w}", [P, DC, HID], F32R) for w in range(2)],
            "down_hi": sb("down_hi", [P, HC, D], F32R),
            "down_lo": sb("down_lo", [P, HC, D], F32R),
            "qkv_sign": sb("qkv_sign", [P, DC, D + 2 * KVD], F16),
            "o_sign": sb("o_sign", [P, DC, D], F32R),
            "qk_scale": sb("qk_scale", [P, DC + 1], F32),
            "vo_scale": sb("vo_scale", [P, KVD + D], F32),
        }
        weight_prep(nc, ctx, sem, io, W)
        ffn(nc, sem, "ffn1", W, io["x"], io["x1"])
        projections(nc, sem, W, io["x1"], io["qparts"], io["kparts"], io["vaug"])
        attention(nc, sem, W, io["qparts"], io["kparts"], io["vaug"], io["attn_out"])
        output_projection(nc, sem, W, io["attn_out"], io["x1"], io["x2"])
        ffn(nc, sem, "ffn2", W, io["x2"], io["out"])


_INS = {'x': 'L0_attn_hidden_states', 'wq': 'L0_attn_q_weight', 'qs': 'L0_attn_q_scale', 'wk': 'L0_attn_k_weight',
        'ks': 'L0_attn_k_scale', 'wv': 'L0_attn_v_weight', 'vs': 'L0_attn_v_scale', 'wo': 'L0_attn_o_weight',
        'os': 'L0_attn_o_scale', 'w1': 'L0_ffn_w1', 's1': 'L0_ffn_s1', 'w2': 'L0_ffn_w2', 's2': 'L0_ffn_s2',
        'w3': 'L0_ffn_w3', 's3': 'L0_ffn_s3'}


def kernel(**inputs):
    import numpy as np
    import concourse.bacc as bacc
    from concourse import mybir as mb
    from concourse.bass_utils import run_bass_kernel_spmd as run

    nc = bacc.Bacc("TRN2", target_bir_lowering=False, num_devices=1)
    arrays, io = {}, {}
    for short, name in _INS.items():
        a = np.ascontiguousarray(inputs[name])
        arrays[f"in_{short}"] = a
        io[short] = nc.dram_tensor(f"in_{short}", a.shape, mb.dt.from_np(a.dtype), kind="ExternalInput").ap()
    out = nc.dram_tensor("out", (BATCH, SEQ, D), F32, kind="ExternalOutput").ap()
    io["x"] = io["x"].rearrange("b s d -> (b s) d")
    io["out"] = out.rearrange("b s d -> (b s) d")
    for name, shape, dt in (("x1", (TOK, D), F32), ("x2", (TOK, D), F32),
                            ("qparts", (3, BATCH * D, SEQ), BF16), ("kparts", (3, BATCH * KVD, SEQ), BF16),
                            ("vaug", (NG, SEQ // TT, P, SUB, 2 * HD), F32), ("attn_out", (NG, SEQ, REP * HD), F32)):
        io[name] = nc.dram_tensor(name, shape, dt, kind="Internal").ap()
    io["row_scratch"] = nc.dram_tensor("row_scratch", (KVD + D,), F32, kind="Internal").ap()
    build(nc, io)
    r = run(nc, [arrays], core_ids=[0])
    return r.results[0]["out"]
```

```python
import concourse.bass as bass
from concourse import mybir
from contextlib import ExitStack

F32 = mybir.dt.float32
F32R = mybir.dt.float32r
BF16 = mybir.dt.bfloat16
F16 = mybir.dt.float16
I32 = mybir.dt.int32
ACT = mybir.ActivationFunctionType
ALU = mybir.AluOpType
AX = mybir.AxisListType

P = 128
BATCH, SEQ, D = 2, 1024, 512
TOK = BATCH * SEQ
HID = 1376
GROUP = 64
NH, NKV, HD = 32, 8, 16
REP = NH // NKV
KVD = NKV * HD
DC = D // P
HC = -(-HID // P)
HTAIL = HID - (HC - 1) * P
TT = 512
NT = TOK // TT
SUB = TT // P
LN_EPS = 1e-5
FIN_LIMIT = 1e6
FREE = 16


class Chain:

    def __init__(self, eng, sem, apart=None):
        self.eng, self.sem, self.apart, self.n, self.at = eng, sem, apart, 0, 0

    def enter(self, base):
        self.at, self.n = base, 0

    def add(self, ins):
        self.n += 1
        ins.then_inc(self.sem, 1)

    def wait(self):
        self.eng.wait_ge(self.sem, self.at + self.n)

    def wait_apart(self):
        self.wait()
        self.eng.sem_inc(self.apart, 1)

    def link(self, ins):
        self.add(ins)
        self.wait()


def layernorm_stats(nc, dve, chain, xin, stats, mv, stats_ready):
    for s in range(SUB):
        chain.add(nc.vector.bn_stats(stats[:, s, :], xin[:, s, :]))
    chain.wait_apart()
    for s in range(SUB):
        last = nc.vector.bn_aggr(mv[:, s, :], stats[:, s, :])
    last.then_inc(stats_ready, 1)


def rstd_on_pool(nc, chain, mv, ve, rstd, tmp, neg_half, rstd_ready):
    g = nc.gpsimd
    chain.link(g.tensor_scalar(ve[:, :], mv[:, :, 1], LN_EPS, None, ALU.add))
    chain.link(g.tensor_tensor(rstd[:, :], ve[:, :], neg_half[:, :], ALU.pow))
    chain.link(g.tensor_tensor(tmp[:, :], rstd[:, :], rstd[:, :], ALU.mult))
    chain.add(g.tensor_tensor(tmp[:, :], tmp[:, :], ve[:, :], ALU.mult))
    chain.wait_apart()
    chain.link(g.tensor_scalar(tmp[:, :], tmp[:, :], -0.5, 1.5, ALU.mult, ALU.add))
    g.tensor_tensor(rstd[:, :], rstd[:, :], tmp[:, :], ALU.mult).then_inc(rstd_ready, 1)


RSTD_LINKS = 5


def weight_prep(nc, sem, io, W):
    with ExitStack() as c:
        sb = lambda n, s, d: c.enter_context(nc.sbuf_tensor(n, s, d))
        RING = 4
        bank = [c.enter_context(nc.psum_tensor(f"prep_bank{i}", [P, DC, P], F32)) for i in range(8)]
        down_bank, sign_bank = bank[4:6], bank[6:8]
        ident = W["ident"]
        packed = [sb(f"packed_up{i}", [P, DC, GROUP], I32) for i in range(RING)]
        gscale = [sb(f"gscale_up{i}", [P, DC, 2], F32) for i in range(RING)]
        nib = [sb(f"nib{i}", [P, DC, 2, GROUP], I32) for i in range(RING)]
        PR = HID * 4 // (2 * GROUP)
        packed2 = sb("packed2", [P, PR, GROUP], I32)
        gscale2 = sb("gscale2", [P, PR, 2], F32)
        deq2 = sb("deq2", [P, PR, 2, GROUP], F32)
        wrow = [sb(f"wrow{i}", [P, D], F32) for i in range(2)]
        wsign = [sb(f"wsign{i}", [P, D], F32) for i in range(2)]
        NS = DC + 1 + 1 + DC
        wmean = sb("wmean", [P, NS], F32)
        wrecip = sb("wrecip", [P, NS], F32)
        par_scale = sb("par_scale", [P, NS], F32)
        row_scale = sb("row_scale", [P, NS], F32)

        w_view = [io[n].rearrange("(o k) c -> o (k c)", k=DC) for n in ("w1", "w3")]
        s_view = [io[n].rearrange("(o g) -> o g", g=2 * DC) for n in ("s1", "s3")]
        FULL = HC - 1
        UNITS = 2 * HC
        LOOPS = UNITS // RING - 1

        def rows_of(ch):
            if not isinstance(ch, int):
                return P, bass.ds(ch * P, P)
            n = P if ch < FULL else HTAIL
            return n, slice(ch * P, ch * P + n)

        packed_ready = [sem(f"packed_ready{i}") for i in range(RING)]
        nib_ready, nib_float, deq_ready, deq_turned = (sem(n) for n in ("nib_ready", "nib_float", "deq_ready", "deq_turned"))
        hi_done, lo_done = sem("prep_hi_done"), sem("prep_lo_done")
        packed2_ready, deq2_ready, tr2_ready = sem("packed2_ready"), sem("deq2_ready"), sem("tr2_ready")
        hi2_done, lo2_done = sem("hi2_done"), sem("lo2_done")
        wrow_ready = [sem(f"wrow_ready{i}") for i in range(2)]
        sign_taken, wrecip_ready = sem("sign_taken"), sem("wrecip_ready")
        sign_turned, sign_out = sem("sign_turned"), sem("sign_out")
        par_ready, row_ready, row_stored, row_back = (sem(n) for n in ("par_ready", "row_ready", "row_stored", "row_back"))
        ident_zero, ident_ready, prep_dve = sem("ident_zero"), sem("ident_ready"), sem("prep_dve")

        SIGN = [("wq", j) for j in range(DC)] + [("wk", 0), ("wv", 0)] + [("wo", j) for j in range(DC)]

        block = c.enter_context(nc.Block())

        @block.sync
        def _(sp):
            def load(u, ch, w, slot, before):
                n, rows = rows_of(ch)
                if before is None or before > 0:
                    sp.wait_ge(deq_ready, u - RING + 1 + FREE)
                sp.dma_start(packed[slot][0:n].rearrange("p k c -> p (k c)"), w_view[w][rows, :]).then_inc(packed_ready[slot], 16)
                sp.dma_start(gscale[slot][0:n].rearrange("p k h -> p (k h)"), s_view[w][rows, :]).then_inc(packed_ready[slot], 16)

            for v in range(RING):
                load(v, v // 2, v % 2, v, 0)
            sp.dma_start(packed2.rearrange("p r c -> p (r c)"), io["w2"].rearrange("(p r) c -> p (r c)", p=P)).then_inc(packed2_ready, 16)
            sp.dma_start(gscale2.rearrange("p r h -> p (r h)"), io["s2"].rearrange("(p g) -> p g", p=P)).then_inc(packed2_ready, 16)
            with sp.Fori(0, LOOPS) as i:
                for v in range(RING):
                    load(i * RING + RING + v, i * 2 + 2 + v // 2, v % 2, v, None)
            for u in range(RING * (LOOPS + 1), UNITS):
                load(u, u // 2, u % 2, u % RING, 1)
            with nc.allow_non_contiguous_dma("one scale per row"):
                for name, at, n in (("qs", 0, DC), ("ks", DC, 1), ("vs", DC + 1, 1), ("os", DC + 2, DC)):
                    sp.dma_start(par_scale[:, at:at + n], io[name].rearrange("(c p) -> p c", p=P)).then_inc(par_ready, 16)
            for u in range(NS):
                name, j = SIGN[u]
                if u >= 2:
                    sp.wait_ge(sign_taken, u - 1)
                sp.dma_start(wrow[u % 2][:, :], io[name][j * P:(j + 1) * P, :]).then_inc(wrow_ready[u % 2], 16)
            sp.wait_ge(row_ready, 1)
            with nc.allow_non_contiguous_dma("one scale per row"):
                sp.dma_start(io["row_scratch"].rearrange("(c p) -> p c", p=P), row_scale[:, DC + 1:NS]).then_inc(row_stored, 16)
            sp.wait_ge(row_stored, 16)
            sp.dma_start(W["vo_scale"][:, :], io["row_scratch"][None, :].to_broadcast([P, KVD + D])).then_inc(row_back, 16)
            sp.wait_ge(row_back, 16)

        @block.gpsimd
        def _(pool):
            def scale(u, ch, slot):
                n, _ = rows_of(ch)
                pool.wait_ge(nib_float, u + 1)
                pair = nib[slot][0:n].rearrange("p k h c -> p (k h) c").bitcast(F32)
                nc.gpsimd.tensor_tensor(pair,
                                        gscale[slot][0:n].rearrange("p k h -> p (k h)").unsqueeze(2).to_broadcast([n, 2 * DC, GROUP]),
                                        pair, ALU.mult).then_inc(deq_ready, 1)

            pool.sem_inc(deq_ready, FREE)
            nc.gpsimd.memset(ident[:, :], 0.0).then_inc(ident_zero, 1)
            pool.wait_ge(ident_zero, 1)
            nc.gpsimd.affine_select(out=ident[:, :], in_=ident[:, :], compare_op=ALU.not_equal, fill=1.0, base=0,
                                    pattern=[[-1, P]], channel_multiplier=1).then_inc(ident_ready, 1)
            nc.gpsimd.memset(W["neg_half"][:, :], -0.5)
            with pool.Fori(0, LOOPS) as i:
                for v in range(RING):
                    scale(i * RING + v, i * 2 + v // 2, v)
            for u in range(RING * LOOPS, UNITS):
                scale(u, u // 2, u % RING)

        @block.vector
        def _(dve):
            chain = Chain(dve, prep_dve)

            def unpack(u, ch, slot, uses):
                n, _ = rows_of(ch)
                dve.wait_ge(packed_ready[slot], 32 * uses)
                dve.wait_ge(deq_turned, u - RING + 1 + FREE)
                nc.vector.tensor_scalar(nib[slot][0:n, :, 0, :], packed[slot][0:n], 4, None, ALU.arith_shift_right)
                nc.vector.tensor_scalar(nib[slot][0:n, :, 1, :], packed[slot][0:n], 28, 28, ALU.arith_shift_left,
                                        ALU.arith_shift_right).then_inc(nib_ready, 1)

            def low_part(u, ch, w, slot):
                n, cols = rows_of(ch)
                dve.wait_ge(hi_done, u + 1)
                nc.vector.tensor_tensor(W["up_lo"][w][:, :, cols], bank[slot][:, :, 0:n],
                                        W["up_hi"][w][:, :, cols].bitcast(F32), ALU.subtract).then_inc(lo_done, 1)

            AHEAD = 3
            dve.sem_inc(lo_done, FREE)
            for u in range(AHEAD):
                unpack(u, u // 2, u, 1)
            with dve.Fori(0, LOOPS) as i:
                for v in range(RING):
                    a = v + AHEAD
                    unpack(i * RING + a, i * 2 + a // 2, a % RING, i + a // RING + 1)
                    low_part(i * RING + v, i * 2 + v // 2, v % 2, v)
            for u in range(RING * LOOPS, UNITS):
                a = u + AHEAD
                if a < UNITS:
                    unpack(a, a // 2, a % RING, a // RING + 1)
                low_part(u, u // 2, u % 2, u % RING)

            dve.wait_ge(packed2_ready, 32)
            deq2_int = deq2.bitcast(I32)
            chain.add(nc.vector.tensor_scalar(deq2_int[:, :, 0, :], packed2[:, :, :], 4, None, ALU.arith_shift_right))
            chain.link(nc.vector.tensor_scalar(deq2_int[:, :, 1, :], packed2[:, :, :], 28, 28, ALU.arith_shift_left,
                                               ALU.arith_shift_right))
            nc.vector.tensor_tensor(deq2[:, :, :, :], deq2_int[:, :, :, :],
                                    gscale2[:, :, :].unsqueeze(3).to_broadcast([P, PR, 2, GROUP]),
                                    ALU.mult).then_inc(deq2_ready, 1)

            def low_part2(u):
                n, _ = rows_of(u)
                dve.wait_ge(hi2_done, u + 1)
                nc.vector.tensor_tensor(W["down_lo"][0:n, u, :].rearrange("h (p j) -> h j p", j=4), down_bank[u % 2][0:n],
                                        W["down_hi"][0:n, u, :].bitcast(F32).rearrange("h (p j) -> h j p", j=4),
                                        ALU.subtract).then_inc(lo2_done, 1)

            for u in range(NS):
                dve.wait_ge(wrow_ready[u % 2], (u // 2 + 1) * 16)
                chain.link(nc.vector.tensor_reduce(wmean[:, u:u + 1], wrow[u % 2][:, :], AX.X, ALU.add,
                                                   apply_absolute_value=True))
                chain.link(nc.vector.tensor_scalar(wmean[:, u:u + 1], wmean[:, u:u + 1], 1.0 / D, 1e-8, ALU.mult, ALU.max))
                nc.vector.reciprocal(wrecip[:, u:u + 1], wmean[:, u:u + 1]).then_inc(wrecip_ready, 1)
                low_part2(u)
            for u in range(NS, HC):
                low_part2(u)
            dve.wait_ge(par_ready, 64)
            chain.link(nc.vector.tensor_tensor(row_scale[:, :], wmean[:, :], par_scale[:, :], ALU.mult))
            nc.vector.tensor_copy(W["qk_scale"][:, :], row_scale[:, 0:DC + 1]).then_inc(row_ready, 1)

        @block.scalar
        def _(act):
            def to_float(u, ch, slot):
                n, _ = rows_of(ch)
                act.wait_ge(nib_ready, u + 1)
                values = nib[slot][0:n].rearrange("p k h c -> p (k h c)")
                nc.scalar.copy(values.bitcast(F32), values).then_inc(nib_float, 1)

            def high_part(u, ch, w, slot):
                n, cols = rows_of(ch)
                act.wait_ge(deq_turned, u + 1 + FREE)
                nc.scalar.copy(W["up_hi"][w][:, :, cols], bank[slot][:, :, 0:n]).then_inc(hi_done, 1)

            def sign_copy(u):
                act.wait_ge(sign_turned, u + 1)
                name, j = SIGN[u]
                if name == "wo":
                    out = W["o_sign"][:, :, j * P:(j + 1) * P]
                else:
                    at = {"wq": 0, "wk": D, "wv": D + KVD}[name] + j * P
                    out = W["qkv_sign"][:, :, at:at + P]
                nc.scalar.copy(out, sign_bank[u % 2][:, :, :]).then_inc(sign_out, 1)

            AHEAD = 2
            for u in range(AHEAD):
                to_float(u, u // 2, u)
            with act.Fori(0, LOOPS) as i:
                for v in range(RING):
                    a = v + AHEAD
                    to_float(i * RING + a, i * 2 + a // 2, a % RING)
                    high_part(i * RING + v, i * 2 + v // 2, v % 2, v)
            for u in range(RING * LOOPS, UNITS):
                a = u + AHEAD
                if a < UNITS:
                    to_float(a, a // 2, a % RING)
                high_part(u, u // 2, u % 2, u % RING)
            for u in range(HC):
                n, _ = rows_of(u)
                if u < NS:
                    act.wait_ge(wrecip_ready, u + 1)
                    if u >= 2:
                        act.wait_ge(sign_turned, u - 1)
                    nc.scalar.activation(wsign[u % 2][:, :], wrow[u % 2][:, :], ACT.Sign,
                                         scale=wrecip[:, u:u + 1]).then_inc(sign_taken, 1)
                act.wait_ge(tr2_ready, u + 1)
                nc.scalar.copy(W["down_hi"][0:n, u, :].rearrange("h (p j) -> h j p", j=4), down_bank[u % 2][0:n]).then_inc(hi2_done, 1)
                if u >= 1:
                    sign_copy(u - 1)

        @block.tensor
        def _(pe):
            pe.sem_inc(deq_turned, FREE)
            pe.wait_ge(ident_ready, 1)

            def turn(u, ch, slot):
                n, _ = rows_of(ch)
                pe.wait_ge(deq_ready, u + 1 + FREE)
                pe.wait_ge(lo_done, u - RING + 1 + FREE)
                for k in range(DC):
                    last = nc.tensor.transpose(bank[slot][:, k, 0:n], nib[slot][0:n, k].rearrange("p h c -> p (h c)").bitcast(F32),
                                               ident[0:n, 0:n])
                last.then_inc(deq_turned, 1)

            with pe.Fori(0, LOOPS) as i:
                for v in range(RING):
                    turn(i * RING + v, i * 2 + v // 2, v)
            for u in range(RING * LOOPS, UNITS):
                turn(u, u // 2, u % RING)
            pe.wait_ge(deq2_ready, 1)
            d2 = deq2.rearrange("p r h c -> p (r h c)").rearrange("p (j n) -> p j n", j=4)
            for u in range(HC):
                n, _ = rows_of(u)
                if u >= 2:
                    pe.wait_ge(lo2_done, u - 1)
                for j in range(4):
                    last = nc.tensor.transpose(down_bank[u % 2][0:n, j, :], d2[:, j, u * P:u * P + n], ident[:, :])
                last.then_inc(tr2_ready, 1)
                if u < NS:
                    if u >= 2:
                        pe.wait_ge(sign_out, u - 1)
                    pe.wait_ge(sign_taken, u + 1)
                    for k in range(DC):
                        last = nc.tensor.transpose(sign_bank[u % 2][:, k, :], wsign[u % 2][:, k * P:(k + 1) * P], ident[:, :])
                    last.then_inc(sign_turned, 1)


def ffn(nc, sem, tag, W, src, dst):
    with ExitStack() as c:
        sb = lambda n, s, d: c.enter_context(nc.sbuf_tensor(f"{tag}_{n}", s, d))
        S = lambda n: sem(f"{tag}_{n}")
        up_bank = [[c.enter_context(nc.psum_tensor(f"{tag}_up{i}{w}", [P, TT], F32)) for w in range(2)] for i in range(2)]
        y_bank = [c.enter_context(nc.psum_tensor(f"{tag}_y{s}", [P, D], F32)) for s in range(SUB)]
        turn_bank = [up_bank[1][0], up_bank[1][1], up_bank[0][0], up_bank[1][0]]
        xin = sb("xin", [P, SUB, D], F32)
        xres = sb("xres", [P, SUB, D], F32)
        xT_hi, xT_lo = sb("xT_hi", [P, DC, TT], F32R), sb("xT_lo", [P, DC, TT], F32R)
        sil, h = sb("sil", [P, TT], F32), sb("h", [P, TT], F32)
        h_hi = [sb(f"h_hi{i}", [P, TT], F32R) for i in range(2)]
        h_lo = [sb(f"h_lo{i}", [P, TT], F32R) for i in range(2)]
        stats, mv = sb("stats", [P, SUB, 6], F32), sb("mv", [P, SUB, 2], F32)
        ve, rstd, tmp = sb("ve", [P, SUB], F32), sb("rstd", [P, SUB], F32), sb("tmp", [P, SUB], F32)

        xin_ready, xres_ready, out_stored = S("xin_ready"), S("xres_ready"), S("out_stored")
        stats_ready, rstd_ready, xn_ready = S("stats_ready"), S("rstd_ready"), S("xn_ready")
        turned, xT_hi_done, xT_lo_done = S("turned"), S("xT_hi_done"), S("xT_lo_done")
        up_ready, a_read, b_read, hi_done, lo_done = (S(n) for n in ("up_ready", "a_read", "b_read", "h_hi_done", "h_lo_done"))
        down_done, y_done = S("down_done"), S("y_done")
        dve_chain, pool_chain = S("dve_chain"), S("pool_chain")
        rows = lambda m: P if m < HC - 1 else HTAIL
        tile = lambda ap, t: (ap[bass.ds(t * TT, TT), :] if not isinstance(t, int) else ap[t * TT:(t + 1) * TT, :]
                              ).rearrange("(s p) d -> p s d", p=P)

        block = c.enter_context(nc.Block())

        @block.sync
        def _(sp):
            def load_in(t):
                sp.wait_ge(turned, SUB * t)
                sp.dma_start(xin[:, :, :], tile(src, t)).then_inc(xin_ready, 16)

            def residual(t):
                sp.wait_ge(out_stored, 16 * t + FREE)
                sp.dma_start(xres[:, :, :], tile(src, t)).then_inc(xres_ready, 16)

            def store(t):
                sp.wait_ge(y_done, SUB * (t + 1) + FREE)
                sp.dma_start(tile(dst, t), xres[:, :, :]).then_inc(out_stored, 16)

            sp.sem_inc(out_stored, FREE)
            load_in(0)
            with sp.Fori(0, NT - 1) as t:
                residual(t)
                load_in(t + 1)
                store(t)
            residual(NT - 1)
            store(NT - 1)
            sp.wait_ge(out_stored, 16 * NT + FREE)

        @block.gpsimd
        def _(pool):
            chain = Chain(pool, pool_chain, S("pool_apart"))
            with pool.Fori(0, NT) as t:
                chain.enter(t * RSTD_LINKS)
                pool.wait_ge(stats_ready, t + 1)
                pool.wait_ge(xn_ready, t + FREE)
                pool.sem_inc(chain.apart, 1)
                rstd_on_pool(nc, chain, mv, ve, rstd, tmp, W["neg_half"], rstd_ready)

        @block.vector
        def _(dve):
            chain = Chain(dve, dve_chain, S("dve_apart"))
            PER_TILE = SUB

            def stats_of(t):
                dve.wait_ge(xin_ready, 16 * (t + 1))
                dve.wait_ge(rstd_ready, t)
                chain.enter(t * PER_TILE)
                layernorm_stats(nc, dve, chain, xin, stats, mv, stats_ready)

            def normalise(t):
                dve.wait_ge(rstd_ready, t + 1)
                for s in range(SUB):
                    last = nc.vector.tensor_scalar(xin[:, s, :], xin[:, s, :], mv[:, s, 0:1], rstd[:, s:s + 1],
                                                   ALU.subtract, ALU.mult)
                last.then_inc(xn_ready, 1)

            def xT_low(t):
                for s in range(SUB):
                    dve.wait_ge(xT_hi_done, SUB * t + s + 1)
                    nc.vector.tensor_tensor(xT_lo[:, :, s * P:(s + 1) * P],
                                            turn_bank[s][:, :].rearrange("p (k n) -> p k n", k=DC),
                                            xT_hi[:, :, s * P:(s + 1) * P].bitcast(F32), ALU.subtract).then_inc(xT_lo_done, 1)

            def main(t, has_next):
                for m in range(HC):
                    n, c0 = rows(m), t * HC + m
                    dve.wait_ge(a_read, c0 + 1)
                    dve.wait_ge(hi_done, c0 + FREE)
                    dve.wait_ge(lo_done, c0 + FREE)
                    nc.vector.tensor_tensor(h[0:n], sil[0:n], up_bank[m % 2][1][0:n, :], ALU.mult).then_inc(b_read, 1)
                    dve.wait_ge(hi_done, c0 + 1 + FREE)
                    nc.vector.tensor_tensor(h_lo[m % 2][0:n], h[0:n], h_hi[m % 2][0:n].bitcast(F32),
                                            ALU.subtract).then_inc(lo_done, 1)
                    if m == 2 and has_next:
                        stats_of(t + 1)
                    if m == 4 and has_next:
                        normalise(t + 1)
                if has_next:
                    xT_low(t + 1)
                dve.wait_ge(xres_ready, 16 * (t + 1))
                dve.wait_ge(down_done, HC * (t + 1) + FREE)
                for s in range(SUB):
                    nc.vector.scalar_tensor_tensor(xres[:, s, :], y_bank[s][:, :], 0.5, xres[:, s, :],
                                                   ALU.mult, ALU.add).then_inc(y_done, 1)

            for signal in (b_read, lo_done, y_done, xn_ready):
                dve.sem_inc(signal, FREE)
            stats_of(0)
            normalise(0)
            xT_low(0)
            with dve.Fori(0, NT - 1) as t:
                main(t, True)
            main(NT - 1, False)

        @block.scalar
        def _(act):
            def xT_high(t):
                for s in range(SUB):
                    act.wait_ge(turned, SUB * t + s + 1)
                    nc.scalar.copy(xT_hi[:, :, s * P:(s + 1) * P],
                                   turn_bank[s][:, :].rearrange("p (k n) -> p k n", k=DC)).then_inc(xT_hi_done, 1)

            def main(t, has_next):
                for m in range(HC):
                    n, c0 = rows(m), t * HC + m
                    act.wait_ge(up_ready, c0 + 1)
                    act.wait_ge(b_read, c0 + FREE)
                    nc.scalar.activation(sil[0:n], up_bank[m % 2][0][0:n, :], ACT.Silu).then_inc(a_read, 1)
                    act.wait_ge(b_read, c0 + 1 + FREE)
                    act.wait_ge(down_done, t * HC + max(m - 1, 0) + FREE)
                    nc.scalar.copy(h_hi[m % 2][0:n], h[0:n]).then_inc(hi_done, 1)
                if has_next:
                    xT_high(t + 1)

            act.sem_inc(hi_done, FREE)
            xT_high(0)
            with act.Fori(0, NT - 1) as t:
                main(t, True)
            main(NT - 1, False)

        @block.tensor
        def _(pe):
            def turn(t, s):
                for k in range(DC):
                    last = nc.tensor.transpose(turn_bank[s][:, k * P:(k + 1) * P], xin[:, s, k * P:(k + 1) * P], W["ident"][:, :])
                last.then_inc(turned, 1)

            def up(t, m):
                n, c0 = rows(m), t * HC + m
                if m >= 2:
                    pe.wait_ge(a_read, c0 - 1)
                    pe.wait_ge(b_read, c0 - 1 + FREE)
                cols = slice(m * P, m * P + n)
                for w in range(2):
                    for k in range(DC):
                        parts = ((W["up_hi"], xT_hi), (W["up_hi"], xT_lo), (W["up_lo"], xT_hi))
                        for i, (wt, xt) in enumerate(parts):
                            last = nc.tensor.matmul(up_bank[m % 2][w][0:n, :], wt[w][:, k, cols], xt[:, k, :],
                                                    start=(k == 0 and i == 0), stop=(k == DC - 1 and i == 2))
                last.then_inc(up_ready, 1)

            def down(t, m):
                n, c0 = rows(m), t * HC + m
                if m == 0:
                    pe.wait_ge(y_done, SUB * t + FREE)
                pe.wait_ge(lo_done, c0 + 1 + FREE)
                for s in range(SUB):
                    cols = slice(s * P, (s + 1) * P)
                    parts = ((h_hi, W["down_hi"]), (h_lo, W["down_hi"]), (h_hi, W["down_lo"]))
                    for i, (ht, wt) in enumerate(parts):
                        last = nc.tensor.matmul(y_bank[s][:, :], ht[m % 2][0:n, cols], wt[0:n, m, :],
                                                start=(m == 0 and i == 0), stop=(m == HC - 1 and i == 2))
                last.then_inc(down_done, 1)

            def main(t, has_next):
                pe.wait_ge(xT_lo_done, SUB * (t + 1))
                up(t, 0)
                for m in range(1, HC):
                    up(t, m)
                    if m < HC - 1:
                        down(t, m - 1)
                if has_next:
                    pe.wait_ge(xn_ready, t + 2 + FREE)
                    pe.wait_ge(a_read, t * HC + HC - 1)
                    pe.wait_ge(b_read, t * HC + HC - 1 + FREE)
                    turn(t + 1, 0)
                    turn(t + 1, 1)
                down(t, HC - 2)
                if has_next:
                    pe.wait_ge(a_read, t * HC + HC)
                    pe.wait_ge(b_read, t * HC + HC + FREE)
                    turn(t + 1, 2)
                    pe.wait_ge(xT_lo_done, SUB * (t + 1) + 1)
                    turn(t + 1, 3)
                down(t, HC - 1)

            pe.sem_inc(down_done, FREE)
            pe.wait_ge(xn_ready, 1 + FREE)
            for s in range(SUB):
                if s == 3:
                    pe.wait_ge(xT_lo_done, 1)
                turn(0, s)
            with pe.Fori(0, NT - 1) as t:
                main(t, True)
            main(NT - 1, False)


def split_by_sign(nc, raw, pos, neg, mask, signs_ready, mask_ready):
    nc.vector.tensor_scalar(pos, raw, 0.0, FIN_LIMIT, ALU.max, ALU.min)
    nc.vector.tensor_scalar(neg, raw, 0.0, -FIN_LIMIT, ALU.min, ALU.max).then_inc(signs_ready, 1)
    nc.vector.tensor_scalar(mask, raw, 0.0, 0.0, ALU.mult, ALU.is_equal).then_inc(mask_ready, 1)


def projections(nc, sem, W, src, qparts, kparts, vaug):
    with ExitStack() as c:
        sb = lambda n, s, d: c.enter_context(nc.sbuf_tensor(f"qkv_{n}", s, d))
        S = lambda n: sem(f"qkv_{n}")
        turn_bank = [c.enter_context(nc.psum_tensor(f"qkv_turn{s}", [P, DC, P], F32)) for s in range(SUB)]
        mm_bank = [c.enter_context(nc.psum_tensor(f"qkv_mm{i}", [P, TT], F32)) for i in range(2)]
        xin = sb("xin", [P, SUB, D], F32)
        xT_hi, xT_lo = sb("xT_hi", [P, DC, TT], F16), sb("xT_lo", [P, DC, TT], F16)
        raw = [sb(f"raw{i}", [P, TT], F32) for i in range(3)]
        fin = [sb(f"fin{i}", [P, TT], F32) for i in range(3)]
        neg = [sb(f"neg{i}", [P, TT], F32) for i in range(2)]
        rest = [sb(f"rest{i}", [P, TT], F32) for i in range(2)]
        mask = [sb(f"mask{i}", [P, TT], I32) for i in range(2)]
        parts = [sb(f"parts{i}", [P, 3, TT], BF16) for i in range(2)]
        vt = sb("vt", [P, NKV, SUB, 2 * HD], F32)
        stats, mv = sb("stats", [P, SUB, 6], F32), sb("mv", [P, SUB, 2], F32)
        ve, rstd, tmp = sb("ve", [P, SUB], F32), sb("rstd", [P, SUB], F32), sb("tmp", [P, SUB], F32)

        xin_ready, stats_ready, rstd_ready, xn_ready = (S(n) for n in ("xin_ready", "stats_ready", "rstd_ready", "xn_ready"))
        turned, xT_hi_done, xT_lo_done = S("turned"), S("xT_hi_done"), S("xT_lo_done")
        mm_ready, scaled, v_scaled = S("mm_ready"), S("scaled"), S("v_scaled")
        signs_ready, mask_ready, pool_cleaned, cleaned = (S(n) for n in ("signs_ready", "mask_ready", "pool_cleaned", "cleaned"))
        part1_done, rest_done, part2_done, part3_done = (S(n) for n in ("part1_done", "rest_done", "part2_done", "part3_done"))
        v_placed, v_stored, ones_set = S("v_placed"), S("v_stored"), S("ones_set")
        parts_stored = [S(f"parts_stored{i}") for i in range(2)]
        dve_chain, pool_chain = S("dve_chain"), S("pool_chain")
        NQK = DC + 1
        V = NQK
        UNITS = NQK + 1
        stores_before = lambda t, u: ((NQK + 1) // 2 if u % 2 == 0 else NQK // 2) * t + u // 2
        rowsof = lambda t: bass.ds(t * TT, TT) if not isinstance(t, int) else slice(t * TT, (t + 1) * TT)

        block = c.enter_context(nc.Block())

        @block.sync
        def _(sp):
            for signal in (parts_stored[0], parts_stored[1], v_stored):
                sp.sem_inc(signal, FREE)
            sp.dma_start(xin[:, :, :], src[0:TT, :].rearrange("(s p) d -> p s d", p=P)).then_inc(xin_ready, 16)

            def main(t, has_next):
                if has_next:
                    sp.wait_ge(turned, SUB * (t + 1))
                    sp.dma_start(xin[:, :, :], src[rowsof(t + 1), :].rearrange("(s p) d -> p s d", p=P)).then_inc(xin_ready, 16)
                b, half = t // 2, t % 2
                cols = bass.ds(half * TT, TT)
                for u in range(NQK):
                    sp.wait_ge(part3_done, NQK * t + u + 1 + FREE)
                    dst, row = (qparts, b * D + u * P) if u < DC else (kparts, b * KVD)
                    sp.dma_start(dst[:, bass.ds(row, P), cols].rearrange("a r t -> r a t"),
                                 parts[u % 2][:, :, :]).then_inc(parts_stored[u % 2], 16)
                sp.wait_ge(v_placed, t + 1 + FREE)
                dst = vaug.rearrange("(b k) h p s c -> b h p k (s c)", b=BATCH)
                sp.dma_start(dst[bass.ds(b, 1), bass.ds(half, 1)].rearrange("a o p k n -> (a o p) k n"),
                             vt.rearrange("p k s c -> p k (s c)")).then_inc(v_stored, 16)

            with sp.Fori(0, NT - 1) as t:
                main(t, True)
            main(NT - 1, False)
            sp.wait_ge(parts_stored[0], 16 * stores_before(NT, 0) + FREE)
            sp.wait_ge(parts_stored[1], 16 * stores_before(NT, 1) + FREE)
            sp.wait_ge(v_stored, 16 * NT + FREE)

        def wait_scaled(eng, t, u):
            if u < V:
                eng.wait_ge(scaled, NQK * t + u + 1 + FREE)
            else:
                eng.wait_ge(v_scaled, t + 1 + FREE)

        STEPS = UNITS + 2

        @block.gpsimd
        def _(pool):
            chain = Chain(pool, pool_chain, S("pool_apart"))
            nc.gpsimd.memset(vt[:, :, :, :], 1.0).then_inc(ones_set, 1)

            def rstd_of(t):
                chain.enter(t * RSTD_LINKS)
                pool.wait_ge(stats_ready, t + 1)
                pool.wait_ge(xn_ready, t + FREE)
                pool.sem_inc(chain.apart, 1)
                rstd_on_pool(nc, chain, mv, ve, rstd, tmp, W["neg_half"], rstd_ready)

            def main(t, has_next):
                for step in range(STEPS):
                    u = step
                    if u < UNITS:
                        pool.wait_ge(signs_ready, UNITS * t + u + 1)
                        nc.gpsimd.tensor_tensor(fin[u % 3][:, :], fin[u % 3][:, :], neg[u % 2][:, :], ALU.add).then_inc(pool_cleaned, 1)
                    u = step - 3
                    if 0 <= u < NQK:
                        pool.wait_ge(part2_done, NQK * t + u + 1)
                        nc.gpsimd.tensor_tensor(parts[u % 2][:, 2, :], rest[u % 2][:, :], parts[u % 2][:, 1, :],
                                                ALU.subtract).then_inc(part3_done, 1)
                    if step == 2 and has_next:
                        rstd_of(t + 1)

            for signal in (pool_cleaned, rstd_ready, part3_done):
                pool.sem_inc(signal, FREE)
            rstd_of(0)
            with pool.Fori(0, NT - 1) as t:
                main(t, True)
            main(NT - 1, False)

        @block.vector
        def _(dve):
            chain = Chain(dve, dve_chain, S("dve_apart"))

            def stats_of(t):
                chain.enter(t * SUB)
                dve.wait_ge(xin_ready, 16 * (t + 1))
                dve.wait_ge(rstd_ready, t + FREE)
                layernorm_stats(nc, dve, chain, xin, stats, mv, stats_ready)

            def normalise(t):
                dve.wait_ge(rstd_ready, t + 1 + FREE)
                for s in range(SUB):
                    last = nc.vector.tensor_scalar(xin[:, s, :], xin[:, s, :], mv[:, s, 0:1], rstd[:, s:s + 1],
                                                   ALU.subtract, ALU.mult)
                last.then_inc(xn_ready, 1)

            def xT_low(t):
                for s in range(SUB):
                    dve.wait_ge(xT_hi_done, SUB * t + s + 1)
                    nc.vector.tensor_tensor(xT_lo[:, :, s * P:(s + 1) * P], turn_bank[s][:, :, :],
                                            xT_hi[:, :, s * P:(s + 1) * P], ALU.subtract).then_inc(xT_lo_done, 1)

            def signs(t, u):
                if u == V:
                    dve.wait_ge(mm_ready, UNITS * t + u + 1)
                    dve.wait_ge(cleaned, UNITS * t + u - 2 + FREE)
                    nc.vector.tensor_tensor(raw[u % 3][:, :].rearrange("p (s c) -> p s c", s=SUB),
                                            mm_bank[u % 2][:, :].rearrange("p (s c) -> p s c", s=SUB),
                                            W["vo_scale"][:, 0:KVD].unsqueeze(1).to_broadcast([P, SUB, KVD]),
                                            ALU.mult).then_inc(v_scaled, 1)
                wait_scaled(dve, t, u)
                if u == 2:
                    dve.wait_ge(v_placed, t + FREE)
                else:
                    dve.wait_ge(rest_done, NQK * t + (u - 1 if u < 2 else u - 2) + FREE)
                dve.wait_ge(cleaned, UNITS * t + u - 1 + FREE)
                split_by_sign(nc, raw[u % 3][:, :], fin[u % 3][:, :], neg[u % 2][:, :], mask[u % 2][:, :], signs_ready, mask_ready)

            def keep_finite(t, u):
                dve.wait_ge(mask_ready, UNITS * t + u + 1)
                dve.wait_ge(pool_cleaned, UNITS * t + u + 1 + FREE)
                dve.sem_inc(chain.apart, 1)
                nc.vector.copy_predicated(fin[u % 3][:, :], mask[u % 2][:, :], raw[u % 3][:, :]).then_inc(cleaned, 1)

            def take_rest(t, u):
                dve.wait_ge(part1_done, NQK * t + u + 1)
                dve.wait_ge(part3_done, NQK * t + u - 1 + FREE)
                nc.vector.scalar_tensor_tensor(rest[u % 2][:, :], fin[u % 3][:, :], HD ** -0.5 if u < DC else 1.0,
                                               parts[u % 2][:, 0, :], ALU.mult, ALU.subtract).then_inc(rest_done, 1)

            def main(t, has_next):
                for step in range(STEPS):
                    if step < UNITS:
                        signs(t, step)
                    if 0 <= step - 2 < NQK:
                        take_rest(t, step - 2)
                    if 0 <= step - 1 < UNITS:
                        keep_finite(t, step - 1)
                    if step == 1 and has_next:
                        stats_of(t + 1)
                    if step == 3 and has_next:
                        normalise(t + 1)
                if has_next:
                    xT_low(t + 1)

            for signal in (v_scaled, cleaned, rest_done, xn_ready):
                dve.sem_inc(signal, FREE)
            stats_of(0)
            normalise(0)
            xT_low(0)
            with dve.Fori(0, NT - 1) as t:
                main(t, True)
            main(NT - 1, False)

        @block.scalar
        def _(act):
            def xT_high(t):
                for s in range(SUB):
                    act.wait_ge(turned, SUB * t + s + 1)
                    nc.scalar.copy(xT_hi[:, :, s * P:(s + 1) * P], turn_bank[s][:, :, :]).then_inc(xT_hi_done, 1)

            def scale(t, u):
                act.wait_ge(mm_ready, UNITS * t + u + 1)
                act.wait_ge(cleaned, UNITS * t + u - 2 + FREE)
                nc.scalar.activation(raw[u % 3][:, :], mm_bank[u % 2][:, :], ACT.Copy,
                                     scale=W["qk_scale"][:, u:u + 1]).then_inc(scaled, 1)

            def main(t, has_next):
                scale(t, 0)
                for step in range(STEPS):
                    if step + 1 < NQK:
                        scale(t, step + 1)
                    u = step - 2
                    if 0 <= u < NQK:
                        act.wait_ge(rest_done, NQK * t + u + 1 + FREE)
                        nc.scalar.copy(parts[u % 2][:, 1, :], rest[u % 2][:, :]).then_inc(part2_done, 1)
                    u = step - 1
                    if 0 <= u < NQK:
                        act.wait_ge(cleaned, UNITS * t + u + 1 + FREE)
                        act.wait_ge(parts_stored[u % 2], 16 * stores_before(t, u) + FREE)
                        nc.scalar.mul(parts[u % 2][:, 0, :], fin[u % 3][:, :], HD ** -0.5 if u < DC else 1.0).then_inc(part1_done, 1)
                act.wait_ge(cleaned, UNITS * (t + 1) + FREE)
                act.wait_ge(v_stored, 16 * t + FREE)
                nc.scalar.copy(vt[:, :, :, 0:HD], fin[V % 3][:, :].rearrange("p (s k c) -> p k s c", s=SUB, k=NKV)
                               ).then_inc(v_placed, 1)
                if has_next:
                    xT_high(t + 1)

            for signal in (scaled, v_placed):
                act.sem_inc(signal, FREE)
            act.wait_ge(ones_set, 1)
            xT_high(0)
            with act.Fori(0, NT - 1) as t:
                main(t, True)
            main(NT - 1, False)

        @block.tensor
        def _(pe):
            def turn(t, s):
                for k in range(DC):
                    last = nc.tensor.transpose(turn_bank[s][:, k, :], xin[:, s, k * P:(k + 1) * P], W["ident"][:, :])
                last.then_inc(turned, 1)

            def main(t, has_next):
                pe.wait_ge(xT_lo_done, SUB * (t + 1))
                for u in range(UNITS):
                    if u == 1:
                        pe.wait_ge(v_scaled, t + FREE)
                    else:
                        pe.wait_ge(scaled, NQK * t + max(u - 1, 0) + FREE)
                    if u < V:
                        for k in range(DC):
                            for i, xt in enumerate((xT_hi, xT_lo)):
                                last = nc.tensor.matmul(mm_bank[u % 2][:, :], W["qkv_sign"][:, k, u * P:(u + 1) * P], xt[:, k, :],
                                                        start=(k == 0 and i == 0), stop=(k == DC - 1 and i == 1))
                    else:
                        for s in range(SUB):
                            cols = slice(s * P, (s + 1) * P)
                            for k in range(DC):
                                for i, xt in enumerate((xT_hi, xT_lo)):
                                    last = nc.tensor.matmul(mm_bank[u % 2][:, cols], xt[:, k, cols], W["qkv_sign"][:, k, D + KVD:],
                                                            start=(k == 0 and i == 0), stop=(k == DC - 1 and i == 1))
                    last.then_inc(mm_ready, 1)
                if has_next:
                    pe.wait_ge(xn_ready, t + 2 + FREE)
                    for s in range(SUB):
                        turn(t + 1, s)

            pe.wait_ge(xn_ready, 1 + FREE)
            for s in range(SUB):
                turn(0, s)
            with pe.Fori(0, NT - 1) as t:
                main(t, True)
            main(NT - 1, False)


PARTS_OF_BLOCK = ((0, 0), (0, 1), (1, 0), (1, 1), (0, 2), (2, 0))
NBLK = len(PARTS_OF_BLOCK)
SROWS = NBLK * HD
MAXROW = SROWS
QT = SEQ // P
NG = BATCH * NKV


def attention(nc, sem, W, qparts, kparts, vaug, attn_out):
    with ExitStack() as c:
        sb = lambda n, s, d: c.enter_context(nc.sbuf_tensor(f"at_{n}", s, d))
        pb = lambda n, s: c.enter_context(nc.psum_tensor(f"at_{n}", s, F32))
        S = lambda n: sem(f"at_{n}")
        HALVES = SEQ // TT
        NQ = HALVES * QT
        NS = NQ * REP
        NM = REP * QT
        HM = NM // HALVES
        HEAD = 3
        COPY_AT = QT
        TURN_AT = (COPY_AT + 1, 1)
        FOLD_AT = (HEAD + HM // 2 + 1, HEAD + 1)

        max_bank = [pb(f"max{i}", [P, SEQ]) for i in range(2)]
        s_bank = [pb(f"s{i}", [P, TT]) for i in range(2)]
        o_bank, turn_bank = pb("o", [P, TT]), pb("turn", [P, SUB, P])
        qst = [sb(f"qst{i}", [P, HALVES, REP, TT], BF16) for i in range(2)]
        kst = [sb(f"kst{i}", [P, SEQ], BF16) for i in range(2)]
        vst = [sb(f"vst{i}", [P, QT, 2 * HD], F32) for i in range(2)]
        prob = [sb(f"prob{i}", [P, REP, TT], F32) for i in range(2)]
        negmax = [sb(f"negmax{h}", [P, HM], F32) for h in range(HALVES)]
        mrest = sb("mrest", [HM, P], F32)
        mparts = [sb(f"mparts{h}", [HM, 3, P], BF16) for h in range(HALVES)]
        osb = sb("osb", [P, TT], F32)
        recip = sb("recip", [P, SUB, REP], F32)
        out = sb("out", [P, QT, REP, HD], F32)

        q_ready = [[S(f"q_ready{i}{h}") for h in range(2)] for i in range(2)]
        k_ready, v_ready = [S(f"k_ready{i}") for i in range(2)], [S(f"v_ready{i}") for i in range(2)]
        rows_set = S("rows_set")
        max_ready, max_read, max_turned, mparts_done = (S(n) for n in ("max_ready", "max_read", "max_turned", "mparts_done"))
        maxrow_ready = [S(f"maxrow_ready{h}") for h in range(HALVES)]
        s_ready, exp_done, pv_done = S("s_ready"), S("exp_done"), S("pv_done")
        o_copied, o_turned, o_normed, out_stored = (S(n) for n in ("o_copied", "o_turned", "o_normed", "out_stored"))
        dve_chain = S("dve_chain")
        rowsof = lambda g, n: bass.ds(g * n, n) if not isinstance(g, int) else slice(g * n, (g + 1) * n)

        block = c.enter_context(nc.Block())

        @block.sync
        def _(sp):
            def load_q(g, i, half):
                for b, (part, _) in enumerate(PARTS_OF_BLOCK):
                    sp.dma_start(qst[i][b * HD:(b + 1) * HD, half, :, :],
                                 qparts[part, rowsof(g, REP * HD), half * TT:(half + 1) * TT].rearrange("(h d) t -> d h t", h=REP)
                                 ).then_inc(q_ready[i][half], 16)

            def load_k(g, i):
                for b, (_, part) in enumerate(PARTS_OF_BLOCK):
                    sp.dma_start(kst[i][b * HD:(b + 1) * HD, :], kparts[part, rowsof(g, HD), :]).then_inc(k_ready[i], 16)

            def load_v(g, i):
                sp.dma_start(vst[i][:, :, :].rearrange("p (h s) c -> p h (s c)", h=HALVES),
                             vaug[rowsof(g, 1)].rearrange("o h p s c -> p (o h) (s c)")).then_inc(v_ready[i], 16)

            def max_rows(g, i, half):
                sp.wait_ge(mparts_done, HALVES * g + half + 1 + FREE)
                for part in range(3):
                    sp.dma_start(qst[i][MAXROW + part:MAXROW + part + 1, half, :, :].rearrange(
                        "o h (t p) -> o (h t) p", p=P), mparts[half][:, part, :]).then_inc(maxrow_ready[half], 16)

            def store_out(g):
                sp.wait_ge(o_normed, HALVES * (g + 1) + FREE)
                sp.dma_start(attn_out[rowsof(g, 1)].rearrange("o (t p) c -> (o p) t c", p=P),
                             out.rearrange("p t h d -> p t (h d)")).then_inc(out_stored, 16)

            def step(g, i, has_load):
                max_rows(g, i, 1)
                if has_load:
                    sp.wait_ge(s_ready, NS * g + NS // 2)
                    load_q(g + 2, i, 0)
                max_rows(g + 1, 1 - i, 0)
                if has_load:
                    sp.wait_ge(s_ready, NS * (g + 1))
                    load_k(g + 2, i)
                    load_q(g + 2, i, 1)
                    sp.wait_ge(pv_done, NQ * (g + 1) + FREE)
                    load_v(g + 2, i)
                store_out(g)

            for signal in (*maxrow_ready, out_stored):
                sp.sem_inc(signal, FREE)
            for i in range(2):
                load_k(i, i)
                load_q(i, i, 0)
                load_q(i, i, 1)
                load_v(i, i)
            sp.wait_ge(rows_set, 4)
            max_rows(0, 0, 0)
            with sp.Fori(0, NG // 2 - 1) as pair:
                for i in range(2):
                    step(pair * 2 + i, i, True)
            step(NG - 2, 0, False)
            max_rows(NG - 1, 1, 1)
            store_out(NG - 1)
            sp.wait_ge(out_stored, 16 * NG + FREE)

        @block.gpsimd
        def _(pool):
            for i in range(2):
                nc.gpsimd.memset(qst[i][MAXROW:P, :, :, :], 0.0).then_inc(rows_set, 1)
                nc.gpsimd.memset(kst[i][MAXROW:P, :], 1.0).then_inc(rows_set, 1)

        @block.vector
        def _(dve):
            chain = Chain(dve, dve_chain)

            def max_unit(g, j):
                half = j // HM
                col = (j % REP) * SUB + j // REP % SUB
                if j % HM == 0:
                    dve.wait_ge(max_turned, HALVES * g + half - 1 + FREE)
                dve.wait_ge(max_ready, NM * g + j + 1)
                nc.vector.tensor_reduce(negmax[half][:, col:col + 1], max_bank[j % 2][:, :], AX.X, ALU.max,
                                        negate=True).then_inc(max_read, 1)

            def split_max(g, half):
                dve.wait_ge(max_turned, HALVES * g + half + 1 + FREE)
                dve.wait_ge(maxrow_ready[half], 48 * g + FREE)
                dve.wait_ge(mparts_done, HALVES * g + half + FREE)
                m, parts = turn_bank[0:HM, 0, :], mparts[half]
                chain.link(nc.vector.tensor_copy(parts[:, 0, :], m))
                chain.link(nc.vector.tensor_tensor(mrest[:, :], m, parts[:, 0, :], ALU.subtract))
                chain.link(nc.vector.tensor_copy(parts[:, 1, :], mrest[:, :]))
                nc.vector.tensor_tensor(parts[:, 2, :], mrest[:, :], parts[:, 1, :], ALU.subtract).then_inc(mparts_done, 1)

            def normalise(g, half):
                dve.wait_ge(o_turned, HALVES * g + half + 1 + FREE)
                if half == 0:
                    dve.wait_ge(out_stored, 16 * g + FREE)
                dve.wait_ge(o_normed, HALVES * g + half + FREE)
                t = turn_bank[:, :, :].rearrange("p s (h e) -> p s h e", h=REP)
                chain.link(nc.vector.reciprocal(recip[:, :, :], t[:, :, :, HD]))
                nc.vector.tensor_tensor(out[:, half * SUB:(half + 1) * SUB, :, :], t[:, :, :, 0:HD],
                                        recip[:, :, :].unsqueeze(3).to_broadcast([P, SUB, REP, HD]),
                                        ALU.mult).then_inc(o_normed, 1)

            def around(g, n, first):
                if n == TURN_AT[0] + 1:
                    normalise(g, 0)
                if n == TURN_AT[1] + 1 and not first:
                    normalise(g - 1, 1)
                if n == FOLD_AT[1]:
                    split_max(g, 1)

            def step(g):
                j = 0
                for n in range(HEAD, NQ + HEAD):
                    for j in (2 * (n - HEAD), 2 * (n - HEAD) + 1):
                        max_unit(g + 1, j)
                    around(g if n < NQ else g + 1, n % NQ, False)
                    if n == FOLD_AT[0]:
                        split_max(g + 1, 0)

            for signal in (max_read, mparts_done, o_normed):
                dve.sem_inc(signal, FREE)
            for j in range(NM):
                max_unit(0, j)
                if j == HM:
                    split_max(0, 0)
            PER_STEP = HALVES * 4
            with dve.Fori(0, NG // 2 - 1) as pair:
                chain.enter(pair * (2 * PER_STEP) + 3)
                for i in range(2):
                    step(pair * 2 + i)
            chain.enter((NG - 2) * PER_STEP + 3)
            step(NG - 2)
            for n in range(HEAD, NQ):
                around(NG - 1, n, False)
            normalise(NG - 1, 1)

        @block.scalar
        def _(act):
            def quad(g, n, first):
                act.wait_ge(pv_done, NQ * g + max(n - 1, 0) + FREE)
                for h in range(REP):
                    s = n * REP + h
                    act.wait_ge(s_ready, NS * g + s + 1)
                    nc.scalar.activation(prob[n % 2][:, h, :], s_bank[s % 2][:, :], ACT.Exp).then_inc(exp_done, 1)
                    if h == 1 and n == COPY_AT:
                        copy_out(g, 0)
                    if h == 1 and n == 0 and not first:
                        copy_out(g - 1, 1)

            def copy_out(g, half):
                act.wait_ge(pv_done, NQ * g + (half + 1) * QT + FREE)
                act.wait_ge(o_turned, HALVES * g + half + FREE)
                nc.scalar.copy(osb[:, :], o_bank[:, :]).then_inc(o_copied, 1)

            act.sem_inc(o_copied, FREE)
            for n in range(HEAD):
                quad(0, n, True)
            with act.Fori(0, NG - 1) as g:
                for n in range(HEAD, NQ):
                    quad(g, n, False)
                for n in range(HEAD):
                    quad(g + 1, n, False)
            for n in range(HEAD, NQ):
                quad(NG - 1, n, False)
            copy_out(NG - 1, 1)

        @block.tensor
        def _(pe):
            def max_unit(g, i, k, j):
                t, h = j // REP, j % REP
                if j == 0:
                    pe.wait_ge(k_ready[i], 16 * NBLK * (k + 1))
                    pe.wait_ge(q_ready[i][0], 16 * NBLK * (k + 1))
                if j == HM:
                    pe.wait_ge(q_ready[i][1], 16 * NBLK * (k + 1))
                pe.wait_ge(max_read, NM * g + j - 1 + FREE)
                for half in range(HALVES):
                    last = nc.tensor.matmul(max_bank[j % 2][:, half * TT:(half + 1) * TT], qst[i][0:SROWS, t // SUB, h, t % SUB * P:(t % SUB + 1) * P],
                                            kst[i][0:SROWS, half * TT:(half + 1) * TT], start=True, stop=True)
                last.then_inc(max_ready, 1)

            def turn_max(g, half):
                pe.wait_ge(max_read, NM * g + (half + 1) * HM + FREE)
                pe.wait_ge(mparts_done, HALVES * g + half + FREE)
                pe.wait_ge(o_normed, HALVES * g + half - 1 + FREE)
                nc.tensor.transpose(turn_bank[0:HM, 0, :], negmax[half][:, :], W["ident"][:, :]).then_inc(max_turned, 1)

            def turn_out(g, half, folds):
                pe.wait_ge(o_copied, HALVES * g + half + 1 + FREE)
                pe.wait_ge(o_normed, HALVES * g + half + FREE)
                pe.wait_ge(mparts_done, folds + FREE)
                for s in range(SUB):
                    last = nc.tensor.transpose(turn_bank[:, s, :], osb[:, s * P:(s + 1) * P], W["ident"][:, :])
                last.then_inc(o_turned, 1)

            def scores(g, i, n, h):
                s, half, kt = n * REP + h, n // QT, n % QT
                pe.wait_ge(exp_done, NS * g + s - 1 + FREE)
                nc.tensor.matmul(s_bank[s % 2][:, :], kst[i][:, kt * P:(kt + 1) * P], qst[i][:, half, h, :],
                                 start=True, stop=True).then_inc(s_ready, 1)

            def values(g, i, n):
                half, kt = n // QT, n % QT
                pe.wait_ge(exp_done, NS * g + (n + 1) * REP + FREE)
                if kt == 0:
                    pe.wait_ge(o_copied, HALVES * g + half + FREE)
                for h in range(REP):
                    last = nc.tensor.matmul(o_bank[32 * h:32 * h + 32, :], vst[i][:, kt, :], prob[n % 2][:, h, :],
                                            start=(kt == 0), stop=(kt == QT - 1), tile_position=(0, 32 * h))
                last.then_inc(pv_done, 1)

            def quad(g, i, k, n, units):
                if n % QT == 0:
                    pe.wait_ge(maxrow_ready[n // QT], 48 * (g + 1) + FREE)
                scores(g, i, n, 0)
                scores(g, i, n, 1)
                if n == 1:
                    pe.wait_ge(v_ready[i], 16 * (k + 1))
                if n >= 1:
                    values(g, i, n - 1)
                scores(g, i, n, 2)
                scores(g, i, n, 3)
                units()
                if n == TURN_AT[0]:
                    turn_out(g, 0, HALVES * g + 2)
                if n == FOLD_AT[1]:
                    turn_max(g, 1)
                if n == NQ - 1:
                    values(g, i, n)

            def step(g, i, k):
                for n in range(HEAD, NQ):
                    def units():
                        max_unit(g + 1, 1 - i, k + i, 2 * (n - HEAD))
                        max_unit(g + 1, 1 - i, k + i, 2 * (n - HEAD) + 1)
                    quad(g, i, k, n, units)
                    if n == FOLD_AT[0]:
                        turn_max(g + 1, 0)
                for n in range(HEAD):
                    def units():
                        max_unit(g + 1, 1 - i, k + i, 2 * (n + NQ - HEAD))
                        max_unit(g + 1, 1 - i, k + i, 2 * (n + NQ - HEAD) + 1)
                    quad(g + 1, 1 - i, k + i, n, units)
                    if n == TURN_AT[1]:
                        turn_out(g, 1, HALVES * g + 3)

            for signal in (exp_done, pv_done, max_turned, o_turned):
                pe.sem_inc(signal, FREE)
            for j in range(NM):
                max_unit(0, 0, 0, j)
                if j == HM:
                    turn_max(0, 0)
            pe.wait_ge(rows_set, 4)
            for n in range(HEAD):
                quad(0, 0, 0, n, lambda: None)
            with pe.Fori(0, NG // 2 - 1) as pair:
                for i in range(2):
                    step(pair * 2 + i, i, pair)
            step(NG - 2, 0, NG // 2 - 1)
            for n in range(HEAD, NQ):
                quad(NG - 1, 1, NG // 2 - 1, n, lambda: None)
            turn_out(NG - 1, 1, HALVES * NG)


def output_projection(nc, sem, W, attn_out, src, dst):
    with ExitStack() as c:
        sb = lambda n, s, d: c.enter_context(nc.sbuf_tensor(f"op_{n}", s, d))
        S = lambda n: sem(f"op_{n}")
        turn_bank = [c.enter_context(nc.psum_tensor(f"op_turn{s}", [P, DC, P], F32)) for s in range(SUB)]
        mm_bank = [c.enter_context(nc.psum_tensor(f"op_mm{i}", [P, D], F32)) for i in range(2)]
        ain = sb("ain", [P, SUB, D], F32)
        res = sb("res", [P, SUB, D], F32)
        aT_hi, aT_lo = sb("aT_hi", [P, DC, TT], F32R), sb("aT_lo", [P, DC, TT], F32R)
        raw = [sb(f"raw{i}", [P, TT], F32) for i in range(2)]
        fin = [sb(f"fin{i}", [P, TT], F32) for i in range(SUB)]
        neg = [sb(f"neg{i}", [P, TT], F32) for i in range(2)]
        mask = [sb(f"mask{i}", [P, TT], I32) for i in range(2)]
        ain_ready, res_ready, stored, turned, hi_done, lo_done = (S(n) for n in (
            "ain_ready", "res_ready", "stored", "turned", "hi_done", "lo_done"))
        mm_ready, scaled, pool_cleaned, cleaned, added = (S(n) for n in ("mm_ready", "scaled", "pool_cleaned", "cleaned", "added"))
        signs_ready, mask_ready = S("signs_ready"), S("mask_ready")
        rowsof = lambda t: bass.ds(t * TT, TT) if not isinstance(t, int) else slice(t * TT, (t + 1) * TT)
        attn_v = attn_out.rearrange("(b k) (h s p) c -> b h s p k c", b=BATCH, h=SEQ // TT, p=P)

        block = c.enter_context(nc.Block())

        @block.sync
        def _(sp):
            sp.sem_inc(stored, FREE)

            def load_in(t):
                sp.wait_ge(turned, SUB * t + FREE)
                for s in range(SUB):
                    view = attn_v[bass.ds(t // 2, 1), bass.ds(t % 2, 1), s]
                    sp.dma_start(ain[:, s, :].rearrange("p (k c) -> p k c", k=NKV),
                                 view.rearrange("b h p k c -> (b h p) k c")).then_inc(ain_ready, 16)

            def main(t, has_next):
                sp.wait_ge(stored, 16 * t + FREE)
                sp.dma_start(res[:, :, :], src[rowsof(t), :].rearrange("(s p) d -> p s d", p=P)).then_inc(res_ready, 16)
                if has_next:
                    load_in(t + 1)
                sp.wait_ge(added, SUB * (t + 1) + FREE)
                sp.dma_start(dst[rowsof(t), :].rearrange("(s p) d -> p s d", p=P), res[:, :, :]).then_inc(stored, 16)

            load_in(0)
            with sp.Fori(0, NT - 1) as t:
                main(t, True)
            main(NT - 1, False)
            sp.wait_ge(stored, 16 * NT + FREE)

        @block.gpsimd
        def _(pool):
            for signal in (pool_cleaned, added):
                pool.sem_inc(signal, FREE)
            with pool.Fori(0, NT) as t:
                for step in range(SUB + 2):
                    s = step - 2
                    if s >= 0:
                        pool.wait_ge(cleaned, SUB * t + s + 1 + FREE)
                        if s == 0:
                            pool.wait_ge(res_ready, 16 * (t + 1))
                        nc.gpsimd.tensor_tensor(res[:, s, :], fin[s][:, :], res[:, s, :], ALU.add).then_inc(added, 1)
                    if step < SUB:
                        pool.wait_ge(signs_ready, SUB * t + step + 1)
                        nc.gpsimd.tensor_tensor(fin[step][:, :], fin[step][:, :], neg[step % 2][:, :], ALU.add).then_inc(pool_cleaned, 1)

        @block.vector
        def _(dve):
            apart = S("dve_apart")
            for signal in (cleaned, scaled):
                dve.sem_inc(signal, FREE)

            def signs(t, s):
                dve.wait_ge(mm_ready, SUB * t + s + 1)
                dve.wait_ge(cleaned, SUB * t + s - 1 + FREE)
                nc.vector.tensor_tensor(raw[s % 2][:, :], mm_bank[s % 2][:, :], W["vo_scale"][:, KVD:], ALU.mult).then_inc(scaled, 1)
                dve.wait_ge(scaled, SUB * t + s + 1 + FREE)
                dve.wait_ge(added, SUB * t - SUB + s + 1 + FREE)
                split_by_sign(nc, raw[s % 2][:, :], fin[s][:, :], neg[s % 2][:, :], mask[s % 2][:, :], signs_ready, mask_ready)

            def keep_finite(t, s):
                dve.wait_ge(mask_ready, SUB * t + s + 1)
                dve.wait_ge(pool_cleaned, SUB * t + s + 1 + FREE)
                dve.sem_inc(apart, 1)
                nc.vector.copy_predicated(fin[s][:, :], mask[s % 2][:, :], raw[s % 2][:, :]).then_inc(cleaned, 1)

            with dve.Fori(0, NT) as t:
                for s in range(SUB):
                    dve.wait_ge(hi_done, SUB * t + s + 1)
                    nc.vector.tensor_tensor(aT_lo[:, :, s * P:(s + 1) * P], turn_bank[s][:, :, :],
                                            aT_hi[:, :, s * P:(s + 1) * P].bitcast(F32), ALU.subtract).then_inc(lo_done, 1)
                for step in range(SUB + 1):
                    if step < SUB:
                        signs(t, step)
                    if step >= 1:
                        keep_finite(t, step - 1)

        @block.scalar
        def _(act):
            with act.Fori(0, NT) as t:
                for s in range(SUB):
                    act.wait_ge(turned, SUB * t + s + 1 + FREE)
                    nc.scalar.copy(aT_hi[:, :, s * P:(s + 1) * P], turn_bank[s][:, :, :]).then_inc(hi_done, 1)

        @block.tensor
        def _(pe):
            pe.sem_inc(turned, FREE)
            with pe.Fori(0, NT) as t:
                pe.wait_ge(ain_ready, 16 * SUB * (t + 1))
                for s in range(SUB):
                    for k in range(DC):
                        last = nc.tensor.transpose(turn_bank[s][:, k, :], ain[:, s, k * P:(k + 1) * P], W["ident"][:, :])
                    last.then_inc(turned, 1)
                for s in range(SUB):
                    pe.wait_ge(lo_done, SUB * t + s + 1)
                    pe.wait_ge(scaled, SUB * t + s - 1 + FREE)
                    cols = slice(s * P, (s + 1) * P)
                    for k in range(DC):
                        for i, at in enumerate((aT_hi, aT_lo)):
                            last = nc.tensor.matmul(mm_bank[s % 2][:, :], at[:, k, cols], W["o_sign"][:, k, :],
                                                    start=(k == 0 and i == 0), stop=(k == DC - 1 and i == 1))
                    last.then_inc(mm_ready, 1)


def build(nc, io):
    ctx = ExitStack()
    with ctx:
        sb = lambda n, s, d: ctx.enter_context(nc.sbuf_tensor(n, s, d))
        sem = lambda n: ctx.enter_context(nc.semaphore(n))
        W = {
            "ident": sb("ident", [P, P], F32),
            "neg_half": sb("neg_half", [P, SUB], F32),
            "up_hi": [sb(f"up_hi{w}", [P, DC, HID], F32R) for w in range(2)],
            "up_lo": [sb(f"up_lo{w}", [P, DC, HID], F32R) for w in range(2)],
            "down_hi": sb("down_hi", [P, HC, D], F32R),
            "down_lo": sb("down_lo", [P, HC, D], F32R),
            "qkv_sign": sb("qkv_sign", [P, DC, D + 2 * KVD], F16),
            "o_sign": sb("o_sign", [P, DC, D], F32R),
            "qk_scale": sb("qk_scale", [P, DC + 1], F32),
            "vo_scale": sb("vo_scale", [P, KVD + D], F32),
        }
        weight_prep(nc, sem, io, W)
        ffn(nc, sem, "ffn1", W, io["x"], io["x1"])
        projections(nc, sem, W, io["x1"], io["qparts"], io["kparts"], io["vaug"])
        attention(nc, sem, W, io["qparts"], io["kparts"], io["vaug"], io["attn_out"])
        output_projection(nc, sem, W, io["attn_out"], io["x1"], io["x2"])
        ffn(nc, sem, "ffn2", W, io["x2"], io["out"])


_INS = {'x': 'L0_attn_hidden_states', 'wq': 'L0_attn_q_weight', 'qs': 'L0_attn_q_scale', 'wk': 'L0_attn_k_weight',
        'ks': 'L0_attn_k_scale', 'wv': 'L0_attn_v_weight', 'vs': 'L0_attn_v_scale', 'wo': 'L0_attn_o_weight',
        'os': 'L0_attn_o_scale', 'w1': 'L0_ffn_w1', 's1': 'L0_ffn_s1', 'w2': 'L0_ffn_w2', 's2': 'L0_ffn_s2',
        'w3': 'L0_ffn_w3', 's3': 'L0_ffn_s3'}


def kernel(**inputs):
    import numpy as np
    import concourse.bacc as bacc
    from concourse import mybir as mb
    from concourse.bass_utils import run_bass_kernel_spmd as run

    nc = bacc.Bacc("TRN2", target_bir_lowering=False, num_devices=1)
    arrays, io = {}, {}
    for short, name in _INS.items():
        a = np.ascontiguousarray(inputs[name])
        arrays[f"in_{short}"] = a
        io[short] = nc.dram_tensor(f"in_{short}", a.shape, mb.dt.from_np(a.dtype), kind="ExternalInput").ap()
    out = nc.dram_tensor("out", (BATCH, SEQ, D), F32, kind="ExternalOutput").ap()
    io["x"] = io["x"].rearrange("b s d -> (b s) d")
    io["out"] = out.rearrange("b s d -> (b s) d")
    for name, shape, dt in (("x1", (TOK, D), F32), ("x2", (TOK, D), F32),
                            ("qparts", (3, BATCH * D, SEQ), BF16), ("kparts", (3, BATCH * KVD, SEQ), BF16),
                            ("vaug", (NG, SEQ // TT, P, SUB, 2 * HD), F32), ("attn_out", (NG, SEQ, REP * HD), F32)):
        io[name] = nc.dram_tensor(name, shape, dt, kind="Internal").ap()
    io["row_scratch"] = nc.dram_tensor("row_scratch", (KVD + D,), F32, kind="Internal").ap()
    build(nc, io)
    r = run(nc, [arrays], core_ids=[0])
    return r.results[0]["out"]
```

```python
import concourse.bass as bass
from concourse import mybir
from contextlib import ExitStack

F32 = mybir.dt.float32
F32R = mybir.dt.float32r
BF16 = mybir.dt.bfloat16
F16 = mybir.dt.float16
I32 = mybir.dt.int32
ACT = mybir.ActivationFunctionType
ALU = mybir.AluOpType
AX = mybir.AxisListType

P = 128
BATCH, SEQ, D = 2, 1024, 512
TOK = BATCH * SEQ
HID = 1376
GROUP = 64
NH, NKV, HD = 32, 8, 16
REP = NH // NKV
KVD = NKV * HD
DC = D // P
HC = -(-HID // P)
HTAIL = HID - (HC - 1) * P
TT = 512
NT = TOK // TT
SUB = TT // P
LN_EPS = 1e-5
FIN_LIMIT = 1e6
FREE = 16


class Chain:

    def __init__(self, eng, sem, apart=None):
        self.eng, self.sem, self.apart, self.n, self.at = eng, sem, apart, 0, 0

    def enter(self, base):
        self.at, self.n = base, 0

    def add(self, ins):
        self.n += 1
        ins.then_inc(self.sem, 1)

    def wait(self):
        self.eng.wait_ge(self.sem, self.at + self.n)

    def wait_apart(self):
        self.wait()
        self.eng.sem_inc(self.apart, 1)

    def link(self, ins):
        self.add(ins)
        self.wait()


def shifted(t, step, by, steps, has_prev=True, has_next=True):
    u = step + by
    if u < 0:
        return (t - 1, u + steps) if has_prev else None
    if u >= steps:
        return (t + 1, u - steps) if has_next else None
    return t, u


def all_tiles(eng, main):
    main(0, False, True)
    with eng.Fori(1, NT - 1) as t:
        main(t, True, True)
    main(NT - 1, True, False)


def layernorm_stats(nc, dve, chain, xin, stats, mv, stats_ready):
    for s in range(SUB):
        chain.add(nc.vector.bn_stats(stats[:, s, :], xin[:, s, :]))
    chain.wait_apart()
    for s in range(SUB):
        last = nc.vector.bn_aggr(mv[:, s, :], stats[:, s, :])
    last.then_inc(stats_ready, 1)


def normalise_rows(nc, dve, xin, mv, rstd, rstd_ready, nth, xn_ready):
    dve.wait_ge(rstd_ready, nth)
    for s in range(SUB):
        last = nc.vector.tensor_scalar(xin[:, s, :], xin[:, s, :], mv[:, s, 0:1], rstd[:, s:s + 1],
                                       ALU.subtract, ALU.mult)
    last.then_inc(xn_ready, 1)


def rstd_on_pool(nc, chain, mv, ve, rstd, tmp, neg_half, rstd_ready):
    g = nc.gpsimd
    chain.link(g.tensor_scalar(ve[:, :], mv[:, :, 1], LN_EPS, None, ALU.add))
    chain.link(g.tensor_tensor(rstd[:, :], ve[:, :], neg_half[:, :], ALU.pow))
    chain.link(g.tensor_tensor(tmp[:, :], rstd[:, :], rstd[:, :], ALU.mult))
    chain.add(g.tensor_tensor(tmp[:, :], tmp[:, :], ve[:, :], ALU.mult))
    chain.wait_apart()
    chain.link(g.tensor_scalar(tmp[:, :], tmp[:, :], -0.5, 1.5, ALU.mult, ALU.add))
    g.tensor_tensor(rstd[:, :], rstd[:, :], tmp[:, :], ALU.mult).then_inc(rstd_ready, 1)


RSTD_LINKS = 5


def weight_prep(nc, sem, io, W):
    with ExitStack() as c:
        sb = lambda n, s, d: c.enter_context(nc.sbuf_tensor(n, s, d))
        RING = 4
        bank = [c.enter_context(nc.psum_tensor(f"prep_bank{i}", [P, DC, P], F32)) for i in range(8)]
        BANKS = 4
        sign_bank, down_bank = bank[0:BANKS], bank[BANKS:]
        ident = W["ident"]
        packed = [sb(f"packed_up{i}", [P, DC, GROUP], I32) for i in range(RING)]
        gscale = [sb(f"gscale_up{i}", [P, DC, 2], F32) for i in range(RING)]
        nib = [sb(f"nib{i}", [P, DC, 2, GROUP], I32) for i in range(RING)]
        PR = HID * 4 // (2 * GROUP)
        packed2 = sb("packed2", [P, PR, GROUP], I32)
        gscale2 = sb("gscale2", [P, PR, 2], F32)
        deq2 = sb("deq2", [P, PR, 2, GROUP], F32)
        WRING = 3
        wrow = [sb(f"wrow{i}", [P, D], F32) for i in range(WRING)]
        NS = DC + 1 + 1 + DC
        wmean = sb("wmean", [P, NS], F32)
        wrecip = sb("wrecip", [P, NS], F32)
        par_scale = sb("par_scale", [P, NS], F32)
        row_scale = sb("row_scale", [P, NS], F32)

        w_view = [io[n].rearrange("(o k) c -> o (k c)", k=DC) for n in ("w1", "w3")]
        s_view = [io[n].rearrange("(o g) -> o g", g=2 * DC) for n in ("s1", "s3")]
        UNITS = 2 * HC
        LOOPS = UNITS // RING - 1

        def rows_of(ch):
            if not isinstance(ch, int):
                return P, bass.ds(ch * P, P)
            n = P if ch < HC - 1 else HTAIL
            return n, slice(ch * P, ch * P + n)

        packed_ready = [sem(f"packed_ready{i}") for i in range(RING)]
        nib_ready, nib_float, deq_ready, deq_turned = (sem(n) for n in ("nib_ready", "nib_float", "deq_ready", "deq_turned"))
        hi_done, lo_done = sem("prep_hi_done"), sem("prep_lo_done")
        packed2_ready, nib2_ready, nib2_float, deq2_ready, tr2_ready = (sem(n) for n in (
            "packed2_ready", "nib2_ready", "nib2_float", "deq2_ready", "tr2_ready"))
        hi2_done, lo2_done = sem("hi2_done"), sem("lo2_done")
        wrow_ready = [sem(f"wrow_ready{i}") for i in range(WRING)]
        sign_taken, wrecip_ready = sem("sign_taken"), sem("wrecip_ready")
        sign_turned, sign_out = sem("sign_turned"), sem("sign_out")
        par_ready, row_ready, row_stored, row_back = (sem(n) for n in ("par_ready", "row_ready", "row_stored", "row_back"))
        ident_zero, ident_ready, prep_dve = sem("ident_zero"), sem("ident_ready"), sem("prep_dve")

        SIGN = [("wq", j) for j in range(DC)] + [("wk", 0), ("wv", 0)] + [("wo", j) for j in range(DC)]

        xin = W["xin"]
        stats, mv = sb("prep_stats", [P, SUB, 6], F32), sb("prep_mv", [P, SUB, 2], F32)
        ve, rstd, tmp = (sb(f"prep_{n}", [P, SUB], F32) for n in ("ve", "rstd", "tmp"))
        x_ready, stats_ready, rstd_ready, xn_ready = (sem(f"prep_{n}") for n in ("x_ready", "stats_ready", "rstd_ready", "xn_ready"))
        pool_chain = sem("prep_pool")

        PIECES = 4
        pieces = [slice(PR * i // PIECES, PR * (i + 1) // PIECES) for i in range(PIECES)]
        ON_POOL = 2
        deq2_int = deq2.bitcast(I32)

        def scale_piece(eng, i):
            r, n = pieces[i], pieces[i].stop - pieces[i].start
            source = deq2 if i < ON_POOL else deq2_int
            eng.tensor_tensor(deq2[:, r].rearrange("p r h c -> p (r h) c"), source[:, r].rearrange("p r h c -> p (r h) c"),
                              gscale2[:, r].rearrange("p r h -> p (r h)").unsqueeze(2).to_broadcast([P, 2 * n, GROUP]),
                              ALU.mult).then_inc(deq2_ready, 1)

        block = c.enter_context(nc.Block())

        @block.sync
        def _(sp):
            def load(u, ch, w, slot, before):
                n, rows = rows_of(ch)
                if before is None or before > 0:
                    sp.wait_ge(deq_ready, u - RING + 1 + FREE)
                sp.dma_start(packed[slot][0:n].rearrange("p k c -> p (k c)"), w_view[w][rows, :]).then_inc(packed_ready[slot], 16)
                sp.dma_start(gscale[slot][0:n].rearrange("p k h -> p (k h)"), s_view[w][rows, :]).then_inc(packed_ready[slot], 16)

            for v in range(RING):
                load(v, v // 2, v % 2, v, 0)
            with sp.Fori(0, LOOPS) as i:
                for v in range(RING):
                    load(i * RING + RING + v, i * 2 + 2 + v // 2, v % 2, v, None)
            for u in range(RING * (LOOPS + 1), UNITS):
                load(u, u // 2, u % 2, u % RING, 1)
            sp.dma_start(packed2.rearrange("p r c -> p (r c)"),
                         io["w2"].rearrange("(p r) c -> p (r c)", p=P)).then_inc(packed2_ready, 16)
            sp.dma_start(gscale2.rearrange("p r h -> p (r h)"), io["s2"].rearrange("(p g) -> p g", p=P)).then_inc(packed2_ready, 16)
            with nc.allow_non_contiguous_dma("one scale per row"):
                for name, at, n in (("qs", 0, DC), ("ks", DC, 1), ("vs", DC + 1, 1), ("os", DC + 2, DC)):
                    sp.dma_start(par_scale[:, at:at + n], io[name].rearrange("(c p) -> p c", p=P)).then_inc(par_ready, 16)
            for u in range(NS):
                name, j = SIGN[u]
                if u >= WRING:
                    sp.wait_ge(sign_turned, u - WRING + 1)
                sp.dma_start(wrow[u % WRING][:, :], io[name][j * P:(j + 1) * P, :]).then_inc(wrow_ready[u % WRING], 16)
                if u == WRING - 1:
                    sp.dma_start(xin[:, :, :], io["x"][0:TT, :].rearrange("(s p) d -> p s d", p=P)).then_inc(x_ready, 16)
            sp.wait_ge(row_ready, 1)
            with nc.allow_non_contiguous_dma("one scale per row"):
                sp.dma_start(io["row_scratch"].rearrange("(c p) -> p c", p=P), row_scale[:, DC + 1:NS]).then_inc(row_stored, 16)
            sp.wait_ge(row_stored, 16)
            sp.dma_start(W["vo_scale"][:, :], io["row_scratch"][None, :].to_broadcast([P, KVD + D])).then_inc(row_back, 16)
            sp.wait_ge(row_back, 16)

        @block.gpsimd
        def _(pool):
            def scale(u, ch, slot):
                n, _ = rows_of(ch)
                pool.wait_ge(nib_float, u + 1)
                pair = nib[slot][0:n].rearrange("p k h c -> p (k h) c").bitcast(F32)
                nc.gpsimd.tensor_tensor(pair,
                                        gscale[slot][0:n].rearrange("p k h -> p (k h)").unsqueeze(2).to_broadcast([n, 2 * DC, GROUP]),
                                        pair, ALU.mult).then_inc(deq_ready, 1)

            pool.sem_inc(deq_ready, FREE)
            nc.gpsimd.memset(ident[:, :], 0.0).then_inc(ident_zero, 1)
            pool.wait_ge(ident_zero, 1)
            nc.gpsimd.affine_select(out=ident[:, :], in_=ident[:, :], compare_op=ALU.not_equal, fill=1.0, base=0,
                                    pattern=[[-1, P]], channel_multiplier=1).then_inc(ident_ready, 1)
            nc.gpsimd.memset(W["neg_half"][:, :], -0.5)
            with pool.Fori(0, LOOPS) as i:
                for v in range(RING):
                    scale(i * RING + v, i * 2 + v // 2, v)
            for u in range(RING * LOOPS, UNITS):
                scale(u, u // 2, u % RING)
            for i in range(ON_POOL):
                pool.wait_ge(nib2_float, i + 1)
                scale_piece(nc.gpsimd, i)
            pool.wait_ge(stats_ready, 1)
            rstd_on_pool(nc, Chain(pool, pool_chain, W["pool_apart"]), mv, ve, rstd, tmp, W["neg_half"], rstd_ready)

        @block.vector
        def _(dve):
            chain = Chain(dve, prep_dve, W["dve_apart"])

            def unpack(u, ch, slot, uses):
                n, _ = rows_of(ch)
                dve.wait_ge(packed_ready[slot], 32 * uses)
                dve.wait_ge(deq_turned, u - RING + 1 + FREE)
                nc.vector.tensor_scalar(nib[slot][0:n, :, 0, :], packed[slot][0:n], 4, None, ALU.arith_shift_right)
                nc.vector.tensor_scalar(nib[slot][0:n, :, 1, :], packed[slot][0:n], 28, 28, ALU.arith_shift_left,
                                        ALU.arith_shift_right).then_inc(nib_ready, 1)

            def low_part(u, ch, w, slot):
                n, cols = rows_of(ch)
                dve.wait_ge(hi_done, u + 1)
                nc.vector.tensor_tensor(W["up_lo"][w][:, :, cols], bank[slot][:, :, 0:n],
                                        W["up_hi"][w][:, :, cols].bitcast(F32), ALU.subtract).then_inc(lo_done, 1)

            AHEAD = 3
            dve.sem_inc(lo_done, FREE)
            for u in range(AHEAD):
                unpack(u, u // 2, u, 1)
            with dve.Fori(0, LOOPS) as i:
                for v in range(RING):
                    a = v + AHEAD
                    unpack(i * RING + a, i * 2 + a // 2, a % RING, i + a // RING + 1)
                    low_part(i * RING + v, i * 2 + v // 2, v % 2, v)
            for u in range(RING * LOOPS, UNITS):
                a = u + AHEAD
                if a < UNITS:
                    unpack(a, a // 2, a % RING, a // RING + 1)
                low_part(u, u // 2, u % 2, u % RING)

            dve.wait_ge(packed2_ready, 32)
            for r in pieces:
                nc.vector.tensor_scalar(deq2_int[:, r, 0, :], packed2[:, r, :], 4, None, ALU.arith_shift_right)
                nc.vector.tensor_scalar(deq2_int[:, r, 1, :], packed2[:, r, :], 28, 28, ALU.arith_shift_left,
                                        ALU.arith_shift_right).then_inc(nib2_ready, 1)

            def row_stats(u):
                dve.wait_ge(wrow_ready[u % WRING], (u // WRING + 1) * 16)
                chain.link(nc.vector.tensor_reduce(wmean[:, u:u + 1], wrow[u % WRING][:, :], AX.X, ALU.add,
                                                   apply_absolute_value=True))
                chain.link(nc.vector.tensor_scalar(wmean[:, u:u + 1], wmean[:, u:u + 1], 1.0 / D, 1e-8, ALU.mult, ALU.max))
                nc.vector.reciprocal(wrecip[:, u:u + 1], wmean[:, u:u + 1]).then_inc(wrecip_ready, 1)

            def low_part2(u):
                n, _ = rows_of(u)
                dve.wait_ge(hi2_done, u + 1)
                nc.vector.tensor_tensor(W["down_lo"][0:n, u, :].rearrange("h (p j) -> h j p", j=4), down_bank[u % BANKS][0:n],
                                        W["down_hi"][0:n, u, :].bitcast(F32).rearrange("h (p j) -> h j p", j=4),
                                        ALU.subtract).then_inc(lo2_done, 1)

            for i in range(ON_POOL, PIECES):
                dve.wait_ge(nib2_ready, i + 1)
                scale_piece(nc.vector, i)
            ROWS_AHEAD = 2
            for u in range(ROWS_AHEAD):
                row_stats(u)
            dve.wait_ge(x_ready, 16)
            layernorm_stats(nc, dve, chain, xin, stats, mv, stats_ready)
            for u in range(HC):
                if u + ROWS_AHEAD < NS:
                    row_stats(u + ROWS_AHEAD)
                if u + ROWS_AHEAD == NS:
                    dve.wait_ge(par_ready, 64)
                    chain.link(nc.vector.tensor_tensor(row_scale[:, :], wmean[:, :], par_scale[:, :], ALU.mult))
                    nc.vector.tensor_copy(W["qk_scale"][:, :], row_scale[:, 0:DC + 1]).then_inc(row_ready, 1)
                low_part2(u)
                if u == 3:
                    normalise_rows(nc, dve, xin, mv, rstd, rstd_ready, 1, xn_ready)

        @block.scalar
        def _(act):
            def to_float(u, ch, slot):
                n, _ = rows_of(ch)
                act.wait_ge(nib_ready, u + 1)
                values = nib[slot][0:n].rearrange("p k h c -> p (k h c)")
                nc.scalar.copy(values.bitcast(F32), values).then_inc(nib_float, 1)

            def high_part(u, ch, w, slot):
                n, cols = rows_of(ch)
                act.wait_ge(deq_turned, u + 1 + FREE)
                nc.scalar.copy(W["up_hi"][w][:, :, cols], bank[slot][:, :, 0:n]).then_inc(hi_done, 1)

            def sign_copy(u):
                act.wait_ge(sign_turned, u + 1)
                name, j = SIGN[u]
                if name == "wo":
                    out = W["o_sign"][:, :, j * P:(j + 1) * P]
                else:
                    at = {"wq": 0, "wk": D, "wv": D + KVD}[name] + j * P
                    out = W["qkv_sign"][:, :, at:at + P]
                nc.scalar.copy(out, sign_bank[u % BANKS][:, :, :]).then_inc(sign_out, 1)

            AHEAD = 2
            for u in range(AHEAD):
                to_float(u, u // 2, u)
            with act.Fori(0, LOOPS) as i:
                for v in range(RING):
                    a = v + AHEAD
                    to_float(i * RING + a, i * 2 + a // 2, a % RING)
                    high_part(i * RING + v, i * 2 + v // 2, v % 2, v)
            for u in range(RING * LOOPS, UNITS):
                a = u + AHEAD
                if a < UNITS:
                    to_float(a, a // 2, a % RING)
                high_part(u, u // 2, u % 2, u % RING)
            for i in range(ON_POOL):
                act.wait_ge(nib2_ready, i + 1)
                nc.scalar.copy(deq2[:, pieces[i]], deq2_int[:, pieces[i]]).then_inc(nib2_float, 1)

            def take_sign(u):
                act.wait_ge(wrecip_ready, u + 1)
                nc.scalar.activation(wrow[u % WRING][:, :], wrow[u % WRING][:, :], ACT.Sign,
                                     scale=wrecip[:, u:u + 1]).then_inc(sign_taken, 1)

            take_sign(0)
            for u in range(HC):
                n, _ = rows_of(u)
                if u + 1 < NS:
                    take_sign(u + 1)
                act.wait_ge(tr2_ready, u + 1)
                nc.scalar.copy(W["down_hi"][0:n, u, :].rearrange("h (p j) -> h j p", j=4),
                               down_bank[u % BANKS][0:n]).then_inc(hi2_done, 1)
                if u >= 1:
                    sign_copy(u - 1)

        @block.tensor
        def _(pe):
            pe.sem_inc(deq_turned, FREE)
            pe.wait_ge(ident_ready, 1)

            def turn(u, ch, slot):
                n, _ = rows_of(ch)
                pe.wait_ge(deq_ready, u + 1 + FREE)
                pe.wait_ge(lo_done, u - RING + 1 + FREE)
                for k in range(DC):
                    last = nc.tensor.transpose(bank[slot][:, k, 0:n], nib[slot][0:n, k].rearrange("p h c -> p (h c)").bitcast(F32),
                                               ident[0:n, 0:n])
                last.then_inc(deq_turned, 1)

            with pe.Fori(0, LOOPS) as i:
                for v in range(RING):
                    turn(i * RING + v, i * 2 + v // 2, v)
            for u in range(RING * LOOPS, UNITS):
                turn(u, u // 2, u % RING)
            pe.wait_ge(deq2_ready, PIECES)
            d2 = deq2.rearrange("p r h c -> p (r h c)").rearrange("p (j n) -> p j n", j=4)
            for u in range(HC):
                n, _ = rows_of(u)
                if u >= BANKS:
                    pe.wait_ge(lo2_done, u - BANKS + 1)
                for j in range(4):
                    last = nc.tensor.transpose(down_bank[u % BANKS][0:n, j, :], d2[:, j, u * P:u * P + n], ident[:, :])
                last.then_inc(tr2_ready, 1)
                if u < NS:
                    if u == 0:
                        pe.wait_ge(lo_done, UNITS + FREE)
                    if u >= BANKS:
                        pe.wait_ge(sign_out, u - BANKS + 1)
                    pe.wait_ge(sign_taken, u + 1)
                    for k in range(DC):
                        last = nc.tensor.transpose(sign_bank[u % BANKS][:, k, :], wrow[u % WRING][:, k * P:(k + 1) * P], ident[:, :])
                    last.then_inc(sign_turned, 1)


def ffn(nc, sem, tag, W, src, dst, hand_on):
    with ExitStack() as c:
        sb = lambda n, s, d: c.enter_context(nc.sbuf_tensor(f"{tag}_{n}", s, d))
        S = lambda n: sem(f"{tag}_{n}")
        up_bank = [[c.enter_context(nc.psum_tensor(f"{tag}_up{i}{w}", [P, TT], F32)) for w in range(2)] for i in range(2)]
        y_bank = [c.enter_context(nc.psum_tensor(f"{tag}_y{s}", [P, D], F32)) for s in range(SUB)]
        turn_bank = [up_bank[1][0], up_bank[1][1], up_bank[0][0], up_bank[1][0]]
        xin = W["xin"]
        xres = sb("xres", [P, SUB, D], F32)
        xT_hi, xT_lo = sb("xT_hi", [P, DC, TT], F32R), sb("xT_lo", [P, DC, TT], F32R)
        sil, h = sb("sil", [P, TT], F32), sb("h", [P, TT], F32)
        h_hi = [sb(f"h_hi{i}", [P, TT], F32R) for i in range(2)]
        h_lo = [sb(f"h_lo{i}", [P, TT], F32R) for i in range(2)]
        stats, mv = sb("stats", [P, SUB, 6], F32), sb("mv", [P, SUB, 2], F32)
        ve, rstd, tmp = sb("ve", [P, SUB], F32), sb("rstd", [P, SUB], F32), sb("tmp", [P, SUB], F32)

        xin_ready, xres_ready, out_stored = S("xin_ready"), S("xres_ready"), S("out_stored")
        stats_ready, rstd_ready, xn_ready = S("stats_ready"), S("rstd_ready"), S("xn_ready")
        turned, xT_hi_done, xT_lo_done = S("turned"), S("xT_hi_done"), S("xT_lo_done")
        up_ready, a_read, b_read, hi_done, lo_done = (S(n) for n in ("up_ready", "a_read", "b_read", "h_hi_done", "h_lo_done"))
        down_done, y_done = S("down_done"), S("y_done")
        dve_chain, pool_chain = S("dve_chain"), S("pool_chain")
        rows = lambda m: P if m < HC - 1 else HTAIL
        tile = lambda ap, t: (ap[bass.ds(t * TT, TT), :] if not isinstance(t, int) else ap[t * TT:(t + 1) * TT, :]
                              ).rearrange("(s p) d -> p s d", p=P)

        block = c.enter_context(nc.Block())

        @block.sync
        def _(sp):
            def load_in(t):
                sp.wait_ge(turned, SUB * t)
                sp.dma_start(xin[:, :, :], tile(src, t)).then_inc(xin_ready, 16)

            def residual(t):
                sp.wait_ge(out_stored, 16 * t + FREE)
                sp.dma_start(xres[:, :, :], tile(src, t)).then_inc(xres_ready, 16)

            def store(t):
                sp.wait_ge(y_done, SUB * (t + 1) + FREE)
                sp.dma_start(tile(dst, t), xres[:, :, :]).then_inc(out_stored, 16)

            sp.sem_inc(out_stored, FREE)
            with sp.Fori(0, NT - 1) as t:
                residual(t)
                load_in(t + 1)
                store(t)
            residual(NT - 1)
            if hand_on:
                sp.wait_ge(turned, SUB * NT)
                sp.dma_start(xin[:, :, :], tile(dst, 0)).then_inc(xin_ready, 16)
            for s in range(SUB):
                sp.wait_ge(y_done, SUB * (NT - 1) + s + 1 + FREE)
                sp.dma_start(tile(dst, NT - 1)[:, s, :], xres[:, s, :]).then_inc(out_stored, 16)
            sp.wait_ge(out_stored, 16 * (NT - 1 + SUB) + FREE)

        @block.gpsimd
        def _(pool):
            chain = Chain(pool, pool_chain, W["pool_apart"])
            pool.sem_inc(rstd_ready, FREE)
            with pool.Fori(1, NT + 1 if hand_on else NT) as t:
                chain.enter((t - 1) * RSTD_LINKS)
                pool.wait_ge(stats_ready, t)
                pool.wait_ge(xn_ready, t - 1 + FREE)
                pool.sem_inc(chain.apart, 1)
                rstd_on_pool(nc, chain, mv, ve, rstd, tmp, W["neg_half"], rstd_ready)

        @block.vector
        def _(dve):
            chain = Chain(dve, dve_chain, W["dve_apart"])

            def stats_of(t):
                dve.wait_ge(xin_ready, 16 * t)
                dve.wait_ge(rstd_ready, t - 1 + FREE)
                chain.enter((t - 1) * SUB)
                layernorm_stats(nc, dve, chain, xin, stats, mv, stats_ready)

            def normalise(t):
                normalise_rows(nc, dve, xin, mv, rstd, rstd_ready, t + FREE, xn_ready)

            def xT_low(t):
                for s in range(SUB):
                    dve.wait_ge(xT_hi_done, SUB * t + s + 1)
                    nc.vector.tensor_tensor(xT_lo[:, :, s * P:(s + 1) * P],
                                            turn_bank[s][:, :].rearrange("p (k n) -> p k n", k=DC),
                                            xT_hi[:, :, s * P:(s + 1) * P].bitcast(F32), ALU.subtract).then_inc(xT_lo_done, 1)

            def main(t, has_next):
                for m in range(HC):
                    n, c0 = rows(m), t * HC + m
                    dve.wait_ge(a_read, c0 + 1)
                    dve.wait_ge(hi_done, c0 + FREE)
                    dve.wait_ge(lo_done, c0 + FREE)
                    nc.vector.tensor_tensor(h[0:n], sil[0:n], up_bank[m % 2][1][0:n, :], ALU.mult).then_inc(b_read, 1)
                    dve.wait_ge(hi_done, c0 + 1 + FREE)
                    nc.vector.tensor_tensor(h_lo[m % 2][0:n], h[0:n], h_hi[m % 2][0:n].bitcast(F32),
                                            ALU.subtract).then_inc(lo_done, 1)
                    if m == 2 and (has_next or hand_on):
                        stats_of(t + 1)
                    if m == 4 and (has_next or hand_on):
                        normalise(t + 1)
                if has_next:
                    xT_low(t + 1)
                dve.wait_ge(xres_ready, 16 * (t + 1))
                dve.wait_ge(down_done, HC * (t + 1) + FREE)
                for s in range(SUB):
                    nc.vector.scalar_tensor_tensor(xres[:, s, :], y_bank[s][:, :], 0.5, xres[:, s, :],
                                                   ALU.mult, ALU.add).then_inc(y_done, 1)

            for signal in (b_read, lo_done, y_done, xn_ready):
                dve.sem_inc(signal, FREE)
            xT_low(0)
            with dve.Fori(0, NT - 1) as t:
                main(t, True)
            main(NT - 1, False)

        @block.scalar
        def _(act):
            def xT_high(t):
                for s in range(SUB):
                    act.wait_ge(turned, SUB * t + s + 1)
                    nc.scalar.copy(xT_hi[:, :, s * P:(s + 1) * P],
                                   turn_bank[s][:, :].rearrange("p (k n) -> p k n", k=DC)).then_inc(xT_hi_done, 1)

            def main(t, has_next):
                for m in range(HC):
                    n, c0 = rows(m), t * HC + m
                    act.wait_ge(up_ready, c0 + 1)
                    act.wait_ge(b_read, c0 + FREE)
                    nc.scalar.activation(sil[0:n], up_bank[m % 2][0][0:n, :], ACT.Silu).then_inc(a_read, 1)
                    act.wait_ge(b_read, c0 + 1 + FREE)
                    act.wait_ge(down_done, t * HC + max(m - 1, 0) + FREE)
                    nc.scalar.copy(h_hi[m % 2][0:n], h[0:n]).then_inc(hi_done, 1)
                if has_next:
                    xT_high(t + 1)

            act.sem_inc(hi_done, FREE)
            xT_high(0)
            with act.Fori(0, NT - 1) as t:
                main(t, True)
            main(NT - 1, False)

        @block.tensor
        def _(pe):
            def turn(t, s):
                for k in range(DC):
                    last = nc.tensor.transpose(turn_bank[s][:, k * P:(k + 1) * P], xin[:, s, k * P:(k + 1) * P], W["ident"][:, :])
                last.then_inc(turned, 1)

            def up(t, m):
                n, c0 = rows(m), t * HC + m
                if m >= 2:
                    pe.wait_ge(a_read, c0 - 1)
                    pe.wait_ge(b_read, c0 - 1 + FREE)
                cols = slice(m * P, m * P + n)
                for w in range(2):
                    for k in range(DC):
                        parts = ((W["up_hi"], xT_hi), (W["up_hi"], xT_lo), (W["up_lo"], xT_hi))
                        for i, (wt, xt) in enumerate(parts):
                            last = nc.tensor.matmul(up_bank[m % 2][w][0:n, :], wt[w][:, k, cols], xt[:, k, :],
                                                    start=(k == 0 and i == 0), stop=(k == DC - 1 and i == 2))
                last.then_inc(up_ready, 1)

            def down(t, m):
                n, c0 = rows(m), t * HC + m
                if m == 0:
                    pe.wait_ge(y_done, SUB * t + FREE)
                pe.wait_ge(lo_done, c0 + 1 + FREE)
                for s in range(SUB):
                    cols = slice(s * P, (s + 1) * P)
                    parts = ((h_hi, W["down_hi"]), (h_lo, W["down_hi"]), (h_hi, W["down_lo"]))
                    for i, (ht, wt) in enumerate(parts):
                        last = nc.tensor.matmul(y_bank[s][:, :], ht[m % 2][0:n, cols], wt[0:n, m, :],
                                                start=(m == 0 and i == 0), stop=(m == HC - 1 and i == 2))
                last.then_inc(down_done, 1)

            def main(t, has_next):
                pe.wait_ge(xT_lo_done, SUB * (t + 1))
                up(t, 0)
                for m in range(1, HC):
                    up(t, m)
                    if m < HC - 1:
                        down(t, m - 1)
                if has_next:
                    pe.wait_ge(xn_ready, t + 1 + FREE)
                    pe.wait_ge(a_read, t * HC + HC - 1)
                    pe.wait_ge(b_read, t * HC + HC - 1 + FREE)
                    turn(t + 1, 0)
                    turn(t + 1, 1)
                down(t, HC - 2)
                if has_next:
                    pe.wait_ge(a_read, t * HC + HC)
                    pe.wait_ge(b_read, t * HC + HC + FREE)
                    turn(t + 1, 2)
                    pe.wait_ge(xT_lo_done, SUB * (t + 1) + 1)
                    turn(t + 1, 3)
                down(t, HC - 1)

            pe.sem_inc(down_done, FREE)
            for s in range(SUB):
                if s == 3:
                    pe.wait_ge(xT_lo_done, 1)
                turn(0, s)
            with pe.Fori(0, NT - 1) as t:
                main(t, True)
            main(NT - 1, False)


def split_by_sign(nc, raw, pos, neg, signs_ready):
    nc.vector.tensor_scalar(pos, raw, 0.0, FIN_LIMIT, ALU.max, ALU.min)
    nc.vector.tensor_scalar(neg, raw, 0.0, -FIN_LIMIT, ALU.min, ALU.max).then_inc(signs_ready, 1)


def mask_finite(nc, raw, mask, mask_ready):
    nc.vector.tensor_scalar(mask, raw, 0.0, 0.0, ALU.mult, ALU.is_equal).then_inc(mask_ready, 1)


def projections(nc, sem, W, src, qparts, kparts, vaug):
    with ExitStack() as c:
        sb = lambda n, s, d: c.enter_context(nc.sbuf_tensor(f"qkv_{n}", s, d))
        S = lambda n: sem(f"qkv_{n}")
        turn_bank = [c.enter_context(nc.psum_tensor(f"qkv_turn{s}", [P, DC, P], F32)) for s in range(SUB)]
        mm_bank = [c.enter_context(nc.psum_tensor(f"qkv_mm{i}", [P, TT], F32)) for i in range(3)]
        PRING = 3
        xin = W["xin"]
        xT_hi, xT_lo = sb("xT_hi", [P, 2 * DC, TT], F16), sb("xT_lo", [P, 2 * DC, TT], F16)
        raw = [sb(f"raw{i}", [P, TT], F32) for i in range(3)]
        fin = [sb(f"fin{i}", [P, TT], F32) for i in range(3)]
        neg = [sb(f"neg{i}", [P, TT], F32) for i in range(2)]
        rest = [sb(f"rest{i}", [P, TT], F32) for i in range(2)]
        parts = [sb(f"parts{i}", [P, 3, TT], BF16) for i in range(PRING)]
        vt = sb("vt", [P, NKV, SUB, 2 * HD], F32)
        stats, mv = sb("stats", [P, SUB, 6], F32), sb("mv", [P, SUB, 2], F32)
        ve, rstd, tmp = sb("ve", [P, SUB], F32), sb("rstd", [P, SUB], F32), sb("tmp", [P, SUB], F32)

        xin_ready, stats_ready, rstd_ready, xn_ready = (S(n) for n in ("xin_ready", "stats_ready", "rstd_ready", "xn_ready"))
        turned, xT_hi_done, xT_lo_done = S("turned"), S("xT_hi_done"), S("xT_lo_done")
        mm_ready, scaled, v_scaled = S("mm_ready"), S("scaled"), S("v_scaled")
        signs_ready, mask_ready, pool_cleaned, cleaned = (S(n) for n in ("signs_ready", "mask_ready", "pool_cleaned", "cleaned"))
        part1_done, rest_done, part2_done, part3_done = (S(n) for n in ("part1_done", "rest_done", "part2_done", "part3_done"))
        v_placed, v_stored, ones_set = S("v_placed"), S("v_stored"), S("ones_set")
        parts_stored = [S(f"parts_stored{i}") for i in range(PRING)]
        dve_chain, pool_chain = S("dve_chain"), S("pool_chain")
        NQK = DC + 1
        V = NQK
        UNITS = NQK + 1
        ring_uses = [len(range(i, NQK, PRING)) for i in range(PRING)]
        stores_before = lambda t, u: ring_uses[u % PRING] * t + u // PRING
        half_of = lambda t: slice(t % 2 * DC, t % 2 * DC + DC) if isinstance(t, int) else bass.ds(t % 2 * DC, DC)
        rowsof = lambda t: bass.ds(t * TT, TT) if not isinstance(t, int) else slice(t * TT, (t + 1) * TT)

        block = c.enter_context(nc.Block())

        @block.sync
        def _(sp):
            for signal in (*parts_stored, v_stored):
                sp.sem_inc(signal, FREE)

            def load(t):
                sp.wait_ge(turned, SUB * t)
                sp.dma_start(xin[:, :, :], src[rowsof(t), :].rearrange("(s p) d -> p s d", p=P)).then_inc(xin_ready, 16)

            def main(t, has_load):
                b, half = t // 2, t % 2
                cols = bass.ds(half * TT, TT)
                for u in range(NQK):
                    sp.wait_ge(part3_done, NQK * t + u + 1 + FREE)
                    dst, row = (qparts, b * D + u * P) if u < DC else (kparts, b * KVD)
                    sp.dma_start(dst[:, bass.ds(row, P), cols].rearrange("a r t -> r a t"),
                                 parts[u % PRING][:, :, :]).then_inc(parts_stored[u % PRING], 16)
                    if u == 0 and has_load:
                        load(t + 2)
                sp.wait_ge(v_placed, t + 1 + FREE)
                dst = vaug.rearrange("(b k) h p s c -> b h p k (s c)", b=BATCH)
                sp.dma_start(dst[bass.ds(b, 1), bass.ds(half, 1)].rearrange("a o p k n -> (a o p) k n"),
                             vt.rearrange("p k s c -> p k (s c)")).then_inc(v_stored, 16)

            load(1)
            with sp.Fori(0, NT - 2) as t:
                main(t, True)
            main(NT - 2, False)
            main(NT - 1, False)
            for i in range(PRING):
                sp.wait_ge(parts_stored[i], 16 * ring_uses[i] * NT + FREE)
            sp.wait_ge(v_stored, 16 * NT + FREE)

        def wait_scaled(eng, t, u):
            if u < V:
                eng.wait_ge(scaled, NQK * t + u + 1 + FREE)
            else:
                eng.wait_ge(v_scaled, t + 1 + FREE)

        behind = lambda t, step, by, has_prev: shifted(t, step, -by, UNITS, has_prev, False)

        @block.gpsimd
        def _(pool):
            chain = Chain(pool, pool_chain, W["pool_apart"])
            nc.gpsimd.memset(vt[:, :, :, :], 1.0).then_inc(ones_set, 1)

            def rstd_of(t):
                chain.enter((t - 1) * RSTD_LINKS)
                pool.wait_ge(stats_ready, t)
                pool.wait_ge(xn_ready, t - 1 + FREE)
                pool.sem_inc(chain.apart, 1)
                rstd_on_pool(nc, chain, mv, ve, rstd, tmp, W["neg_half"], rstd_ready)

            def third_part(at):
                if at is None or at[1] == V:
                    return
                t, u = at
                pool.wait_ge(part2_done, NQK * t + u + 1)
                nc.gpsimd.tensor_tensor(parts[u % PRING][:, 2, :], rest[u % 2][:, :], parts[u % PRING][:, 1, :],
                                        ALU.subtract).then_inc(part3_done, 1)

            def main(t, has_prev, has_next):
                for u in range(UNITS):
                    pool.wait_ge(signs_ready, UNITS * t + u + 1)
                    nc.gpsimd.tensor_tensor(fin[u % 3][:, :], fin[u % 3][:, :], neg[u % 2][:, :], ALU.add).then_inc(pool_cleaned, 1)
                    third_part(behind(t, u, 3, has_prev))
                    if u == 0 and has_next:
                        rstd_of(t + 1)

            def drain():
                for step in range(UNITS, UNITS + 3):
                    third_part(behind(NT - 1, step, 3, True))

            for signal in (pool_cleaned, rstd_ready, part3_done):
                pool.sem_inc(signal, FREE)
            all_tiles(pool, main)
            drain()

        @block.vector
        def _(dve):
            chain = Chain(dve, dve_chain, W["dve_apart"])

            def stats_of(t):
                chain.enter((t - 1) * SUB)
                dve.wait_ge(xin_ready, 16 * t)
                dve.wait_ge(rstd_ready, t - 1 + FREE)
                layernorm_stats(nc, dve, chain, xin, stats, mv, stats_ready)

            def normalise(t):
                normalise_rows(nc, dve, xin, mv, rstd, rstd_ready, t + FREE, xn_ready)

            def xT_low(t, s):
                dve.wait_ge(xT_hi_done, SUB * t + s + 1)
                nc.vector.tensor_tensor(xT_lo[:, half_of(t), s * P:(s + 1) * P], turn_bank[s][:, :, :],
                                        xT_hi[:, half_of(t), s * P:(s + 1) * P], ALU.subtract).then_inc(xT_lo_done, 1)

            def signs(t, u):
                if u == V:
                    dve.wait_ge(mm_ready, UNITS * t + u + 1)
                    dve.wait_ge(cleaned, UNITS * t + u - 2 + FREE)
                    nc.vector.tensor_tensor(raw[u % 3][:, :].rearrange("p (s c) -> p s c", s=SUB),
                                            mm_bank[u % 3][:, :].rearrange("p (s c) -> p s c", s=SUB),
                                            W["vo_scale"][:, 0:KVD].unsqueeze(1).to_broadcast([P, SUB, KVD]),
                                            ALU.mult).then_inc(v_scaled, 1)
                wait_scaled(dve, t, u)
                if u == 2:
                    dve.wait_ge(v_placed, t + FREE)
                else:
                    dve.wait_ge(rest_done, NQK * t + (u - 1 if u < 2 else u - 2) + FREE)
                dve.wait_ge(cleaned, UNITS * t + u - 1 + FREE)
                split_by_sign(nc, raw[u % 3][:, :], fin[u % 3][:, :], neg[u % 2][:, :], signs_ready)

            def keep_finite(at):
                if at is None:
                    return
                t, u = at
                dve.wait_ge(pool_cleaned, UNITS * t + u + 1 + FREE)
                mask = neg[u % 2][:, :].bitcast(I32)
                mask_finite(nc, raw[u % 3][:, :], mask, mask_ready)
                dve.wait_ge(mask_ready, UNITS * t + u + 1)
                dve.sem_inc(chain.apart, 1)
                nc.vector.copy_predicated(fin[u % 3][:, :], mask, raw[u % 3][:, :]).then_inc(cleaned, 1)

            def take_rest(at):
                if at is None or at[1] == V:
                    return
                t, u = at
                dve.wait_ge(part1_done, NQK * t + u + 1)
                dve.wait_ge(part3_done, NQK * t + max(u - 1, 0) + FREE)
                nc.vector.scalar_tensor_tensor(rest[u % 2][:, :], fin[u % 3][:, :], HD ** -0.5 if u < DC else 1.0,
                                               parts[u % PRING][:, 0, :], ALU.mult, ALU.subtract).then_inc(rest_done, 1)

            def main(t, has_prev, has_next):
                for u in range(UNITS):
                    signs(t, u)
                    take_rest(behind(t, u, 2, has_prev))
                    keep_finite(behind(t, u, 1, has_prev))
                    if u == 0 and has_next:
                        stats_of(t + 1)
                    if u == 1 and has_next:
                        normalise(t + 1)
                    if u == 4 and has_next:
                        for s in range(SUB):
                            xT_low(t + 1, s)

            def drain():
                for step in range(UNITS, UNITS + 2):
                    take_rest(behind(NT - 1, step, 2, True))
                    keep_finite(behind(NT - 1, step, 1, True))

            for signal in (v_scaled, cleaned, rest_done, xn_ready):
                dve.sem_inc(signal, FREE)
            for s in range(SUB):
                xT_low(0, s)
            all_tiles(dve, main)
            drain()

        @block.scalar
        def _(act):
            def xT_high(t, s):
                act.wait_ge(turned, SUB * t + s + 1)
                nc.scalar.copy(xT_hi[:, half_of(t), s * P:(s + 1) * P], turn_bank[s][:, :, :]).then_inc(xT_hi_done, 1)

            def scale(t, u):
                act.wait_ge(mm_ready, UNITS * t + u + 1)
                act.wait_ge(cleaned, UNITS * t + u - 2 + FREE)
                nc.scalar.activation(raw[u % 3][:, :], mm_bank[u % 3][:, :], ACT.Copy,
                                     scale=W["qk_scale"][:, u:u + 1]).then_inc(scaled, 1)

            def first_part(at):
                if at is None:
                    return
                t, u = at
                act.wait_ge(cleaned, UNITS * t + u + 1 + FREE)
                if u == V:
                    act.wait_ge(v_stored, 16 * t + FREE)
                    nc.scalar.copy(vt[:, :, :, 0:HD], fin[V % 3][:, :].rearrange("p (s k c) -> p k s c", s=SUB, k=NKV)
                                   ).then_inc(v_placed, 1)
                else:
                    act.wait_ge(parts_stored[u % PRING], 16 * stores_before(t, u) + FREE)
                    nc.scalar.mul(parts[u % PRING][:, 0, :], fin[u % 3][:, :], HD ** -0.5 if u < DC else 1.0).then_inc(part1_done, 1)

            def second_part(at):
                if at is None or at[1] == V:
                    return
                t, u = at
                act.wait_ge(rest_done, NQK * t + u + 1 + FREE)
                nc.scalar.copy(parts[u % PRING][:, 1, :], rest[u % 2][:, :]).then_inc(part2_done, 1)

            def main(t, has_prev, has_next):
                if not has_prev:
                    scale(t, 0)
                for u in range(UNITS):
                    if u + 1 < NQK:
                        scale(t, u + 1)
                    if u + 1 == UNITS and has_next:
                        scale(t + 1, 0)
                    second_part(behind(t, u, 2, has_prev))
                    first_part(behind(t, u, 1, has_prev))
                    if u == 3 and has_next:
                        for s in range(SUB):
                            xT_high(t + 1, s)

            def drain():
                for step in range(UNITS, UNITS + 2):
                    second_part(behind(NT - 1, step, 2, True))
                    first_part(behind(NT - 1, step, 1, True))

            for signal in (scaled, v_placed):
                act.sem_inc(signal, FREE)
            act.wait_ge(ones_set, 1)
            for s in range(SUB):
                xT_high(0, s)
            all_tiles(act, main)
            drain()

        @block.tensor
        def _(pe):
            def turn(t, s):
                for k in range(DC):
                    last = nc.tensor.transpose(turn_bank[s][:, k, :], xin[:, s, k * P:(k + 1) * P], W["ident"][:, :])
                last.then_inc(turned, 1)

            def main(t, has_next):
                pe.wait_ge(xT_lo_done, SUB * (t + 1))
                chunk = lambda xt, k: xt[:, half_of(t), :][:, k, :]
                for u in range(UNITS):
                    if u == 2:
                        pe.wait_ge(v_scaled, t + FREE)
                    else:
                        pe.wait_ge(scaled, NQK * t + (u - 1 if u < 2 else u - 2) + FREE)
                    if u < V:
                        for k in range(DC):
                            for i, xt in enumerate((xT_hi, xT_lo)):
                                last = nc.tensor.matmul(mm_bank[u % 3][:, :], W["qkv_sign"][:, k, u * P:(u + 1) * P], chunk(xt, k),
                                                        start=(k == 0 and i == 0), stop=(k == DC - 1 and i == 1))
                    else:
                        for s in range(SUB):
                            cols = slice(s * P, (s + 1) * P)
                            for k in range(DC):
                                for i, xt in enumerate((xT_hi, xT_lo)):
                                    last = nc.tensor.matmul(mm_bank[u % 3][:, cols], chunk(xt, k)[:, cols], W["qkv_sign"][:, k, D + KVD:],
                                                            start=(k == 0 and i == 0), stop=(k == DC - 1 and i == 1))
                    last.then_inc(mm_ready, 1)
                    if u == 3 and has_next:
                        pe.wait_ge(xn_ready, t + 1 + FREE)
                        for s in range(SUB):
                            turn(t + 1, s)

            for s in range(SUB):
                turn(0, s)
            with pe.Fori(0, NT - 1) as t:
                main(t, True)
            main(NT - 1, False)


PARTS_OF_BLOCK = ((0, 0), (0, 1), (1, 0), (1, 1), (0, 2), (2, 0))
NBLK = len(PARTS_OF_BLOCK)
SROWS = NBLK * HD
MAXROW = SROWS
QT = SEQ // P
NG = BATCH * NKV


def attention(nc, sem, W, qparts, kparts, vaug, attn_out):
    with ExitStack() as c:
        sb = lambda n, s, d: c.enter_context(nc.sbuf_tensor(f"at_{n}", s, d))
        pb = lambda n, s: c.enter_context(nc.psum_tensor(f"at_{n}", s, F32))
        S = lambda n: sem(f"at_{n}")
        HALVES = SEQ // TT
        NQ = HALVES * QT
        NS = NQ * REP
        NM = REP * QT
        HM = NM // HALVES
        HEAD = 3
        BESIDE = 2
        COPY_AT = QT
        COPY_BEHIND = REP - 1
        TURN_AT = (COPY_AT + 1, 1)
        FOLD_AT = (HEAD + HM // 2, HEAD)

        max_bank = [pb(f"max{i}", [P, SEQ]) for i in range(2)]
        s_bank = [pb(f"s{i}", [P, TT]) for i in range(2)]
        o_bank, turn_bank = pb("o", [P, TT]), pb("turn", [P, SUB, P])
        qst = [sb(f"qst{i}", [P, HALVES, REP, TT], BF16) for i in range(2)]
        kst = [sb(f"kst{i}", [P, SEQ], BF16) for i in range(2)]
        vst = [sb(f"vst{i}", [P, QT, 2 * HD], F32) for i in range(2)]
        prob = [sb(f"prob{i}", [P, REP, TT], F32) for i in range(2)]
        negmax = [sb(f"negmax{h}", [P, HM], F32) for h in range(HALVES)]
        mrest = sb("mrest", [HM, P], F32)
        mparts = [sb(f"mparts{h}", [HM, 3, P], BF16) for h in range(HALVES)]
        osb = sb("osb", [P, TT], F32)
        recip = sb("recip", [P, SUB, REP], F32)
        out = sb("out", [P, QT, REP, HD], F32)

        q_ready = [[S(f"q_ready{i}{h}") for h in range(2)] for i in range(2)]
        k_ready, v_ready = [S(f"k_ready{i}") for i in range(2)], [S(f"v_ready{i}") for i in range(2)]
        rows_set = S("rows_set")
        max_ready, max_read, max_turned, mparts_done = (S(n) for n in ("max_ready", "max_read", "max_turned", "mparts_done"))
        maxrow_ready = [S(f"maxrow_ready{h}") for h in range(HALVES)]
        s_ready, exp_done, pv_done = S("s_ready"), S("exp_done"), S("pv_done")
        o_copied, o_turned, o_normed, out_stored = (S(n) for n in ("o_copied", "o_turned", "o_normed", "out_stored"))
        dve_chain = S("dve_chain")
        rowsof = lambda g, n: bass.ds(g * n, n) if not isinstance(g, int) else slice(g * n, (g + 1) * n)

        wide_ring = [s_bank[0], s_bank[1]] + [b[:, h * TT:(h + 1) * TT] for b in max_bank for h in range(HALVES)]
        WIDE = len(wide_ring)
        assert HEAD * REP % WIDE == 0
        bank_of = lambda s, wide: wide_ring[s % WIDE][:, :] if wide else s_bank[s % 2][:, :]

        split_before = lambda g, half: 4 * (HALVES * g + half)

        block = c.enter_context(nc.Block())

        @block.sync
        def _(sp):
            def load_q(g, i, half):
                for b, (part, _) in enumerate(PARTS_OF_BLOCK):
                    sp.dma_start(qst[i][b * HD:(b + 1) * HD, half, :, :],
                                 qparts[part, rowsof(g, REP * HD), half * TT:(half + 1) * TT].rearrange("(h d) t -> d h t", h=REP)
                                 ).then_inc(q_ready[i][half], 16)

            def load_k(g, i):
                for b, (_, part) in enumerate(PARTS_OF_BLOCK):
                    sp.dma_start(kst[i][b * HD:(b + 1) * HD, :], kparts[part, rowsof(g, HD), :]).then_inc(k_ready[i], 16)

            def load_v(g, i):
                sp.dma_start(vst[i][:, :, :].rearrange("p (h s) c -> p h (s c)", h=HALVES),
                             vaug[rowsof(g, 1)].rearrange("o h p s c -> p (o h) (s c)")).then_inc(v_ready[i], 16)

            def max_rows(g, i, half):
                for part, stage in ((0, 0), (1, 2), (2, 3)):
                    sp.wait_ge(mparts_done, split_before(g, half) + stage + 1 + FREE)
                    sp.dma_start(qst[i][MAXROW + part:MAXROW + part + 1, half, :, :].rearrange(
                        "o h (t p) -> o (h t) p", p=P), mparts[half][:, part, :]).then_inc(maxrow_ready[half], 16)

            def store_out(g):
                sp.wait_ge(o_normed, HALVES * (g + 1) + FREE)
                cols = attn_out.rearrange("(b t p) (k c) -> b k p t c", b=BATCH, p=P, k=NKV)
                sp.dma_start(cols[bass.ds(g // NKV, 1), bass.ds(g % NKV, 1)].rearrange("a o p t c -> (a o p) t c"),
                             out.rearrange("p t h d -> p t (h d)")).then_inc(out_stored, 16)

            def step(g, i, has_load):
                max_rows(g, i, 1)
                if has_load:
                    sp.wait_ge(s_ready, NS * g + NS // 2)
                    load_q(g + 2, i, 0)
                max_rows(g + 1, 1 - i, 0)
                if has_load:
                    sp.wait_ge(s_ready, NS * (g + 1))
                    load_k(g + 2, i)
                    load_q(g + 2, i, 1)
                    sp.wait_ge(pv_done, NQ * (g + 1) + FREE)
                    load_v(g + 2, i)
                store_out(g)

            for signal in (*maxrow_ready, out_stored):
                sp.sem_inc(signal, FREE)
            for i in range(2):
                load_k(i, i)
                load_q(i, i, 0)
                load_q(i, i, 1)
                load_v(i, i)
            sp.wait_ge(rows_set, 4)
            max_rows(0, 0, 0)
            with sp.Fori(0, NG // 2 - 1) as pair:
                for i in range(2):
                    step(pair * 2 + i, i, True)
            step(NG - 2, 0, False)
            max_rows(NG - 1, 1, 1)
            sp.wait_ge(out_stored, 16 * (NG // 2) + FREE)
            sp.dma_start(W["xin"][:, :, :], attn_out[0:TT, :].rearrange("(s p) d -> p s d", p=P)).then_inc(W["first_rows"], 16)
            store_out(NG - 1)
            sp.wait_ge(out_stored, 16 * NG + FREE)

        @block.gpsimd
        def _(pool):
            for i in range(2):
                nc.gpsimd.memset(qst[i][MAXROW:P, :, :, :], 0.0).then_inc(rows_set, 1)
                nc.gpsimd.memset(kst[i][MAXROW:P, :], 1.0).then_inc(rows_set, 1)

        @block.vector
        def _(dve):
            chain = Chain(dve, dve_chain)

            def max_unit(g, j):
                half = j // HM
                col = (j % REP) * SUB + j // REP % SUB
                if j % HM == 0:
                    dve.wait_ge(max_turned, HALVES * g + half - 1 + FREE)
                dve.wait_ge(max_ready, NM * g + j + 1)
                nc.vector.tensor_reduce(negmax[half][:, col:col + 1], max_bank[j % 2][:, :], AX.X, ALU.max,
                                        negate=True).then_inc(max_read, 1)

            def split_max(g, half, stage):
                m, parts = turn_bank[0:HM, 0, :], mparts[half]
                if stage == 0:
                    dve.wait_ge(max_turned, HALVES * g + half + 1 + FREE)
                    dve.wait_ge(maxrow_ready[half], 48 * g + FREE)
                    last = nc.vector.tensor_copy(parts[:, 0, :], m)
                else:
                    dve.wait_ge(mparts_done, split_before(g, half) + stage + FREE)
                if stage == 1:
                    last = nc.vector.tensor_tensor(mrest[:, :], m, parts[:, 0, :], ALU.subtract)
                if stage == 2:
                    last = nc.vector.tensor_copy(parts[:, 1, :], mrest[:, :])
                if stage == 3:
                    last = nc.vector.tensor_tensor(parts[:, 2, :], mrest[:, :], parts[:, 1, :], ALU.subtract)
                last.then_inc(mparts_done, 1)

            def normalise(g, half, stage):
                t = turn_bank[:, :, :].rearrange("p s (h e) -> p s h e", h=REP)
                if stage == 0:
                    dve.wait_ge(o_turned, HALVES * g + half + 1 + FREE)
                    dve.wait_ge(o_normed, HALVES * g + half + FREE)
                    chain.add(nc.vector.reciprocal(recip[:, :, :], t[:, :, :, HD]))
                if stage == 1:
                    if half == 0:
                        dve.wait_ge(out_stored, 16 * g + FREE)
                    chain.wait()
                    nc.vector.tensor_tensor(out[:, half * SUB:(half + 1) * SUB, :, :], t[:, :, :, 0:HD],
                                            recip[:, :, :].unsqueeze(3).to_broadcast([P, SUB, REP, HD]),
                                            ALU.mult).then_inc(o_normed, 1)

            def around(g, n, v, first_half_of):
                if n == TURN_AT[0] + 1:
                    normalise(g, 0, v)
                if n == TURN_AT[1] + 1:
                    normalise(g - 1, 1, v)
                if n in (FOLD_AT[1] + 1, FOLD_AT[1] + 2):
                    split_max(g, 1, 2 * (n - FOLD_AT[1] - 1) + v)
                if n in (FOLD_AT[0] + 1, FOLD_AT[0] + 2) and first_half_of is not None:
                    split_max(first_half_of, 0, 2 * (n - FOLD_AT[0] - 1) + v)

            def step(g):
                for n in range(HEAD, NQ + HEAD):
                    for v in range(2):
                        max_unit(g + 1, 2 * (n - HEAD) + v)
                        around(g if n < NQ else g + 1, n % NQ, v, g + 1)

            for signal in (max_read, mparts_done, o_normed):
                dve.sem_inc(signal, FREE)
            for j in range(NM):
                max_unit(0, j)
                if j == HM:
                    for stage in range(4):
                        split_max(0, 0, stage)
            PER_STEP = HALVES
            with dve.Fori(0, NG // 2 - 1) as pair:
                chain.enter(pair * (2 * PER_STEP))
                for i in range(2):
                    step(pair * 2 + i)
            chain.enter((NG - 2) * PER_STEP)
            step(NG - 2)
            for n in range(HEAD, NQ):
                for v in range(2):
                    around(NG - 1, n, v, None)
            for v in range(2):
                normalise(NG - 1, 1, v)

        @block.scalar
        def _(act):
            def quad(g, n, first, wide=False):
                act.wait_ge(pv_done, NQ * g + n - 1 + FREE)
                for h in range(REP):
                    s = n * REP + h
                    act.wait_ge(s_ready, NS * g + s + 1)
                    nc.scalar.activation(prob[n % 2][:, h, :], bank_of(s, wide), ACT.Exp).then_inc(exp_done, 1)
                    if h == COPY_BEHIND and n == COPY_AT:
                        copy_out(g, 0)
                    if h == COPY_BEHIND and n == 0 and not first:
                        copy_out(g - 1, 1)

            def copy_out(g, half):
                act.wait_ge(pv_done, NQ * g + (half + 1) * QT + FREE)
                act.wait_ge(o_turned, HALVES * g + half + FREE)
                nc.scalar.copy(osb[:, :], o_bank[:, :]).then_inc(o_copied, 1)

            act.sem_inc(o_copied, FREE)
            for n in range(HEAD):
                quad(0, n, True)
            with act.Fori(0, NG - 1) as g:
                for n in range(HEAD, NQ):
                    quad(g, n, False)
                for n in range(HEAD):
                    quad(g + 1, n, False)
            for n in range(HEAD, NQ):
                quad(NG - 1, n, False, True)
            copy_out(NG - 1, 1)

        @block.tensor
        def _(pe):
            def max_unit(g, i, k, j):
                t, h = j // REP, j % REP
                if j == 0:
                    pe.wait_ge(k_ready[i], 16 * NBLK * (k + 1))
                    pe.wait_ge(q_ready[i][0], 16 * NBLK * (k + 1))
                if j == HM:
                    pe.wait_ge(q_ready[i][1], 16 * NBLK * (k + 1))
                pe.wait_ge(max_read, NM * g + j - 1 + FREE)
                for half in range(HALVES):
                    last = nc.tensor.matmul(max_bank[j % 2][:, half * TT:(half + 1) * TT],
                                            qst[i][0:SROWS, t // SUB, h, t % SUB * P:(t % SUB + 1) * P],
                                            kst[i][0:SROWS, half * TT:(half + 1) * TT], start=True, stop=True)
                last.then_inc(max_ready, 1)

            def turn_max(g, half):
                pe.wait_ge(max_read, NM * g + (half + 1) * HM + FREE)
                pe.wait_ge(mparts_done, split_before(g, half) + FREE)
                pe.wait_ge(o_normed, HALVES * g + half - 1 + FREE)
                nc.tensor.transpose(turn_bank[0:HM, 0, :], negmax[half][:, :], W["ident"][:, :]).then_inc(max_turned, 1)

            def turn_out(g, half, folds):
                pe.wait_ge(o_copied, HALVES * g + half + 1 + FREE)
                pe.wait_ge(o_normed, HALVES * g + half + FREE)
                pe.wait_ge(mparts_done, 4 * folds + FREE)
                for s in range(SUB):
                    last = nc.tensor.transpose(turn_bank[:, s, :], osb[:, s * P:(s + 1) * P], W["ident"][:, :])
                last.then_inc(o_turned, 1)

            def scores(g, i, n, h, wide=False):
                s, half, kt = n * REP + h, n // QT, n % QT
                taken = s - HEAD * REP
                if not wide or taken < 2:
                    pe.wait_ge(exp_done, NS * g + s - 1 + FREE)
                elif taken < WIDE:
                    pe.wait_ge(max_read, NM * NG + FREE)
                else:
                    pe.wait_ge(exp_done, NS * g + s - WIDE + 1 + FREE)
                nc.tensor.matmul(bank_of(s, wide), kst[i][:, kt * P:(kt + 1) * P], qst[i][:, half, h, :],
                                 start=True, stop=True).then_inc(s_ready, 1)

            def values(g, i, n):
                half, kt = n // QT, n % QT
                pe.wait_ge(exp_done, NS * g + (n + 1) * REP + FREE)
                if kt == 0:
                    pe.wait_ge(o_copied, HALVES * g + half + FREE)
                for h in range(REP):
                    last = nc.tensor.matmul(o_bank[32 * h:32 * h + 32, :], vst[i][:, kt, :], prob[n % 2][:, h, :],
                                            start=(kt == 0), stop=(kt == QT - 1), tile_position=(0, 32 * h))
                last.then_inc(pv_done, 1)

            def quad(g, i, k, n, unit, first=False):
                if n % QT == 0:
                    pe.wait_ge(maxrow_ready[n // QT], 48 * (g + 1) + FREE)
                scores(g, i, n, 0)
                scores(g, i, n, 1)
                if n == 1:
                    pe.wait_ge(v_ready[i], 16 * (k + 1))
                if n >= 1:
                    values(g, i, n - 1)
                elif not first:
                    values(g - 1, 1 - i, NQ - 1)
                scores(g, i, n, 2)
                scores(g, i, n, 3)
                unit(0)
                unit(1)
                if n == TURN_AT[0]:
                    turn_out(g, 0, HALVES * g + 2)
                if n == FOLD_AT[1]:
                    turn_max(g, 1)

            def step(g, i, k):
                for n in range(HEAD, NQ):
                    quad(g, i, k, n, lambda v: max_unit(g + 1, 1 - i, k + i, 2 * (n - HEAD) + v))
                    if n == FOLD_AT[0]:
                        turn_max(g + 1, 0)
                for n in range(HEAD):
                    quad(g + 1, 1 - i, k + i, n, lambda v: max_unit(g + 1, 1 - i, k + i, 2 * (n + NQ - HEAD) + v))
                    if n == TURN_AT[1]:
                        turn_out(g, 1, HALVES * g + 3)

            for signal in (exp_done, pv_done, max_turned, o_turned):
                pe.sem_inc(signal, FREE)
            FIRST = NM - 2 * HEAD * BESIDE
            for j in range(FIRST):
                max_unit(0, 0, 0, j)
                if j == HM:
                    turn_max(0, 0)
            pe.wait_ge(rows_set, 4)
            for n in range(HEAD):
                def unit(v):
                    for j in range(BESIDE):
                        max_unit(0, 0, 0, FIRST + (2 * n + v) * BESIDE + j)
                quad(0, 0, 0, n, unit, True)
            with pe.Fori(0, NG // 2 - 1) as pair:
                for i in range(2):
                    step(pair * 2 + i, i, pair)
            step(NG - 2, 0, NG // 2 - 1)
            for n in range(HEAD, NQ):
                if n == QT:
                    pe.wait_ge(maxrow_ready[1], 48 * NG + FREE)
                for h in range(REP):
                    scores(NG - 1, 1, n, h, True)
                values(NG - 1, 1, n - 1)
                if n == TURN_AT[0]:
                    turn_out(NG - 1, 0, HALVES * (NG - 1) + 2)
                if n == FOLD_AT[1]:
                    turn_max(NG - 1, 1)
            values(NG - 1, 1, NQ - 1)
            turn_out(NG - 1, 1, HALVES * NG)


def output_projection(nc, sem, W, attn_out, src, dst):
    with ExitStack() as c:
        sb = lambda n, s, d: c.enter_context(nc.sbuf_tensor(f"op_{n}", s, d))
        S = lambda n: sem(f"op_{n}")
        turn_bank = [c.enter_context(nc.psum_tensor(f"op_turn{s}", [P, DC, P], F32)) for s in range(SUB)]
        mm_bank = [c.enter_context(nc.psum_tensor(f"op_mm{i}", [P, D], F32)) for i in range(SUB)]
        ain = [sb(f"ain{s}", [P, D], F32) for s in range(SUB)]
        res = [sb(f"res{s}", [P, D], F32) for s in range(SUB)]
        aT_hi = [sb(f"aT_hi{s}", [P, DC, P], F32R) for s in range(SUB)]
        aT_lo = [sb(f"aT_lo{s}", [P, DC, P], F32R) for s in range(SUB)]
        raw = [sb(f"raw{i}", [P, TT], F32) for i in range(2)]
        fin = [sb(f"fin{i}", [P, TT], F32) for i in range(SUB)]
        neg = [sb(f"neg{i}", [P, TT], F32) for i in range(2)]
        xin = W["xin"]
        stats, mv = sb("stats", [P, SUB, 6], F32), sb("mv", [P, SUB, 2], F32)
        ve, rstd, tmp = sb("ve", [P, SUB], F32), sb("rstd", [P, SUB], F32), sb("tmp", [P, SUB], F32)
        ain_ready, res_ready, stored = ([S(f"{n}{s}") for s in range(SUB)] for n in ("ain_ready", "res_ready", "stored"))
        turned, hi_done, lo_done = S("turned"), S("hi_done"), S("lo_done")
        mm_ready, scaled, pool_cleaned, cleaned, added = (S(n) for n in ("mm_ready", "scaled", "pool_cleaned", "cleaned", "added"))
        signs_ready, mask_ready = S("signs_ready"), S("mask_ready")
        x_ready, stats_ready, rstd_ready, xn_ready = (S(n) for n in ("x_ready", "stats_ready", "rstd_ready", "xn_ready"))
        rows_v = lambda ap, t, s: ap.rearrange("(t s p) d -> t s p d", s=SUB, p=P)[bass.ds(t, 1), s].rearrange("o p d -> (o p) d")
        TURN_AHEAD, LOW_AHEAD = 2, 1

        block = c.enter_context(nc.Block())

        @block.sync
        def _(sp):
            def load_in(t, s):
                sp.dma_start(ain[s][:, :], rows_v(attn_out, t, s)).then_inc(ain_ready[s], 16)

            def residual(at):
                if at is None:
                    return
                t, s = at
                sp.wait_ge(stored[s], 16 * t + FREE)
                sp.sem_inc(W["sp_apart"], 1)
                sp.dma_start(res[s][:, :], rows_v(src, t, s)).then_inc(res_ready[s], 16)

            def store(at):
                if at is None:
                    return
                t, s = at
                sp.wait_ge(added, SUB * t + s + 1)
                sp.sem_inc(W["sp_apart"], 1)
                sp.dma_start(rows_v(dst, t, s), res[s][:, :]).then_inc(stored[s], 16)

            def main(t, has_prev, has_next):
                if not has_next:
                    sp.wait_ge(turned, SUB)
                    for i in range(SUB):
                        sp.wait_ge(stored[i], 16 + FREE)
                    sp.dma_start(xin[:, :, :], dst[0:TT, :].rearrange("(s p) d -> p s d", p=P)).then_inc(x_ready, 16)
                for s in range(SUB):
                    if has_next:
                        if has_prev:
                            sp.wait_ge(turned, SUB * t + s + 1)
                            sp.sem_inc(W["sp_apart"], 1)
                        load_in(t + 1, s)
                    store(shifted(t, s, -2, SUB, has_prev, False))
                    residual(shifted(t, s, 1, SUB, True, has_next))

            for signal in stored:
                sp.sem_inc(signal, FREE)
            residual((0, 0))
            all_tiles(sp, main)
            for step in range(SUB, SUB + 2):
                store(shifted(NT - 1, step, -2, SUB, True, False))
            for s in range(SUB):
                sp.wait_ge(stored[s], 16 * NT + FREE)

        @block.gpsimd
        def _(pool):
            chain = Chain(pool, S("pool_chain"), W["pool_apart"])

            def add_residual(at):
                if at is None:
                    return
                t, s = at
                pool.wait_ge(cleaned, SUB * t + s + 1 + FREE)
                pool.wait_ge(res_ready[s], 16 * (t + 1))
                nc.gpsimd.tensor_tensor(res[s][:, :], fin[s][:, :], res[s][:, :], ALU.add).then_inc(added, 1)

            def main(t, has_prev, has_next):
                for s in range(SUB):
                    pool.wait_ge(signs_ready, SUB * t + s + 1)
                    nc.gpsimd.tensor_tensor(fin[s][:, :], fin[s][:, :], neg[s % 2][:, :], ALU.add).then_inc(pool_cleaned, 1)
                    add_residual(shifted(t, s, -2, SUB, has_prev, False))
                    if s == 2 and not has_next:
                        pool.wait_ge(stats_ready, 1)
                        rstd_on_pool(nc, chain, mv, ve, rstd, tmp, W["neg_half"], rstd_ready)

            pool.sem_inc(pool_cleaned, FREE)
            all_tiles(pool, main)
            for step in range(SUB, SUB + 2):
                add_residual(shifted(NT - 1, step, -2, SUB, True, False))

        @block.vector
        def _(dve):
            chain = Chain(dve, S("dve_chain"), W["dve_apart"])

            def low_part(at):
                if at is None:
                    return
                t, s = at
                dve.wait_ge(hi_done, SUB * t + s + 1)
                nc.vector.tensor_tensor(aT_lo[s][:, :, :], turn_bank[s][:, :, :],
                                        aT_hi[s][:, :, :].bitcast(F32), ALU.subtract).then_inc(lo_done, 1)

            def signs(t, s):
                dve.wait_ge(mm_ready, SUB * t + s + 1 + FREE)
                dve.wait_ge(cleaned, SUB * t + s - 1 + FREE)
                nc.vector.tensor_tensor(raw[s % 2][:, :], mm_bank[s][:, :], W["vo_scale"][:, KVD:], ALU.mult).then_inc(scaled, 1)
                dve.wait_ge(scaled, SUB * t + s + 1 + FREE)
                if not isinstance(t, int) or t > 0:
                    dve.wait_ge(added, SUB * (t - 1) + s + 1)
                split_by_sign(nc, raw[s % 2][:, :], fin[s][:, :], neg[s % 2][:, :], signs_ready)

            def keep_finite(at):
                if at is None:
                    return
                t, s = at
                dve.wait_ge(pool_cleaned, SUB * t + s + 1 + FREE)
                mask = neg[s % 2][:, :].bitcast(I32)
                mask_finite(nc, raw[s % 2][:, :], mask, mask_ready)
                dve.wait_ge(mask_ready, SUB * t + s + 1)
                dve.sem_inc(chain.apart, 1)
                nc.vector.copy_predicated(fin[s][:, :], mask, raw[s % 2][:, :]).then_inc(cleaned, 1)

            def main(t, has_prev, has_next):
                for s in range(SUB):
                    low_part(shifted(t, s, LOW_AHEAD, SUB, True, has_next))
                    signs(t, s)
                    keep_finite(shifted(t, s, -1, SUB, has_prev, False))
                    if s == 2 and not has_next:
                        dve.wait_ge(x_ready, 16)
                        layernorm_stats(nc, dve, chain, xin, stats, mv, stats_ready)
                    if s == 3 and not has_next:
                        normalise_rows(nc, dve, xin, mv, rstd, rstd_ready, 1, xn_ready)

            for signal in (cleaned, scaled):
                dve.sem_inc(signal, FREE)
            low_part((0, 0))
            all_tiles(dve, main)
            keep_finite((NT - 1, SUB - 1))

        @block.scalar
        def _(act):
            with act.Fori(0, NT) as t:
                for s in range(SUB):
                    act.wait_ge(turned, SUB * t + s + 1)
                    act.wait_ge(mm_ready, SUB * (t - 1) + s + 1 + FREE)
                    nc.scalar.copy(aT_hi[s][:, :, :], turn_bank[s][:, :, :]).then_inc(hi_done, 1)

        @block.tensor
        def _(pe):
            def turn(at):
                if at is None:
                    return
                t, s = at
                if isinstance(t, int) and t == 0:
                    pe.wait_ge(W["first_rows"], 16)
                    rows = xin[:, s, :]
                else:
                    pe.wait_ge(ain_ready[s], 16 * t)
                    pe.wait_ge(lo_done, SUB * (t - 1) + s + 1)
                    rows = ain[s]
                for k in range(DC):
                    last = nc.tensor.transpose(turn_bank[s][:, k, :], rows[:, k * P:(k + 1) * P], W["ident"][:, :])
                last.then_inc(turned, 1)

            def main(t, has_prev, has_next):
                for s in range(SUB):
                    turn(shifted(t, s, TURN_AHEAD, SUB, True, has_next))
                    pe.wait_ge(lo_done, SUB * t + s + 1)
                    pe.wait_ge(scaled, SUB * (t - 1) + s + 1 + FREE)
                    for k in range(DC):
                        for i, at in enumerate((aT_hi, aT_lo)):
                            last = nc.tensor.matmul(mm_bank[s][:, :], at[s][:, k, :], W["o_sign"][:, k, :],
                                                    start=(k == 0 and i == 0), stop=(k == DC - 1 and i == 1))
                    last.then_inc(mm_ready, 1)

            pe.sem_inc(mm_ready, FREE)
            for s in range(TURN_AHEAD):
                turn((0, s))
            all_tiles(pe, main)


def build(nc, io):
    ctx = ExitStack()
    with ctx:
        sb = lambda n, s, d: ctx.enter_context(nc.sbuf_tensor(n, s, d))
        sem = lambda n: ctx.enter_context(nc.semaphore(n))
        W = {
            "ident": sb("ident", [P, P], F32),
            "neg_half": sb("neg_half", [P, SUB], F32),
            "first_rows": sem("first_rows"),
            "dve_apart": sem("dve_apart"),
            "sp_apart": sem("sp_apart"),
            "pool_apart": sem("pool_apart"),
            "xin": sb("xin", [P, SUB, D], F32),
            "up_hi": [sb(f"up_hi{w}", [P, DC, HID], F32R) for w in range(2)],
            "up_lo": [sb(f"up_lo{w}", [P, DC, HID], F32R) for w in range(2)],
            "down_hi": sb("down_hi", [P, HC, D], F32R),
            "down_lo": sb("down_lo", [P, HC, D], F32R),
            "qkv_sign": sb("qkv_sign", [P, DC, D + 2 * KVD], F16),
            "o_sign": sb("o_sign", [P, DC, D], F32R),
            "qk_scale": sb("qk_scale", [P, DC + 1], F32),
            "vo_scale": sb("vo_scale", [P, KVD + D], F32),
        }
        weight_prep(nc, sem, io, W)
        ffn(nc, sem, "ffn1", W, io["x"], io["x1"], hand_on=True)
        projections(nc, sem, W, io["x1"], io["qparts"], io["kparts"], io["vaug"])
        attention(nc, sem, W, io["qparts"], io["kparts"], io["vaug"], io["attn_out"])
        output_projection(nc, sem, W, io["attn_out"], io["x1"], io["x2"])
        ffn(nc, sem, "ffn2", W, io["x2"], io["out"], hand_on=False)


_INS = {'x': 'L0_attn_hidden_states', 'wq': 'L0_attn_q_weight', 'qs': 'L0_attn_q_scale', 'wk': 'L0_attn_k_weight',
        'ks': 'L0_attn_k_scale', 'wv': 'L0_attn_v_weight', 'vs': 'L0_attn_v_scale', 'wo': 'L0_attn_o_weight',
        'os': 'L0_attn_o_scale', 'w1': 'L0_ffn_w1', 's1': 'L0_ffn_s1', 'w2': 'L0_ffn_w2', 's2': 'L0_ffn_s2',
        'w3': 'L0_ffn_w3', 's3': 'L0_ffn_s3'}


def kernel(**inputs):
    import numpy as np
    import concourse.bacc as bacc
    from concourse import mybir as mb
    from concourse.bass_utils import run_bass_kernel_spmd as run

    nc = bacc.Bacc("TRN2", target_bir_lowering=False, num_devices=1)
    arrays, io = {}, {}
    for short, name in _INS.items():
        a = np.ascontiguousarray(inputs[name])
        arrays[f"in_{short}"] = a
        io[short] = nc.dram_tensor(f"in_{short}", a.shape, mb.dt.from_np(a.dtype), kind="ExternalInput").ap()
    out = nc.dram_tensor("out", (BATCH, SEQ, D), F32, kind="ExternalOutput").ap()
    io["x"] = io["x"].rearrange("b s d -> (b s) d")
    io["out"] = out.rearrange("b s d -> (b s) d")
    for name, shape, dt in (("x1", (TOK, D), F32), ("x2", (TOK, D), F32),
                            ("qparts", (3, BATCH * D, SEQ), BF16), ("kparts", (3, BATCH * KVD, SEQ), BF16),
                            ("vaug", (NG, SEQ // TT, P, SUB, 2 * HD), F32), ("attn_out", (TOK, D), F32)):
        io[name] = nc.dram_tensor(name, shape, dt, kind="Internal").ap()
    io["row_scratch"] = nc.dram_tensor("row_scratch", (KVD + D,), F32, kind="Internal").ap()
    build(nc, io)
    r = run(nc, [arrays], core_ids=[0])
    return r.results[0]["out"]
```
